# Optimizing a Trainium2 kernel written in Bass

```python
import numpy as np
import jax
import jax.numpy as jnp

def _softmax(x, axis=-1):
    return jax.nn.softmax(x, axis=axis)

def _gelu(x):
    return jax.nn.gelu(x, approximate=True)

def _silu(x):
    return jax.nn.silu(x)

def _sigmoid(x):
    return jax.nn.sigmoid(x)

def _layernorm(x, axis=-1, eps=1e-05):
    m = jnp.mean(x, axis=axis, keepdims=True)
    v = jnp.var(x, axis=axis, keepdims=True)
    return (x - m) / jnp.sqrt(v + eps)

def _scatter_add(tgt, idx, src, axis=0):
    return tgt.at[idx].add(src)

def _segment_sum(src, seg, n):
    return jax.ops.segment_sum(src, seg, n)
kernel_name = 'mk_vit_tower_d1_tok_img512_r4_301ed6'

def setup_inputs(seed: int=0):
    np.random.seed(seed)
    _w = jnp.asarray

    def _rec_inputs():
        import jax
        import jax.numpy as jnp
        _rk = jax.random.key(seed)
        x = -0.000190493 + 0.999948 * jax.random.normal(jax.random.fold_in(_rk, 1), (128, 2, 104, 104), jnp.float32)
        return x
    x = _rec_inputs()

    def _L0_tok_setup():
        import jax, jax.numpy as jnp
        import numpy as np
        HP = 4
        PATCH = 8
        EPS = 1e-07

        def _shifts(x):
            h, w = (x.shape[2], x.shape[3])
            pad2 = ((0, 0), (0, 0))
            left_up = jnp.pad(x[:, :, HP:, :w - HP], pad2 + ((0, HP), (HP, 0)))
            right_up = jnp.pad(x[:, :, HP:, HP:], pad2 + ((0, HP), (0, HP)))
            left_down = jnp.pad(x[:, :, :h - HP, :w - HP], pad2 + ((HP, 0), (HP, 0)))
            right_down = jnp.pad(x[:, :, :h - HP, HP:], pad2 + ((HP, 0), (0, HP)))
            return (left_up, right_up, left_down, right_down)
        key = jax.random.key(seed)
        k1, k2, k3, k4 = jax.random.split(key, 4)
        B, C, S = (128, 2, 104)
        embed_dim = 128
        x = jax.random.normal(k1, (B, C, S, S), dtype=jnp.float32)
        gamma = 1.0 + 0.05 * jax.random.normal(k2, (10, S, S), dtype=jnp.float32)
        beta = 0.05 * jax.random.normal(k3, (10, S, S), dtype=jnp.float32)
        W = 0.02 * jax.random.normal(k4, (embed_dim, 10, PATCH, PATCH), dtype=jnp.float32)
        b = jnp.zeros((embed_dim,), dtype=jnp.float32)
        return {'x': x, 'gamma': gamma, 'beta': beta, 'W': W, 'b': b}
    _L0_tok_all = _L0_tok_setup()
    _L0_tok_in = {k: v for k, v in _L0_tok_all.items() if k in ('gamma', 'beta', 'W', 'b')}
    del _L0_tok_all

    def _L0_attn_setup():
        import jax, jax.numpy as jnp
        import numpy as np
        B, S, D_IN, UNITS = (8, 512, 128, 128)

        def _glorot(key, fan_in, fan_out):
            limit = np.sqrt(6.0 / (fan_in + fan_out)).astype(np.float32)
            return jax.random.uniform(key, (fan_in, fan_out), jnp.float32, -limit, limit)
        key = jax.random.key(seed)
        kq, kwq, kwv, kwk = jax.random.split(key, 4)
        return {'query': jax.random.normal(kq, (B, S, D_IN), jnp.float32), 'Wq': _glorot(kwq, D_IN, UNITS), 'Wv': _glorot(kwv, D_IN, UNITS), 'Wk': _glorot(kwk, D_IN, UNITS)}
    _L0_attn_all = _L0_attn_setup()
    _L0_attn_in = {k: v for k, v in _L0_attn_all.items() if k in ('Wq', 'Wv', 'Wk')}
    del _L0_attn_all

    def _L0_ffn_setup():
        import jax, jax.numpy as jnp
        import numpy as np
        B, S, D, F, E = (4, 512, 128, 512, 8)
        key = jax.random.key(seed)
        k = jax.random.split(key, 5)
        x = jax.random.normal(k[0], (B, S, D), dtype=jnp.float32)
        Ws = jax.random.normal(k[1], (D, E), dtype=jnp.float32) * 0.02
        bs = jnp.zeros((E,), dtype=jnp.float32)
        W1 = jax.random.normal(k[2], (E, D, F), dtype=jnp.float32) * 0.02
        b1 = jnp.zeros((E, F), dtype=jnp.float32)
        W2 = jax.random.normal(k[3], (E, F, D), dtype=jnp.float32) * 0.02
        b2 = jnp.zeros((E, D), dtype=jnp.float32)
        return {'x': x, 'Ws': Ws, 'bs': bs, 'W1': W1, 'b1': b1, 'W2': W2, 'b2': b2}
    _L0_ffn_all = _L0_ffn_setup()
    _L0_ffn_in = {k: v for k, v in _L0_ffn_all.items() if k in ('Ws', 'bs', 'W1', 'b1', 'W2', 'b2')}
    del _L0_ffn_all
    return {'x': x, 'L0_tok_gamma': _L0_tok_in['gamma'], 'L0_tok_beta': _L0_tok_in['beta'], 'L0_tok_W': _L0_tok_in['W'], 'L0_tok_b': _L0_tok_in['b'], 'L0_attn_Wq': _L0_attn_in['Wq'], 'L0_attn_Wv': _L0_attn_in['Wv'], 'L0_attn_Wk': _L0_attn_in['Wk'], 'L0_ffn_Ws': _L0_ffn_in['Ws'], 'L0_ffn_bs': _L0_ffn_in['bs'], 'L0_ffn_W1': _L0_ffn_in['W1'], 'L0_ffn_b1': _L0_ffn_in['b1'], 'L0_ffn_W2': _L0_ffn_in['W2'], 'L0_ffn_b2': _L0_ffn_in['b2']}

def reference(x, L0_tok_gamma, L0_tok_beta, L0_tok_W, L0_tok_b, L0_attn_Wq, L0_attn_Wv, L0_attn_Wk, L0_ffn_Ws, L0_ffn_bs, L0_ffn_W1, L0_ffn_b1, L0_ffn_W2, L0_ffn_b2):
    import jax
    import jax.numpy as jnp

    def _L0_tok_ref(x, gamma, beta, W, b):
        import jax, jax.numpy as jnp
        import numpy as np
        HP = 4
        PATCH = 8
        EPS = 1e-07

        def _shifts(x):
            h, w = (x.shape[2], x.shape[3])
            pad2 = ((0, 0), (0, 0))
            left_up = jnp.pad(x[:, :, HP:, :w - HP], pad2 + ((0, HP), (HP, 0)))
            right_up = jnp.pad(x[:, :, HP:, HP:], pad2 + ((0, HP), (0, HP)))
            left_down = jnp.pad(x[:, :, :h - HP, :w - HP], pad2 + ((HP, 0), (HP, 0)))
            right_down = jnp.pad(x[:, :, :h - HP, HP:], pad2 + ((HP, 0), (0, HP)))
            return (left_up, right_up, left_down, right_down)
        lu, ru, ld, rd = _shifts(x)
        concat = jnp.concatenate((x, lu, ru, ld, rd), axis=1)
        mean = jnp.mean(concat, axis=(1, 2, 3), keepdims=True)
        var = jnp.var(concat, axis=(1, 2, 3), keepdims=True)
        normed = (concat - mean) * jax.lax.rsqrt(var + EPS)
        normed = normed * gamma[None] + beta[None]
        y = jax.lax.conv_general_dilated(normed, W, window_strides=(PATCH, PATCH), padding='VALID', dimension_numbers=('NCHW', 'OIHW', 'NCHW'))
        y = y + b[None, :, None, None]
        B, E = (y.shape[0], y.shape[1])
        y = y.reshape(B, E, -1).transpose(0, 2, 1)
        return y

    def _L0_attn_ref(query, Wq, Wv, Wk):
        import jax, jax.numpy as jnp
        import numpy as np
        B, S, D_IN, UNITS = (8, 512, 128, 128)

        def _glorot(key, fan_in, fan_out):
            limit = np.sqrt(6.0 / (fan_in + fan_out)).astype(np.float32)
            return jax.random.uniform(key, (fan_in, fan_out), jnp.float32, -limit, limit)
        q = jax.nn.sigmoid(jnp.einsum('bsd,du->bsu', query, Wq))
        k = jax.nn.sigmoid(jnp.einsum('bsd,du->bsu', query, Wv))
        v = jax.nn.sigmoid(jnp.einsum('bsd,du->bsu', query, Wk))
        d_in = query.shape[-1]
        score = jnp.einsum('bqu,bku->bqk', q, k) / jnp.sqrt(jnp.float32(d_in))
        s = score.shape[1]
        masked = jnp.where(jnp.triu(jnp.ones((s, s), bool)), -jnp.inf, score)
        rest = jax.nn.softmax(masked[:, 1:, :], axis=-1)
        attn = jnp.concatenate([jnp.zeros((score.shape[0], 1, s), score.dtype), rest], axis=1)
        return jnp.einsum('bqk,bku->bqu', attn, v)

    def _L0_ffn_ref(x, Ws, bs, W1, b1, W2, b2):
        import jax, jax.numpy as jnp
        import numpy as np
        B, S, D, F, E = (4, 512, 128, 512, 8)
        Bb, Ss, Dd = x.shape
        xt = x.reshape(-1, Dd)
        logits = xt @ Ws + bs
        probs = jax.nn.softmax(logits, axis=-1)
        prob_max = jnp.max(probs, axis=-1)
        routes = jnp.argmax(probs, axis=-1)
        onehot = jax.nn.one_hot(routes, W1.shape[0], dtype=xt.dtype)

        def expert_ffn(w1, bb1, w2, bb2):
            h = jax.nn.gelu(xt @ w1 + bb1, approximate=False)
            return h @ w2 + bb2
        y = jax.vmap(expert_ffn)(W1, b1, W2, b2)
        out = jnp.einsum('te,etd->td', onehot, y)
        out = out * prob_max[:, None]
        return out.reshape(Bb, Ss, Dd)
    h = _L0_tok_ref(x, L0_tok_gamma, L0_tok_beta, L0_tok_W, L0_tok_b)
    h = h + _L0_attn_ref(_layernorm(h, axis=-1), L0_attn_Wq, L0_attn_Wv, L0_attn_Wk)
    h = h + _L0_ffn_ref(_layernorm(h, axis=-1), L0_ffn_Ws, L0_ffn_bs, L0_ffn_W1, L0_ffn_b1, L0_ffn_W2, L0_ffn_b2)
    return h

_drawn_inputs = setup_inputs


def setup_inputs(seed=0):
    import zlib

    import numpy as np

    out = dict(_drawn_inputs(seed))
    spreads = {'L0_tok_b': (0.0, 0.1),
     'L0_ffn_bs': (0.0, 0.439),
     'L0_ffn_b1': (0.0, 0.8),
     'L0_ffn_b2': (0.0, 0.336)}
    factors = {'L0_attn_Wq': 8.0, 'L0_attn_Wv': 8.0, 'L0_ffn_W1': 4.314, 'L0_ffn_W2': 3.905}
    for name, (base, spread) in spreads.items():
        noise = np.random.default_rng([zlib.crc32(name.encode()), seed]).standard_normal(out[name].shape)
        drawn = base * np.exp(spread * noise) if base else spread * noise
        out[name] = jnp.asarray(drawn.astype(out[name].dtype))
    for name, factor in factors.items():
        out[name] = (out[name] * factor).astype(out[name].dtype)
    return out
```

```python
from contextlib import ExitStack

import numpy as np
import concourse.bass as bass
from concourse import mybir

F32 = mybir.dt.float32
BF16 = mybir.dt.bfloat16
F16 = mybir.dt.float16
I32 = mybir.dt.int32
ALU = mybir.AluOpType
ACT = mybir.ActivationFunctionType
AX = mybir.AxisListType

IMAGES = 128
D = 128
GRID = 13
TOKENS = GRID * GRID
ALL = IMAGES * TOKENS
VARIANTS = 5
PIXELS = 10 * 104 * 104
TOK_EPS = 1e-7
LN_EPS = 1e-5
GROUP_AT = [0, 4, 7, 10]
GROUP_N = [4, 3, 3, 3]
GROUPS = len(GROUP_AT)
ROW_UNROLL = 4
PARTS = 12
CHUNKS = [(0, 4), (4, 7), (7, 10), (10, 13)]
RUNS = [(0, 0, 1), (0, 1, 4), (1, 4, 7), (2, 7, 10), (3, 10, 12), (3, 12, 13)]

PAIRS = IMAGES // 2
HEAD = 105
TAIL = TOKENS - HEAD
PAIR = 2 * TOKENS
EXPERTS = 8
F = 512
FC = F // 128
SLOT = 256
REGION = ALL + SLOT
DUMMY = EXPERTS * REGION
SLOTS = (ALL + EXPERTS * (SLOT - 1)) // SLOT
PAY = D + 4
NOBODY = 1 << 20
SLOT_UNROLL = 4
W_SCALE = 64.0
MASKED = -30000.0
SCORE_SCALE = 0.25 / float(np.sqrt(np.float32(D)))

C_ID, C_UP, C_TRI, C_TRIT, C_MULT = 0, 128, 256, 384, 448
C_DESC, C_RUN0, C_ID0, C_SLOT, C_END = 457, 465, 473, 476, 476 + 92


def constants():
    c = np.zeros((128, C_END), np.float32)
    k = np.arange(128)
    c[:, C_ID:C_ID + 128] = np.eye(128)
    c[:, C_UP:C_UP + 128] = k[:, None] < k[None, :]
    c[:, C_TRI:C_TRI + 128] = np.where(k[:, None] < k[None, :], 0.0, MASKED)
    c[:, C_TRIT:C_TRIT + 64] = np.where(k[:, None] % 64 < k[None, :64], 0.0, MASKED)
    r, s = k // 64, k // 32 % 2
    for a in range(3):
        for b in range(3):
            over = 2 - ((a == 0) & (r == 0)) - ((a == 2) & (r == 1))
            across = 2 - ((b == 0) & (s == 0)) - ((b == 2) & (s == 1))
            c[:, C_MULT + 3 * a + b] = 1 + over * across
    e = np.arange(EXPERTS)
    c[:, C_DESC:C_DESC + EXPERTS] = EXPERTS - e
    c[:, C_RUN0:C_RUN0 + EXPERTS] = e * REGION
    c[:, C_ID0] = k
    c[:, C_ID0 + 1] = TOKENS + k
    c[:, C_ID0 + 2] = np.where(k < TAIL, HEAD + k, TOKENS + HEAD + k - TAIL)
    c[:, C_SLOT:C_END] = np.arange(SLOTS)
    return c


def own_wait(eng, sem, value, passed):
    if not isinstance(value, int):
        value = eng.to_reg(value)
    eng.wait_ge(passed, 1)
    eng.wait_ge(sem, value)


class Kept:

    def __init__(self, nc):
        def sb(name, shape, dt=F32):
            return nc.alloc_sbuf_tensor(name, shape, dt)

        def dram(name, shape, dt=F32):
            return nc.dram_tensor(name, shape, dt, kind="Internal").ap()

        self.banks = [nc.alloc_psum_tensor(f"bank{i}", [128, 512], F32) for i in range(8)]
        self.const = sb("constants", [128, C_END])
        self.ident_bf = sb("ident_bf", [128, 128], BF16)
        self.w_qkv = sb("w_qkv", [128, 3, D])
        self.w_s = sb("w_s_sb", [128, EXPERTS])
        self.b_s = sb("b_s_sb", [128, EXPERTS])
        self.b1 = sb("b1_sb", [128, EXPERTS * FC])
        self.b2 = sb("b2_sb", [128, EXPERTS * D])
        self.w1_hi = sb("w1_hi", [128, EXPERTS * F], F16)
        self.w1_lo = sb("w1_lo", [128, EXPERTS * F], F16)
        self.run = [sb(f"run{i}", [128, EXPERTS]) for i in range(2)]
        self.h = dram("h_rows", (IMAGES, TOKENS * D))
        self.gb = dram("gamma_beta_parts", (PARTS, TOKENS * D), BF16)
        self.by_expert = dram("rows_by_expert", (DUMMY + SLOT, PAY))

    def col(self, at, n=1):
        return self.const[:, at:at + n]


def image_statistics(nc, kept, hnT, tok, a):
    with ExitStack() as ctx:
        def sb(name, shape, dt=F32):
            return ctx.enter_context(nc.sbuf_tensor("stats_" + name, shape, dt))

        def sem(name):
            return nc.alloc_semaphore("stats_" + name)

        ROW = GRID * IMAGES
        x_dram = a["x_al"].rearrange("p r c b -> p (r c b)")
        x = hnT[:, :].rearrange("p (r c b) -> p r c b", r=GRID, c=GRID)
        sq = sb("squares", [128, 2, 4 * ROW])
        red = sb("reduced_rows", [128, 2 * len(RUNS), IMAGES])
        beta = sb("beta_sb", [128, TOKENS, VARIANTS])
        b_tok = sb("b_tok_sb", [128, D])
        w1 = sb("w1_f32", [128, EXPERTS * F])
        rest = sb("parts_rest", [128, 2, 2, D])
        rest2 = sb("parts_rest2", [128, 2, 2, D])
        rest3 = sb("parts_rest3", [128, 2, 2, D])
        part = sb("parts", [128, 2, 2, 3, D], BF16)
        s12 = sb("image_sums", [128, 8])
        mhalf = sb("minus_half", [128, 1])
        sv = sb("minus_mean_and_deviation", [128, 2])
        svr = sb("image_parts_rest", [128, 2, 2])
        sp = sb("image_parts", [128, 2, 3], BF16)
        stp = sb("image_part_columns", [128, 2, 6])
        gb_ps, sum_ps, ssq_ps, st_ps = kept.banks[0], kept.banks[1], kept.banks[2], kept.banks[3]

        s_cst, s_wt, s_w, s_w1 = sem("c_loaded"), sem("tok_w_loaded"), sem("w_loaded"), sem("w1_loaded")
        s_x = [sem(f"x_chunk_loaded{i}") for i in range(4)]
        s_idb, s_sq, s_xred, s_sqred = sem("ident_cast"), sem("squared"), sem("x_reduced"), sem("sq_reduced")
        s_sums, s_gbp, s_ch, s_gbw = sem("sums_done"), sem("gb_products"), sem("split_step"), sem("gb_stored")
        s_pool, s_pow, s_stp, s_stT = sem("pool_step"), sem("rstd_img"), sem("stp_ready"), sem("stp_transposed")
        s_done, s_hi = sem("stT_ready"), sem("w1_hi_ready")
        s_ssq = sem("sq_products_done")
        T_AT, T_N = [0, 128], [128, TOKENS - 128]

        def squares(c):
            lo, hi = CHUNKS[c]
            return sq[:, c % 2, 0:(hi - lo) * ROW].rearrange("p (r c b) -> p r c b", c=GRID, b=IMAGES)

        with nc.Block() as block:
            @block.sync
            def _(sp_):
                sp_.dma_start(tok["w"][:, :, :], a["w_tok"]).then_inc(s_wt, 16)
                sp_.dma_start(tok["gamma"][:, :, :], a["gamma"]).then_inc(s_wt, 16)
                sp_.dma_start(beta[:, :, :], a["beta"]).then_inc(s_wt, 16)
                sp_.dma_start(kept.const[:, :], a["const"]).then_inc(s_cst, 16)
                for c, (lo, hi) in enumerate(CHUNKS):
                    sp_.dma_start(hnT[:, lo * ROW:hi * ROW], x_dram[:, lo * ROW:hi * ROW]).then_inc(s_x[c], 16)
                sp_.dma_start(w1[:, :], a["w1"]).then_inc(s_w1, 16)
                sp_.dma_start(b_tok[:, :], a["b_tok"].broadcast_to([128, D])).then_inc(s_w, 16)
                for i, n in enumerate(("w_q", "w_k", "w_v")):
                    sp_.dma_start(kept.w_qkv[:, i, :], a[n]).then_inc(s_w, 16)
                sp_.dma_start(kept.w_s[:, :], a["w_s"]).then_inc(s_w, 16)
                sp_.dma_start(kept.b_s[:, :], a["b_s"].broadcast_to([128, EXPERTS])).then_inc(s_w, 16)
                sp_.dma_start(kept.b1[:, :], a["b1"]).then_inc(s_w, 16)
                sp_.dma_start(kept.b2[:, :], a["b2"].broadcast_to([128, EXPERTS * D])).then_inc(s_w, 16)
                gb = kept.gb.rearrange("(q r) (t e) -> t q r e", q=2, e=D)
                for j in range(2):
                    sp_.wait_ge(s_ch, 6 * (j + 1))
                    for q in range(2):
                        for at, n in ((0, 3), (3, 2), (5, 1)):
                            sp_.dma_start(gb[T_AT[j]:T_AT[j] + T_N[j], q, at:at + n, :],
                                          part[0:T_N[j], j, q, 0:n, :]).then_inc(s_gbw, 16)
                sp_.wait_ge(s_gbw, 16 * 12)
                sp_.wait_ge(s_w, 16 * 8)

            @block.gpsimd
            def _(pool):
                nc.gpsimd.memset(mhalf[:, :], -0.5).then_inc(s_pool, 1)
                pool.wait_ge(s_hi, 1)
                nc.gpsimd.tensor_scalar(w1[:, :], w1[:, :], W_SCALE, None, ALU.mult).then_inc(s_pool, 1)
                pool.wait_ge(s_pool, 2)
                nc.gpsimd.tensor_tensor(kept.w1_lo[:, :], w1[:, :], kept.w1_hi[:, :], ALU.subtract)\
                    .then_inc(s_pool, 1)
                pool.wait_ge(s_stp, 4)
                nc.gpsimd.tensor_tensor(tok["rstd"][:, :], s12[:, 5:6], mhalf[:, :], ALU.pow).then_inc(s_pow, 1)

            @block.scalar
            def _(act):
                for c, (lo, hi) in enumerate(CHUNKS):
                    act.wait_ge(s_x[c], 16)
                    if c >= 2:
                        act.wait_ge(s_sqred, {2: 2, 3: 3}[c])
                        act.wait_ge(s_ssq, {2: 2, 3: 3}[c])
                    nc.scalar.activation(squares(c), x[:, lo:hi, :, :], ACT.Square).then_inc(s_sq, 1)
                act.wait_ge(s_w1, 16)
                nc.scalar.activation(kept.w1_hi[:, :], w1[:, :], ACT.Copy, scale=W_SCALE).then_inc(s_hi, 1)

            @block.vector
            def _(dve):
                dve.wait_ge(s_cst, 16)
                nc.vector.tensor_copy(kept.ident_bf[:, :], kept.col(C_ID, 128)).then_inc(s_idb, 1)
                for n, (c, first, end) in enumerate(RUNS):
                    dve.wait_ge(s_x[c], 16)
                    nc.vector.tensor_reduce(red[:, n, :], x[:, first:end, 1:GRID - 1, :]
                                            .rearrange("p r c b -> p b r c"), AX.XY, ALU.add).then_inc(s_xred, 1)
                for n, (c, first, end) in enumerate(RUNS):
                    dve.wait_ge(s_sq, c + 1)
                    at = CHUNKS[c][0]
                    nc.vector.tensor_reduce(red[:, len(RUNS) + n, :],
                                            squares(c)[:, first - at:end - at, 1:GRID - 1, :]
                                            .rearrange("p r c b -> p b r c"), AX.XY, ALU.add).then_inc(s_sqred, 1)
                dve.wait_ge(s_gbp, 1)
                dve.wait_ge(s_w, 16 * 8)
                steps = 0

                def link(ins):
                    nonlocal steps
                    steps += 1
                    ins.then_inc(s_ch, 1)
                    dve.wait_ge(s_ch, steps)

                for j in range(2):
                    n = T_N[j]
                    ps = gb_ps[0:n, 256 * j:256 * j + 256].rearrange("p (q e) -> p q e", q=2)
                    r = [t[0:n, j, :, :] for t in (rest, rest2, rest3)]
                    nc.vector.tensor_copy(r[0][:, 0, :], ps[:, 0, :])
                    link(nc.vector.tensor_tensor(r[0][:, 1, :], ps[:, 1, :], b_tok[0:n, :], ALU.add))
                    link(nc.vector.tensor_copy(part[0:n, j, :, 0, :], r[0]))
                    link(nc.vector.tensor_tensor(r[1], r[0], part[0:n, j, :, 0, :], ALU.subtract))
                    link(nc.vector.tensor_copy(part[0:n, j, :, 1, :], r[1]))
                    link(nc.vector.tensor_tensor(r[2], r[1], part[0:n, j, :, 1, :], ALU.subtract))
                    link(nc.vector.tensor_copy(part[0:n, j, :, 2, :], r[2]))
                dve.wait_ge(s_sums, 2)
                stp_steps = 0

                def then(ins):
                    nonlocal stp_steps
                    stp_steps += 1
                    ins.then_inc(s_stp, 1)
                    dve.wait_ge(s_stp, stp_steps)

                then(nc.vector.tensor_scalar(s12[:, 0:1], sum_ps[:, 0:1], 1.0 / PIXELS, None, ALU.mult))
                nc.vector.tensor_scalar(s12[:, 2:3], ssq_ps[:, 0:1], 1.0 / PIXELS, TOK_EPS, ALU.mult, ALU.add)
                then(nc.vector.tensor_tensor(s12[:, 3:4], s12[:, 0:1], s12[:, 0:1], ALU.mult))
                then(nc.vector.tensor_tensor(s12[:, 4:5], s12[:, 2:3], s12[:, 3:4], ALU.subtract))
                then(nc.vector.tensor_scalar(s12[:, 5:6], s12[:, 4:5], TOK_EPS, None, ALU.max))
                dve.wait_ge(s_pow, 1)
                nc.vector.tensor_scalar(sv[:, 0:1], s12[:, 0:1], -1.0, None, ALU.mult)
                then(nc.vector.tensor_tensor(sv[:, 1:2], s12[:, 5:6], tok["rstd"][:, :], ALU.mult))
                then(nc.vector.tensor_copy(sp[:, :, 0], sv[:, :]))
                then(nc.vector.tensor_tensor(svr[:, 0, :], sv[:, :], sp[:, :, 0], ALU.subtract))
                then(nc.vector.tensor_copy(sp[:, :, 1], svr[:, 0, :]))
                then(nc.vector.tensor_tensor(svr[:, 1, :], svr[:, 0, :], sp[:, :, 1], ALU.subtract))
                then(nc.vector.tensor_copy(sp[:, :, 2], svr[:, 1, :]))
                for q in range(2):
                    for at, n, p in ((0, 3, 0), (3, 2, 1), (5, 1, 2)):
                        last = nc.vector.tensor_copy(stp[:, q, at:at + n], sp[:, q, p:p + 1].broadcast_to([128, n]))
                then(last)
                dve.wait_ge(s_stT, 1)
                nc.vector.tensor_copy(tok["stT"][:, :], st_ps[0:PARTS, 0:IMAGES]).then_inc(s_done, 1)

            @block.tensor
            def _(pe):
                pe.wait_ge(s_wt, 48)
                for j in range(2):
                    for q, g in enumerate((tok["gamma"], beta)):
                        for v in range(VARIANTS):
                            last = nc.tensor.matmul(gb_ps[0:T_N[j], 256 * j + 128 * q:256 * j + 128 * q + D],
                                                    g[:, T_AT[j]:T_AT[j] + T_N[j], v], tok["w"][:, v, :],
                                                    start=v == 0, stop=v == VARIANTS - 1)
                last.then_inc(s_gbp, 1)
                pe.wait_ge(s_cst, 16)

                def edge(r):
                    return 0 if r == 0 else 2 if r == GRID - 1 else 1

                def sums(ps, source, ready, reduced, base, chunk_done):
                    for c, (lo, hi) in enumerate(CHUNKS):
                        ready(c)
                        for r in range(lo, hi):
                            for col, k in ((0, 0), (GRID - 1, 2)):
                                m = C_MULT + 3 * edge(r) + k
                                last = nc.tensor.matmul(ps[:, 0:1], source(c, r - lo, col), kept.col(m),
                                                        start=r == 0 and col == 0, stop=False)
                        if chunk_done is not None:
                            last.then_inc(chunk_done, 1)
                    for n, (c, first, end) in enumerate(RUNS):
                        pe.wait_ge(reduced, n + 1)
                        last = nc.tensor.matmul(ps[:, 0:1], red[:, base + n, :], kept.col(C_MULT + 3 * edge(first) + 1),
                                                start=False, stop=n == len(RUNS) - 1)
                    last.then_inc(s_sums, 1)

                sums(sum_ps, lambda c, r, col: x[:, CHUNKS[c][0] + r, col, :], lambda c: pe.wait_ge(s_x[c], 16),
                     s_xred, 0, None)
                sums(ssq_ps, lambda c, r, col: squares(c)[:, r, col, :], lambda c: pe.wait_ge(s_sq, c + 1),
                     s_sqred, len(RUNS), s_ssq)
                pe.wait_ge(s_stp, 11)
                nc.tensor.transpose(st_ps[0:PARTS, 0:IMAGES], stp[:, :, :].rearrange("p q r -> p (q r)"),
                                    kept.col(C_ID, 128)).then_inc(s_stT, 1)


def tokenizer(nc, kept, hnT, tok, a):
    with ExitStack() as ctx:
        def sb(name, shape, dt=F32):
            return ctx.enter_context(nc.sbuf_tensor("tok_" + name, shape, dt))

        def sem(name):
            return nc.alloc_semaphore("tok_" + name)

        xa = sb("x_aligned", [128, 2, GRID * IMAGES])
        xo = sb("x_offset", [128, 4, (GRID + 1) * IMAGES])
        gbr = sb("parts_row", [PARTS, 2, GRID * D], BF16)
        wg = sb("scaled_weights", [128, 4, VARIANTS, D])
        hrow = sb("h_row", [128, 2, GRID, D])
        hn = sb("h_normalised", [128, 2, 4, D])
        bn6 = sb("bn_stats", [128, 2, GRID, 6])
        mv = sb("mean_var", [128, 2, GRID, 2])
        ve = sb("var_eps", [128, 4])
        rs = sb("rstd", [128, 2, GRID])
        mhalf = sb("minus_half", [128, 4])
        eps = sb("eps", [128, 4])
        acc, tp = kept.banks[0:4], kept.banks[4:6]

        s_xa = [sem(f"x_aligned_loaded{i}") for i in range(2)]
        s_xo = [sem(f"x_offset_loaded{i}") for i in range(4)]
        s_gb = [sem(f"parts_row_loaded{i}") for i in range(2)]
        s_wgd, s_wga, s_tok = sem("weights_scaled_dve"), sem("weights_scaled_act"), sem("token_products")
        s_h, s_hst = sem("h_ready"), [sem(f"h_stored{i}") for i in range(2)]
        s_bn, s_mv, s_ve, s_rs = sem("bn_stats_done"), sem("mean_var_ready"), sem("var_eps_ready"), sem("rstd_ready")
        s_hn, s_tp, s_hnT, s_mh = sem("hn_ready"), sem("hn_transposed"), sem("hnT_written"), sem("mhalf_set")

        xa_d = a["x_al"].rearrange("p r c b -> p (r c b)")
        xo_d = a["x_off"].rearrange("p r c b -> p (r c b)")
        hnT_t = hnT[:, :].rearrange("p (b t) -> p t b", t=TOKENS)
        XA, XO, RD = GRID * IMAGES, (GRID + 1) * IMAGES, GRID * D

        def rows(eng, row):
            row(0, 0)
            with eng.Fori(0, (GRID - 1) // ROW_UNROLL) as i:
                for j in range(1, ROW_UNROLL + 1):
                    row(i, j)

        def lagged(i, j, g, lag):
            n = GROUPS * j + g - lag
            return None if n < 0 else (i, n // GROUPS, n % GROUPS)

        def drained(step, lag):
            i, j = (GRID - 1) // ROW_UNROLL - 1, ROW_UNROLL
            for n in range(lag):
                step(*lagged(i, j + 1, n, lag))

        def weights_free(eng, i, j, pj):
            before = GRID if pj == GRID - 1 else 4 if pj < 3 else 3
            if GRID * j + pj - before >= 0:
                eng.wait_ge(s_tok, GRID * (ROW_UNROLL * i + j) + pj - before + 1)

        def slot(pj):
            return 3 if pj == GRID - 1 else pj % 3

        with nc.Block() as block:
            @block.sync
            def _(sp):
                def load_xa(pi, n):
                    sp.dma_start(xa[:, n % 2, :], xa_d[:, bass.ds(pi * XA, XA)]).then_inc(s_xa[n % 2], 16)
                    sp.dma_start(gbr[:, n % 2, :], kept.gb[:, bass.ds(pi * RD, RD)]).then_inc(s_gb[n % 2], 16)

                def load_xo(pi, n):
                    sp.dma_start(xo[:, n % 4, :], xo_d[:, bass.ds(pi * XO, XO)]).then_inc(s_xo[n % 4], 16)

                def store(pi, j):
                    sp.wait_ge(s_h, GROUPS * (pi + 1))
                    sp.dma_start(kept.h[:, bass.ds(pi * RD, RD)],
                                 hrow[:, j % 2, :, :].rearrange("p t d -> p (t d)")).then_inc(s_hst[j % 2], 16)

                def refill(i, j, last):
                    pi = ROW_UNROLL * i + j
                    sp.wait_ge(s_tok, GRID * pi)
                    if not last or pi + 1 < GRID:
                        load_xa(pi + 1, j + 1)
                    if not last or pi + 3 < GRID + 1:
                        load_xo(pi + 3, j + 3)
                    store(pi - 1, j - 1)

                load_xa(0, 0)
                for n in range(4):
                    load_xo(n, n)
                    if n == 1:
                        load_xa(1, 1)
                with sp.Fori(0, 2) as i:
                    for j in range(1, ROW_UNROLL + 1):
                        refill(i, j, False)
                for j in range(1, ROW_UNROLL + 1):
                    refill(2, j, True)
                store(GRID - 1, 0)
                sp.wait_ge(s_hst[0], 16 * 7)
                sp.wait_ge(s_hst[1], 16 * 6)

            @block.scalar
            def _(act):
                def evacuate(i, j, g):
                    q, t = GROUPS * (ROW_UNROLL * i + j) + g, GRID * (ROW_UNROLL * i + j)
                    n = GROUP_N[g]
                    act.wait_ge(s_tok, t + GROUP_AT[g] + n)
                    nc.scalar.activation(hrow[:, j % 2, GROUP_AT[g]:GROUP_AT[g] + n, :].rearrange("p t d -> p (t d)"),
                                         acc[g][:, 0:n * D], ACT.Copy, scale=tok["rstd"][:, 0:1]).then_inc(s_h, 1)

                def write_hnT(i, j, g):
                    q, t = GROUPS * (ROW_UNROLL * i + j) + g, GRID * (ROW_UNROLL * i + j)
                    n = GROUP_N[g]
                    act.wait_ge(s_tp, q + 1)
                    nc.scalar.activation(hnT_t[:, bass.ds(t + GROUP_AT[g], n), :],
                                         tp[g % 2][:, 0:n * D].rearrange("p (t b) -> p t b", t=n),
                                         ACT.Copy).then_inc(s_hnT, 1)

                def row(i, j):
                    for g in range(GROUPS):
                        for pj in range(GROUP_AT[g], GROUP_AT[g] + GROUP_N[g]):
                            weights_free(act, i, j, pj)
                            t = GRID * (ROW_UNROLL * i + j) + pj
                            for v in (3, 4):
                                last = nc.scalar.activation(wg[:, slot(pj), v, :], tok["w"][:, v, :], ACT.Copy,
                                                            scale=tok["gamma"][:, bass.ds(t, 1), v])
                            last.then_inc(s_wga, 1)
                        if g == GROUPS - 1 and j > 0:
                            pi = ROW_UNROLL * i + j
                            act.wait_ge(s_hst[(j - 1) % 2], 16 * (2 * i + (j - 1) // 2 + 1))
                            act.wait_ge(s_hn, GROUPS * pi)
                        if (at := lagged(i, j, g, 1)) is not None:
                            evacuate(*at)
                        if (at := lagged(i, j, g, 4)) is not None:
                            write_hnT(*at)

                rows(act, row)
                last_i, last_j = (GRID - 1) // ROW_UNROLL - 1, ROW_UNROLL
                evacuate(last_i, last_j, GROUPS - 1)
                drained(write_hnT, 4)

            @block.vector
            def _(dve):
                nc.vector.memset(mhalf[:, :], -0.5).then_inc(s_mh, 1)
                nc.vector.memset(eps[:, :], LN_EPS).then_inc(s_mh, 1)

                def statistics(i, j, g):
                    q, t = GROUPS * (ROW_UNROLL * i + j) + g, GRID * (ROW_UNROLL * i + j)
                    dve.wait_ge(s_h, q + 1)
                    for pj in range(GROUP_AT[g], GROUP_AT[g] + GROUP_N[g]):
                        last = nc.vector.bn_stats(bn6[:, j % 2, pj, :], hrow[:, j % 2, pj, :])
                    last.then_inc(s_bn, 1)

                def aggregate(i, j, g):
                    q = GROUPS * (ROW_UNROLL * i + j) + g
                    own_wait(dve, s_bn, q + 1, s_mh)
                    for pj in range(GROUP_AT[g], GROUP_AT[g] + GROUP_N[g]):
                        last = nc.vector.bn_aggr(mv[:, j % 2, pj, :], bn6[:, j % 2, pj, :])
                    last.then_inc(s_mv, 1)

                def normalise(i, j, g):
                    q = GROUPS * (ROW_UNROLL * i + j) + g
                    dve.wait_ge(s_rs, q + 1)
                    if GROUPS * j + g >= 2:
                        dve.wait_ge(s_tp, q - 1)
                    for n in range(GROUP_N[g]):
                        pj = GROUP_AT[g] + n
                        last = nc.vector.tensor_scalar(hn[:, g % 2, n, :], hrow[:, j % 2, pj, :],
                                                       mv[:, j % 2, pj, 0:1], rs[:, j % 2, pj:pj + 1],
                                                       ALU.subtract, ALU.mult)
                    last.then_inc(s_hn, 1)

                def row(i, j):
                    for g in range(GROUPS):
                        for pj in range(GROUP_AT[g], GROUP_AT[g] + GROUP_N[g]):
                            weights_free(dve, i, j, pj)
                            t = GRID * (ROW_UNROLL * i + j) + pj
                            for v in range(3):
                                last = nc.vector.tensor_scalar(wg[:, slot(pj), v, :], tok["w"][:, v, :],
                                                               tok["gamma"][:, bass.ds(t, 1), v], None, ALU.mult)
                            last.then_inc(s_wgd, 1)
                        if g == GROUPS - 1 and j > 0:
                            dve.wait_ge(s_hn, GROUPS * (ROW_UNROLL * i + j))
                        if (at := lagged(i, j, g, 1)) is not None:
                            statistics(*at)
                        if (at := lagged(i, j, g, 2)) is not None:
                            normalise(*at)
                        if (at := lagged(i, j, g, 1)) is not None:
                            aggregate(*at)

                rows(dve, row)
                last_i, last_j = (GRID - 1) // ROW_UNROLL - 1, ROW_UNROLL
                statistics(last_i, last_j, GROUPS - 1)
                aggregate(last_i, last_j, GROUPS - 1)
                drained(normalise, 2)

            @block.gpsimd
            def _(pool):
                pool.wait_ge(s_mh, 2)

                def row(i, j):
                    for g in range(GROUPS):
                        q = GROUPS * (ROW_UNROLL * i + j) + g
                        pj, n = GROUP_AT[g], GROUP_N[g]
                        pool.wait_ge(s_mv, q + 1)
                        if GROUPS * j + g > 0:
                            pool.wait_ge(s_rs, q)
                        nc.gpsimd.tensor_tensor(ve[:, 0:n], mv[:, j % 2, pj:pj + n, 1], eps[:, 0:n], ALU.add)\
                            .then_inc(s_ve, 1)
                        pool.wait_ge(s_ve, q + 1)
                        nc.gpsimd.tensor_tensor(rs[:, j % 2, pj:pj + n], ve[:, 0:n], mhalf[:, 0:n], ALU.pow)\
                            .then_inc(s_rs, 1)

                rows(pool, row)

            @block.tensor
            def _(pe):
                def transposes(i, j, g):
                    q = GROUPS * (ROW_UNROLL * i + j) + g
                    pe.wait_ge(s_hn, q + 1)
                    if GROUPS * j + g >= 2:
                        pe.wait_ge(s_hnT, q - 1)
                    for n in range(GROUP_N[g]):
                        last = nc.tensor.transpose(tp[g % 2][:, n * D:(n + 1) * D], hn[:, g % 2, n, :],
                                                   kept.col(C_ID, 128))
                    last.then_inc(s_tp, 1)

                def row(i, j):
                    pi = ROW_UNROLL * i + j
                    pe.wait_ge(s_xa[j % 2], 16 * (2 * i + j // 2 + 1))
                    pe.wait_ge(s_gb[j % 2], 16 * (2 * i + j // 2 + 1))
                    pe.wait_ge(s_xo[j % 4], 16 * (i + j // 4 + 1))
                    pe.wait_ge(s_xo[(j + 1) % 4], 16 * (i + (j + 1) // 4 + 1))
                    for g in range(GROUPS):
                        if j > 0:
                            pe.wait_ge(s_h, GROUPS * pi + g - 3)
                        for n in range(GROUP_N[g]):
                            pj = GROUP_AT[g] + n
                            o = acc[g][:, n * D:(n + 1) * D]
                            nc.tensor.matmul(o, tok["stT"][:, :], gbr[:, j % 2, pj * D:(pj + 1) * D],
                                             start=True, stop=False)
                            pe.wait_ge(s_wgd, GRID * pi + pj + 1)
                            for v in range(VARIANTS):
                                if v == 3:
                                    pe.wait_ge(s_wga, GRID * pi + pj + 1)
                                if v == 0:
                                    patch = xa[:, j % 2, pj * IMAGES:(pj + 1) * IMAGES]
                                else:
                                    up, left = v <= 2, v in (1, 3)
                                    r, c = (j + up) % 4, pj + (not left)
                                    patch = xo[:, r, c * IMAGES:(c + 1) * IMAGES]
                                last = nc.tensor.matmul(o, patch, wg[:, slot(pj), v, :], start=False,
                                                        stop=v == VARIANTS - 1)
                            last.then_inc(s_tok, 1)
                        if (at := lagged(i, j, g, 3)) is not None:
                            transposes(*at)

                rows(pe, row)
                drained(transposes, 3)


def attention(nc, kept, hnT, a):
    with ExitStack() as ctx:
        def sb(name, shape, dt=F32):
            return ctx.enter_context(nc.sbuf_tensor("attn_" + name, shape, dt))

        def sem(name):
            return nc.alloc_semaphore("attn_" + name)

        upper_bf = sb("upper_bf", [128, 128], BF16)
        ones_bf = sb("ones_bf", [128, 128], BF16)
        tri_bf = sb("tri_bf", [128, 128 + 64], BF16)
        x2 = sb("x_pair", [128, 2, PAIR])
        tqk = sb("tanh_qk", [128, 2, 2, PAIR])
        qk = sb("sigmoid_qk", [128, 2, 2, PAIR])
        tv = sb("tanh_v", [128, 2, 3, D])
        v1 = sb("sigmoid_v_and_twos", [128, 2, 3, D + 1])
        e = sb("exp_scores", [128, 2, PAIR + TAIL])
        hin = sb("h_in", [128, 2, 3, D])
        den = sb("denominators", [128, 2, 3])
        pay = sb("payload", [128, 2, 3, PAY])
        bn6 = sb("bn_stats2", [128, 3, 6])
        ve = sb("var_eps2", [128, 3])
        mhalf = sb("minus_half2", [128, 3])
        eps, two_pairs = sb("eps", [128, 3]), sb("two_pairs", [128, 3], I32)
        xn = sb("x_normalised", [128, 2, 3, D])
        xT = sb("x_transposed", [128, 2, 3, D])
        lb, d = sb("logits", [128, 3, EXPERTS]), sb("logits_less_max", [128, 3, EXPERTS])
        w, m, m2 = sb("tie_order", [128, 3, EXPERTS]), sb("max_logit", [128, 3]), sb("first_max", [128, 3])
        oh = sb("one_hot", [128, 2, 3, EXPERTS], BF16)
        ex = sb("exp_logits", [128, 2, 3, EXPERTS])
        se, rr, rro, pos = (sb("sum_exp", [128, 3]), sb("ranks", [128, 3, EXPERTS]),
                            sb("own_rank", [128, 3, EXPERTS]), sb("position", [128, 3]))
        idx = sb("row_index", [128, 2, 3], I32)
        qk_ps = kept.banks[0:2]
        v_ps, s_ps, o_ps, t_ps, lg_ps, rk_ps = kept.banks[2:8]
        N = [HEAD, HEAD, 128]

        s_init, s_x2, s_qkps, s_tqk, s_qk = sem("a_init"), sem("x2"), sem("qk_ps"), sem("tanh_qk"), sem("qk")
        s_vps, s_tv, s_v = sem("v_ps"), sem("tanh_v"), sem("v")
        s_sps, s_e, s_ops = sem("scores_ps"), sem("exp_scores"), sem("o_ps")
        s_hin = [sem(f"h_in{i}") for i in range(2)]
        s_h2, s_bn, s_mv, s_pool, s_rs = sem("h2"), sem("bn2"), sem("mv2"), sem("pool_step2"), sem("rstd2")
        s_xn, s_tps, s_xT, s_lg = sem("xn2"), sem("xT_ps"), sem("xT"), sem("logits_ps")
        s_placed = sem("placed")
        s_rt, s_ex, s_rk = sem("routing_step"), sem("exp_logits"), sem("ranks_ps")
        s_den = sem("den_step")
        s_sc = [sem(f"scattered{i}") for i in range(2)]
        INITS = 18
        R1, R = 6, 12

        PEEL, UNROLL = 5, 2
        LOOPS = (PAIRS - PEEL) // UNROLL

        def steps(eng, step):
            for n in range(PEEL):
                step(0, n, lambda lag, n=n: n >= lag)
            with eng.Fori(0, LOOPS) as i:
                for j in range(PEEL, PEEL + UNROLL):
                    step(i, j, lambda lag: True)
            for n in range(PEEL + UNROLL * LOOPS, PAIRS + 3):
                step(LOOPS, n - UNROLL * LOOPS, lambda lag, n=n: n - lag < PAIRS)

        with nc.Block() as block:
            @block.sync
            def _(sp):
                def load(i, j):
                    p = 2 * i + j
                    if j >= 2:
                        sp.wait_ge(s_h2, p - 1)
                    h = kept.h
                    sp.dma_start(hin[0:HEAD, j % 2, 0:2, :], h[bass.ds(2 * p, 2), 0:HEAD * D]
                                 .rearrange("b (t e) -> t b e", e=D)).then_inc(s_hin[j % 2], 16)
                    for k in range(2):
                        sp.dma_start(hin[TAIL * k:TAIL * (k + 1), j % 2, 2, :], h[bass.ds(2 * p + k, 1), HEAD * D:]
                                     .rearrange("b (t e) -> (b t) e", e=D)).then_inc(s_hin[j % 2], 16)

                steps(sp, lambda i, j, live: live(0) and load(i, j))

            @block.gpsimd
            def _(pool):
                pool.wait_ge(s_init, INITS)
                last_row = pool.to_reg(DUMMY - 1)

                def rstd(i, j):
                    p = 2 * i + j
                    pool.wait_ge(s_mv, p + 1)
                    o = pay[:, j % 2, :, :]
                    if j >= 1:
                        pool.wait_ge(s_rs, p)
                    nc.gpsimd.tensor_tensor(ve[:, :], o[:, :, D + 1], eps[:, :], ALU.add).then_inc(s_pool, 1)
                    if j >= 2:
                        number = o[:, :, D + 3].bitcast(I32)
                        nc.gpsimd.tensor_tensor(number, number, two_pairs[:, :], ALU.add)
                    pool.wait_ge(s_pool, p + 1)
                    nc.gpsimd.tensor_tensor(o[:, :, D + 1], ve[:, :], mhalf[:, :], ALU.pow).then_inc(s_rs, 1)

                def scatter(i, j):
                    p = 2 * i + j
                    own_wait(pool, s_placed, p + 1, s_init)
                    for k in range(3):
                        n = N[k]
                        nc.gpsimd.indirect_dma_start(
                            out=kept.by_expert[:, :],
                            out_offset=bass.IndirectOffsetOnAxis(ap=idx[0:n, j % 2, k:k + 1], axis=0),
                            in_=pay[0:n, j % 2, k, :], in_offset=None,
                            bounds_check=last_row, oob_is_err=False).then_inc(s_sc[j % 2], 16)

                def step(i, j, live):
                    if live(2):
                        rstd(i, j - 2)
                    if live(3):
                        scatter(i, j - 3)

                steps(pool, step)
                pool.wait_ge(s_sc[0], 48 * (PAIRS // 2))
                pool.wait_ge(s_sc[1], 48 * (PAIRS // 2))

            @block.scalar
            def _(act):
                nc.scalar.preload_act_table(ACT.Exp)
                act.wait_ge(s_init, INITS)

                def copy_x(i, j):
                    if j >= 2:
                        act.wait_ge(s_vps, 2 * i + j - 1)
                    nc.scalar.activation(x2[:, j % 2, :], hnT[:, bass.ds((2 * i + j) * PAIR, PAIR)], ACT.Copy)\
                        .then_inc(s_x2, 1)

                def tanh_qk(i, j):
                    p = 2 * i + j
                    act.wait_ge(s_qkps, p + 1)
                    if j >= 2:
                        act.wait_ge(s_qk, p - 1)
                    for k in range(2):
                        last = nc.scalar.activation(tqk[:, j % 2, k, :], qk_ps[k][:, 0:PAIR], ACT.Tanh, scale=0.5)
                    last.then_inc(s_tqk, 1)

                def tanh_v(i, j):
                    p = 2 * i + j
                    act.wait_ge(s_vps, p + 1)
                    if j >= 2:
                        act.wait_ge(s_v, p - 1)
                    nc.scalar.activation(tv[:, j % 2, :, :].rearrange("p k e -> p (k e)"), v_ps[:, 0:3 * D],
                                         ACT.Tanh, scale=0.5).then_inc(s_tv, 1)

                def exp_scores(i, j):
                    p = 2 * i + j
                    act.wait_ge(s_sps, p + 1)
                    if j >= 2:
                        act.wait_ge(s_ops, p - 1)
                    nc.scalar.activation(e[:, j % 2, :], s_ps[:, 0:PAIR + TAIL], ACT.Exp, scale=SCORE_SCALE)\
                        .then_inc(s_e, 1)

                def copy_xT(i, j):
                    p = 2 * i + j
                    act.wait_ge(s_tps, p + 1)
                    if j >= 2:
                        act.wait_ge(s_lg, p - 1)
                    nc.scalar.activation(xT[:, j % 2, :, :].rearrange("p k e -> p (k e)"), t_ps[:, 0:3 * D],
                                         ACT.Copy).then_inc(s_xT, 1)

                def exp_logits(i, j):
                    p = 2 * i + j
                    act.wait_ge(s_rt, R * p + 3)
                    nc.scalar.activation(ex[:, j % 2, :, :], d[:, :, :], ACT.Exp).then_inc(s_ex, 1)

                def step(i, j, live):
                    if live(0):
                        copy_x(i, j)
                    if live(3):
                        copy_xT(i, j - 3)
                    if live(1):
                        tanh_qk(i, j - 1)
                    if live(3):
                        exp_logits(i, j - 3)
                    if live(1):
                        tanh_v(i, j - 1)
                        exp_scores(i, j - 1)

                steps(act, step)

            @block.vector
            def _(dve):
                inits = [
                    nc.vector.tensor_copy(upper_bf[:, :], kept.col(C_UP, 128)),
                    nc.vector.memset(ones_bf[:, :], 1.0),
                    nc.vector.tensor_copy(tri_bf[:, :], kept.col(C_TRI, 128 + 64)),
                    nc.vector.memset(v1[:, :, :, D:D + 1], 2.0),
                    nc.vector.memset(mhalf[:, :], -0.5),
                    nc.vector.memset(pay[:, :, :, 0:D + 3], 1.0),
                    nc.vector.tensor_copy(pay[:, 0, :, D + 3].bitcast(I32), kept.col(C_ID0, 3)),
                    nc.vector.tensor_scalar(pay[:, 1, :, D + 3].bitcast(I32), kept.col(C_ID0, 3), float(PAIR), None, ALU.add),
                    nc.vector.tensor_copy(kept.run[0][:, :], kept.col(C_RUN0, EXPERTS)),
                    nc.vector.memset(xn[:, :, :, :], 0.0),
                    nc.vector.memset(v_ps[:, :], 0.0),
                    nc.vector.memset(s_ps[:, :], 0.0),
                    nc.vector.memset(o_ps[:, :], 0.0),
                    nc.vector.memset(t_ps[:, :], 0.0),
                    nc.vector.memset(lg_ps[:, :], 0.0),
                    nc.vector.memset(rk_ps[:, :], 0.0),
                    nc.vector.memset(eps[:, :], LN_EPS),
                    nc.vector.memset(two_pairs[:, :], 2 * PAIR),
                ]
                assert len(inits) == INITS
                for ins in inits:
                    ins.then_inc(s_init, 1)
                dve.wait_ge(s_init, INITS)

                def plus_one_qk(i, j):
                    p = 2 * i + j
                    dve.wait_ge(s_tqk, p + 1)
                    if j >= 2:
                        dve.wait_ge(s_sps, p - 1)
                    nc.vector.tensor_scalar(qk[:, j % 2, :, :], tqk[:, j % 2, :, :], 1.0, None, ALU.add)\
                        .then_inc(s_qk, 1)

                def plus_one_v(i, j):
                    p = 2 * i + j
                    dve.wait_ge(s_tv, p + 1)
                    if j >= 2:
                        dve.wait_ge(s_ops, p - 1)
                    nc.vector.tensor_scalar(v1[:, j % 2, :, 0:D], tv[:, j % 2, :, :], 1.0, None, ALU.add)\
                        .then_inc(s_v, 1)

                def residual(i, j):
                    p = 2 * i + j
                    o = o_ps[:, 0:3 * (D + 1)].rearrange("p (k e) -> p k e", k=3)
                    dve.wait_ge(s_ops, p + 1)
                    nc.vector.tensor_scalar(den[:, 0, :], o[:, :, D], 1e-30, None, ALU.max).then_inc(s_den, 1)
                    dve.wait_ge(s_den, 2 * p + 1)
                    nc.vector.reciprocal(den[:, 1, :], den[:, 0, :]).then_inc(s_den, 1)
                    dve.wait_ge(s_den, 2 * p + 2)
                    dve.wait_ge(s_hin[j % 2], 48 * (i + j // 2 + 1))
                    if j >= 2:
                        dve.wait_ge(s_sc[j % 2], 48 * (i + j // 2))
                    for k in range(3):
                        last = nc.vector.scalar_tensor_tensor(
                            out=pay[0:N[k], j % 2, k, 0:D], in0=o[0:N[k], k, 0:D], scalar=den[0:N[k], 1, k:k + 1],
                            in1=hin[0:N[k], j % 2, k, :], op0=ALU.mult, op1=ALU.add)
                    last.then_inc(s_h2, 1)
                    dve.wait_ge(s_h2, p + 1)
                    for k in range(3):
                        last = nc.vector.bn_stats(bn6[0:N[k], k, :], pay[0:N[k], j % 2, k, 0:D])
                    last.then_inc(s_bn, 1)

                def aggregate(i, j):
                    own_wait(dve, s_bn, 2 * i + j + 1, s_init)
                    for k in range(3):
                        last = nc.vector.bn_aggr(pay[0:N[k], j % 2, k, D:D + 2], bn6[0:N[k], k, :])
                    last.then_inc(s_mv, 1)

                def normalise(i, j):
                    p = 2 * i + j
                    dve.wait_ge(s_rs, p + 1)
                    if j >= 2:
                        dve.wait_ge(s_tps, p - 1)
                    for k in range(3):
                        n = N[k]
                        last = nc.vector.tensor_scalar(xn[0:n, j % 2, k, :], pay[0:n, j % 2, k, 0:D],
                                                       pay[0:n, j % 2, k, D:D + 1], pay[0:n, j % 2, k, D + 1:D + 2],
                                                       ALU.subtract, ALU.mult)
                    last.then_inc(s_xn, 1)

                def over_tiles(t):
                    return t[:, :].unsqueeze(1).broadcast_to([128, 3, EXPERTS])

                def over_experts(t):
                    return t[:, :].unsqueeze(2).broadcast_to([128, 3, EXPERTS])

                def choose(i, j):
                    base = R * (2 * i + j)

                    def link(ins, n):
                        ins.then_inc(s_rt, 1)
                        dve.wait_ge(s_rt, base + n)

                    dve.wait_ge(s_lg, 2 * i + j + 1)
                    if j >= 1:
                        dve.wait_ge(s_ex, 2 * i + j)
                    if j >= 2:
                        dve.wait_ge(s_rk, 2 * i + j - 1)
                    desc = kept.col(C_DESC, EXPERTS)
                    lg = lg_ps[:, 0:3 * EXPERTS].rearrange("p (k e) -> p k e", k=3)
                    link(nc.vector.tensor_tensor(lb[:, :, :], lg, over_tiles(kept.b_s), ALU.add), 1)
                    link(nc.vector.tensor_reduce(m[:, :], lb[:, :, :], AX.X, ALU.max), 2)
                    link(nc.vector.tensor_tensor(d[:, :, :], lb[:, :, :], over_experts(m), ALU.subtract), 3)
                    link(nc.vector.scalar_tensor_tensor(out=w[:, :, :], in0=d[:, :, :], scalar=0.0,
                                                        in1=desc.unsqueeze(1).broadcast_to([128, 3, EXPERTS]),
                                                        op0=ALU.is_equal, op1=ALU.mult), 4)
                    link(nc.vector.tensor_reduce(m2[:, :], w[:, :, :], AX.X, ALU.max), 5)
                    link(nc.vector.tensor_tensor(oh[:, j % 2, :, :], w[:, :, :], over_experts(m2), ALU.is_equal), 6)

                def place(i, j):
                    p = 2 * i + j
                    base = R * p

                    def link(ins, n):
                        ins.then_inc(s_rt, 1)
                        dve.wait_ge(s_rt, base + n)

                    if j >= 1:
                        dve.wait_ge(s_placed, p)
                    rk = rk_ps[:, 0:3 * EXPERTS].rearrange("p (k e) -> p k e", k=3)
                    run, run_next = kept.run[j % 2], kept.run[(j + 1) % 2]
                    dve.wait_ge(s_ex, p + 1)
                    link(nc.vector.tensor_reduce(se[:, :], ex[:, j % 2, :, :], AX.X, ALU.add), 7)
                    link(nc.vector.reciprocal(pay[:, j % 2, :, D + 2], se[:, :]), 8)
                    dve.wait_ge(s_rk, p + 1)
                    link(nc.vector.tensor_tensor(rr[:, :, :], rk, over_tiles(run), ALU.add), 9)
                    link(nc.vector.tensor_tensor(rro[:, :, :], rr[:, :, :], oh[:, j % 2, :, :], ALU.mult), 10)
                    link(nc.vector.tensor_reduce(pos[:, :], rro[:, :, :], AX.X, ALU.add), 11)
                    link(nc.vector.tensor_copy(idx[:, j % 2, :], pos[:, :]), 12)
                    nc.vector.tensor_tensor(run_next[:, :], run[:, :], rk_ps[:, 24:32], ALU.add).then_inc(s_placed, 1)

                def step(i, j, live):
                    if live(1):
                        plus_one_qk(i, j - 1)
                    if live(3):
                        choose(i, j - 3)
                    if live(2):
                        residual(i, j - 2)
                    if live(1):
                        plus_one_v(i, j - 1)
                    if live(2):
                        aggregate(i, j - 2)
                        normalise(i, j - 2)
                    if live(3):
                        place(i, j - 3)

                steps(dve, step)

            @block.tensor
            def _(pe):
                pe.wait_ge(s_init, INITS)

                def queries_keys(i, j):
                    p = 2 * i + j
                    pe.wait_ge(s_x2, p + 1)
                    if j >= 1:
                        pe.wait_ge(s_tqk, p)
                    for k in range(2):
                        last = nc.tensor.matmul(qk_ps[k][:, 0:PAIR], kept.w_qkv[:, k, :], x2[:, j % 2, :],
                                                start=True, stop=True)
                    last.then_inc(s_qkps, 1)

                def values(i, j):
                    if j >= 1:
                        pe.wait_ge(s_tv, 2 * i + j)
                    for k in range(2):
                        at = k * TOKENS
                        nc.tensor.matmul(v_ps[0:HEAD, k * D:(k + 1) * D], x2[:, j % 2, at:at + HEAD],
                                         kept.w_qkv[:, 2, :], start=True, stop=True)
                        last = nc.tensor.matmul(v_ps[TAIL * k:TAIL * (k + 1), 2 * D:3 * D],
                                                x2[:, j % 2, at + HEAD:at + TOKENS], kept.w_qkv[:, 2, :],
                                                start=True, stop=True)
                    last.then_inc(s_vps, 1)

                def scores(i, j):
                    p = 2 * i + j
                    pe.wait_ge(s_qk, p + 1)
                    if j >= 1:
                        pe.wait_ge(s_e, p)
                    for k in range(2):
                        at = k * TOKENS
                        q, key = qk[:, j % 2, 0, :], qk[:, j % 2, 1, :]
                        nc.tensor.matmul(s_ps[0:HEAD, at:at + TOKENS], key[:, at:at + HEAD], q[:, at:at + TOKENS],
                                         start=True, stop=False)
                        nc.tensor.matmul(s_ps[0:HEAD, at:at + HEAD], kept.ident_bf[0:HEAD, 0:HEAD],
                                         tri_bf[0:HEAD, 0:HEAD], start=False, stop=True)
                        r = slice(TAIL * k, TAIL * (k + 1))
                        nc.tensor.matmul(s_ps[r, PAIR:PAIR + TAIL], key[:, at + HEAD:at + TOKENS],
                                         q[:, at + HEAD:at + TOKENS], start=True, stop=False)
                        last = nc.tensor.matmul(s_ps[r, PAIR:PAIR + TAIL], kept.ident_bf[r, r], tri_bf[r, 128:192],
                                                start=False, stop=True)
                    last.then_inc(s_sps, 1)

                def attend(i, j):
                    p = 2 * i + j
                    pe.wait_ge(s_e, p + 1)
                    pe.wait_ge(s_v, p + 1)
                    if j >= 1:
                        pe.wait_ge(s_h2, p)
                    es, vs = e[:, j % 2, :], v1[:, j % 2, :, :]
                    for k in range(2):
                        at, r = k * TOKENS, slice(TAIL * k, TAIL * (k + 1))
                        nc.tensor.matmul(o_ps[0:HEAD, k * (D + 1):(k + 1) * (D + 1)], es[0:HEAD, at:at + HEAD],
                                         vs[0:HEAD, k, :], start=True, stop=True)
                        o = o_ps[r, 2 * (D + 1):3 * (D + 1)]
                        nc.tensor.matmul(o, es[0:HEAD, at + HEAD:at + TOKENS], vs[0:HEAD, k, :], start=True, stop=False)
                        last = nc.tensor.matmul(o, es[r, PAIR:PAIR + TAIL], vs[r, 2, :], start=False, stop=True)
                    last.then_inc(s_ops, 1)

                def transposes(i, j):
                    p = 2 * i + j
                    pe.wait_ge(s_xn, p + 1)
                    if j >= 1:
                        pe.wait_ge(s_xT, p)
                    for k in range(3):
                        n = N[k]
                        last = nc.tensor.transpose(t_ps[:, k * D:k * D + n], xn[0:n, j % 2, k, :],
                                                   kept.const[0:n, C_ID:C_ID + n])
                    last.then_inc(s_tps, 1)

                def logits(i, j):
                    p = 2 * i + j
                    pe.wait_ge(s_xT, p + 1)
                    if j >= 1:
                        pe.wait_ge(s_rt, R * p - R + 1)
                    for k in range(3):
                        last = nc.tensor.matmul(lg_ps[0:N[k], k * EXPERTS:(k + 1) * EXPERTS], xT[:, j % 2, k, 0:N[k]],
                                                kept.w_s[:, :], start=True, stop=True)
                    last.then_inc(s_lg, 1)

                def ranks(i, j):
                    p = 2 * i + j
                    pe.wait_ge(s_rt, R * p + R1)
                    if j >= 1:
                        pe.wait_ge(s_placed, p)
                    for k in range(3):
                        o = rk_ps[:, k * EXPERTS:(k + 1) * EXPERTS]
                        for before in range(k):
                            nc.tensor.matmul(o, ones_bf[0:N[before], :], oh[0:N[before], j % 2, before, :],
                                             start=before == 0, stop=False)
                        nc.tensor.matmul(o, upper_bf[0:N[k], :], oh[0:N[k], j % 2, k, :], start=k == 0, stop=True)
                    for k in range(3):
                        last = nc.tensor.matmul(rk_ps[:, 24:32], ones_bf[0:N[k], :], oh[0:N[k], j % 2, k, :],
                                                start=k == 0, stop=k == 2)
                    last.then_inc(s_rk, 1)

                def step(i, j, live):
                    if live(3):
                        transposes(i, j - 3)
                    if live(1):
                        queries_keys(i, j - 1)
                    if live(2):
                        attend(i, j - 2)
                    if live(3):
                        logits(i, j - 3)
                    if live(1):
                        values(i, j - 1)
                        scores(i, j - 1)
                    if live(3):
                        ranks(i, j - 3)

                steps(pe, step)


def plan(nc, kept, table, w2, a):
    with ExitStack() as ctx:
        def sb(name, shape, dt=F32):
            return ctx.enter_context(nc.sbuf_tensor("plan_" + name, shape, dt))

        def sem(name):
            return nc.alloc_semaphore("plan_" + name)

        run_i = sb("run_i", [1, EXPERTS], I32)
        n_i = sb("slots_i", [1, 2, EXPERTS], I32)
        f = sb("expert_rows", [1, 8, EXPERTS])
        le = sb("expert_order", [1, EXPERTS, EXPERTS])
        nle = sb("slots_before", [1, EXPERTS, EXPERTS])
        ge = sb("slot_past_expert", [1, SLOTS, EXPERTS])
        gd = sb("slot_jumps", [1, SLOTS, EXPERTS])
        sl = sb("slot_rows", [1, 6, SLOTS])
        pad = sb("padding", [128, 2, PAY])
        s_pad, s_w2, s_p, s_fill = sem("padding_set"), sem("w2_loaded"), sem("plan_step"), sem("padding_stored")

        with nc.Block() as block:
            @block.sync
            def _(sp):
                sp.dma_start(w2[:, :], a["w2"]).then_inc(s_w2, 16)
                sp.wait_ge(s_pad, 2)
                rows = kept.by_expert
                sp.dma_start(rows[DUMMY:DUMMY + SLOT, :].rearrange("(p k) c -> p k c", k=2), pad[:, :, :])\
                    .then_inc(s_fill, 16)
                sp.wait_ge(s_p, 1)
                for x in range(EXPERTS):
                    at = sp.value_load(run_i[0:1, x:x + 1], min_val=0, max_val=DUMMY - SLOT)
                    sp.dma_start(rows[bass.ds(at, SLOT), :].rearrange("(p k) c -> p k c", k=2), pad[:, :, :])\
                        .then_inc(s_fill, 16)
                sp.wait_ge(s_fill, 16 * (EXPERTS + 1))
                sp.wait_ge(s_w2, 16)

            @block.vector
            def _(dve):
                nc.vector.memset(pad[:, :, 0:D + 3], 0.0).then_inc(s_pad, 1)
                nc.vector.memset(pad[:, :, D + 3:PAY].bitcast(I32), NOBODY).then_inc(s_pad, 1)
                count = 0

                def link(ins):
                    nonlocal count
                    count += 1
                    ins.then_inc(s_p, 1)
                    dve.wait_ge(s_p, count)

                run = kept.run[PAIRS % 2][0:1, :]
                c = kept.const
                link(nc.vector.tensor_copy(run_i[:, :], run))
                link(nc.vector.tensor_tensor(f[:, 0, :], run, c[0:1, C_RUN0:C_RUN0 + EXPERTS], ALU.subtract))
                link(nc.vector.tensor_scalar(f[:, 1, :], f[:, 0, :], float(SLOT - 1), None, ALU.add))
                link(nc.vector.tensor_copy(n_i[:, 0, :], f[:, 1, :]))
                link(nc.vector.tensor_scalar(n_i[:, 1, :], n_i[:, 0, :], int(np.log2(SLOT)), None,
                                             ALU.arith_shift_right))
                link(nc.vector.tensor_copy(f[:, 2, :], n_i[:, 1, :]))
                desc = c[0:1, C_DESC:C_DESC + EXPERTS]
                sq = [1, EXPERTS, EXPERTS]
                link(nc.vector.tensor_tensor(le[:, :, :], desc.unsqueeze(1).broadcast_to(sq),
                                             desc.unsqueeze(2).broadcast_to(sq), ALU.is_ge))
                link(nc.vector.tensor_tensor(nle[:, :, :], le[:, :, :], f[:, 2, :].unsqueeze(1).broadcast_to(sq),
                                             ALU.mult))
                link(nc.vector.tensor_reduce(f[:, 3, :], nle[:, :, :], AX.X, ALU.add))
                link(nc.vector.tensor_scalar(f[:, 4, :], f[:, 2, :], -float(SLOT), float(REGION), ALU.mult, ALU.add))
                se = [1, SLOTS, EXPERTS]
                s = c[0:1, C_SLOT:C_SLOT + SLOTS]
                link(nc.vector.tensor_tensor(ge[:, :, :], f[:, 3, :].unsqueeze(1).broadcast_to(se),
                                             s.unsqueeze(2).broadcast_to(se), ALU.is_le))
                link(nc.vector.tensor_reduce(sl[:, 0, :], ge[:, :, :], AX.X, ALU.add))
                link(nc.vector.tensor_scalar(sl[:, 1, :], sl[:, 0, :], float(EXPERTS - 1), None, ALU.min))
                link(nc.vector.tensor_copy(table[:, 0, :], sl[:, 1, :]))
                link(nc.vector.tensor_tensor(gd[:, :, :], ge[:, :, :], f[:, 4, :].unsqueeze(1).broadcast_to(se),
                                             ALU.mult))
                link(nc.vector.tensor_reduce(sl[:, 2, :], gd[:, :, :], AX.X, ALU.add))
                link(nc.vector.scalar_tensor_tensor(out=sl[:, 3, :], in0=s, scalar=float(SLOT), in1=sl[:, 2, :],
                                                    op0=ALU.mult, op1=ALU.add))
                link(nc.vector.tensor_scalar(sl[:, 4, :], sl[:, 3, :], float(DUMMY), None, ALU.min))
                link(nc.vector.tensor_copy(table[:, 1, :], sl[:, 4, :]))


def experts(nc, kept, table, w2, out):
    with ExitStack() as ctx:
        def sb(name, shape, dt=F32):
            return ctx.enter_context(nc.sbuf_tensor("ffn_" + name, shape, dt))

        def sem(name):
            return nc.alloc_semaphore("ffn_" + name)

        pay = sb("rows", [128, 4, 2, PAY])
        xn = sb("x_n", [128, 2, 2, D])
        xh = sb("x_hi", [128, 2, SLOT], F16)
        xl = sb("x_lo", [128, 2, SLOT], F16)
        g = sb("gelu", [128, 2, FC, SLOT])
        y = sb("ffn", [128, 2, 2, D])
        o = sb("out_rows", [128, 2, 2, D])
        up_ps = [kept.banks[0:2], kept.banks[2:4]]
        down_ps, t_ps = kept.banks[4:6], kept.banks[6:8]

        s_in = [sem(f"rows_loaded{i}") for i in range(4)]
        s_xn, s_t, s_hi, s_lo = sem("x_n"), sem("x_t_ps"), sem("x_hi"), sem("x_lo")
        s_up, s_g, s_down, s_y, s_o = sem("up_ps"), sem("gelu"), sem("down_ps"), sem("y"), sem("out_rows")
        s_st = [sem(f"stored{i}") for i in range(2)]

        PEEL = 5
        LOOPS = (SLOTS - PEEL) // SLOT_UNROLL

        def steps(eng, step):
            for n in range(PEEL):
                step(0, n, lambda lag, n=n: n >= lag)
            with eng.Fori(0, LOOPS) as i:
                for j in range(PEEL, PEEL + SLOT_UNROLL):
                    step(i, j, lambda lag: True)
            for n in range(PEEL + SLOT_UNROLL * LOOPS, SLOTS + 3):
                step(LOOPS, n - SLOT_UNROLL * LOOPS, lambda lag, n=n: n - lag < SLOTS)

        def expert(eng, s):
            return eng.value_load(table[0:1, 0, bass.ds(s, 1)], min_val=0, max_val=EXPERTS - 1)

        with nc.Block() as block:
            @block.sync
            def _(sp):
                def load(i, j):
                    s = SLOT_UNROLL * i + j
                    at = sp.value_load(table[0:1, 1, bass.ds(s, 1)], min_val=0, max_val=DUMMY)
                    if j >= 4:
                        sp.wait_ge(s_st[j % 2], 32 * (2 * i + (j - 4) // 2 + 1))
                    sp.dma_start(pay[:, j % 4, :, :], kept.by_expert[bass.ds(at, SLOT), :]
                                 .rearrange("(k p) c -> p k c", k=2)).then_inc(s_in[j % 4], 16)

                for j in range(SLOT_UNROLL):
                    load(0, j)
                with sp.Fori(0, SLOTS // SLOT_UNROLL - 1) as i:
                    for j in range(SLOT_UNROLL, 2 * SLOT_UNROLL):
                        load(i, j)

            @block.gpsimd
            def _(pool):
                last_row = pool.to_reg(ALL - 1)

                def store(i, j):
                    s = SLOT_UNROLL * i + j
                    own_wait(pool, s_o, s + 1, s_xn)
                    for k in range(2):
                        nc.gpsimd.indirect_dma_start(
                            out=out[:, :], out_offset=bass.IndirectOffsetOnAxis(
                                ap=pay[:, j % 4, k, D + 3:D + 4].bitcast(I32), axis=0),
                            in_=o[:, j % 2, k, :], in_offset=None,
                            bounds_check=last_row, oob_is_err=False).then_inc(s_st[j % 2], 16)

                steps(pool, lambda i, j, live: live(3) and store(i, j - 3))
                pool.wait_ge(s_st[0], 32 * ((SLOTS + 1) // 2))
                pool.wait_ge(s_st[1], 32 * (SLOTS // 2))

            @block.scalar
            def _(act):
                nc.scalar.preload_act_table(ACT.Gelu)

                def high(i, j):
                    s = SLOT_UNROLL * i + j
                    act.wait_ge(s_t, s + 1)
                    if j >= 2:
                        act.wait_ge(s_up, s - 1)
                    nc.scalar.activation(xh[:, j % 2, :], t_ps[j % 2][:, 0:SLOT], ACT.Copy).then_inc(s_hi, 1)

                def gelu(i, j):
                    s = SLOT_UNROLL * i + j
                    x = expert(act, s)
                    act.wait_ge(s_up, s + 1)
                    if j >= 2:
                        act.wait_ge(s_down, s - 1)
                    for c in range(FC):
                        last = nc.scalar.activation(g[:, j % 2, c, :],
                                                    up_ps[j % 2][c // 2][:, c % 2 * SLOT:(c % 2 + 1) * SLOT],
                                                    ACT.Gelu, bias=kept.b1[:, bass.ds(x * FC + c, 1)],
                                                    scale=1.0 / W_SCALE)
                    last.then_inc(s_g, 1)

                def step(i, j, live):
                    if live(1):
                        high(i, j - 1)
                    if live(2):
                        gelu(i, j - 2)

                steps(act, step)

            @block.vector
            def _(dve):
                def normalise(i, j):
                    s = SLOT_UNROLL * i + j
                    dve.wait_ge(s_in[j % 4], 16 * (i + j // 4 + 1))
                    if j >= 2:
                        dve.wait_ge(s_t, s - 1)
                    p = pay[:, j % 4, :, :]
                    for k in range(2):
                        last = nc.vector.tensor_scalar(xn[:, j % 2, k, :], p[:, k, 0:D], p[:, k, D:D + 1],
                                                       p[:, k, D + 1:D + 2], ALU.subtract, ALU.mult)
                    last.then_inc(s_xn, 1)

                def low(i, j):
                    s = SLOT_UNROLL * i + j
                    dve.wait_ge(s_hi, s + 1)
                    if j >= 2:
                        dve.wait_ge(s_up, s - 1)
                    nc.vector.tensor_tensor(xl[:, j % 2, :], t_ps[j % 2][:, 0:SLOT], xh[:, j % 2, :], ALU.subtract)\
                        .then_inc(s_lo, 1)

                def finish(i, j):
                    s = SLOT_UNROLL * i + j
                    x = expert(dve, s)
                    dve.wait_ge(s_down, s + 1)
                    if j >= 2:
                        dve.wait_ge(s_st[j % 2], 32 * (2 * i + j // 2))
                    p = pay[:, j % 4, :, :]
                    last = nc.vector.tensor_tensor(y[:, j % 2, :, :],
                                                   down_ps[j % 2][:, 0:2 * D].rearrange("p (k e) -> p k e", k=2),
                                                   kept.b2[:, bass.ds(x * D, D)].unsqueeze(1)
                                                   .broadcast_to([128, 2, D]), ALU.add)
                    last.then_inc(s_y, 1)
                    dve.wait_ge(s_y, s + 1)
                    for k in range(2):
                        last = nc.vector.scalar_tensor_tensor(out=o[:, j % 2, k, :], in0=y[:, j % 2, k, :],
                                                              scalar=p[:, k, D + 2:D + 3], in1=p[:, k, 0:D],
                                                              op0=ALU.mult, op1=ALU.add)
                    last.then_inc(s_o, 1)

                def step(i, j, live):
                    if live(0):
                        normalise(i, j)
                    if live(1):
                        low(i, j - 1)
                    if live(3):
                        finish(i, j - 3)

                steps(dve, step)

            @block.tensor
            def _(pe):
                def transposes(i, j):
                    s = SLOT_UNROLL * i + j
                    pe.wait_ge(s_xn, s + 1)
                    if j >= 2:
                        pe.wait_ge(s_lo, s - 1)
                    for k in range(2):
                        last = nc.tensor.transpose(t_ps[j % 2][:, k * D:(k + 1) * D], xn[:, j % 2, k, :],
                                                   kept.col(C_ID, 128))
                    last.then_inc(s_t, 1)

                def up(i, j):
                    s = SLOT_UNROLL * i + j
                    x = expert(pe, s)
                    pe.wait_ge(s_lo, s + 1)
                    if j >= 2:
                        pe.wait_ge(s_g, s - 1)
                    for c in range(FC):
                        u = up_ps[j % 2][c // 2][:, c % 2 * SLOT:(c % 2 + 1) * SLOT]
                        hi, lo = (t[:, bass.ds(x * F + c * 128, 128)] for t in (kept.w1_hi, kept.w1_lo))
                        nc.tensor.matmul(u, hi, xh[:, j % 2, :], start=True, stop=False)
                        nc.tensor.matmul(u, hi, xl[:, j % 2, :], start=False, stop=False)
                        last = nc.tensor.matmul(u, lo, xh[:, j % 2, :], start=False, stop=True)
                    last.then_inc(s_up, 1)

                def down(i, j):
                    s = SLOT_UNROLL * i + j
                    x = expert(pe, s)
                    pe.wait_ge(s_g, s + 1)
                    if j >= 2:
                        pe.wait_ge(s_o, s - 1)
                    for k in range(2):
                        for c in range(FC):
                            last = nc.tensor.matmul(down_ps[j % 2][:, k * D:(k + 1) * D],
                                                    g[:, j % 2, c, k * 128:(k + 1) * 128],
                                                    w2[:, bass.ds(x * F + c * D, D)], start=c == 0, stop=c == FC - 1)
                    last.then_inc(s_down, 1)

                def step(i, j, live):
                    if live(1):
                        transposes(i, j - 1)
                    if live(2):
                        up(i, j - 2)
                    if live(3):
                        down(i, j - 3)

                steps(pe, step)


def build(nc, out, **a):
    kept = Kept(nc)
    with nc.sbuf_tensor("hnT", [128, ALL], F32) as hnT:
        with ExitStack() as ctx:
            def sb(name, shape, dt=F32):
                return ctx.enter_context(nc.sbuf_tensor(name, shape, dt))
            tok = {"w": sb("w_tok_sb", [128, VARIANTS, D]), "gamma": sb("gamma_sb", [128, TOKENS, VARIANTS]),
                   "rstd": sb("rstd_image", [128, 1]), "stT": sb("image_parts_T", [PARTS, IMAGES], BF16)}
            image_statistics(nc, kept, hnT, tok, a)
            tokenizer(nc, kept, hnT, tok, a)
        attention(nc, kept, hnT, a)
    with nc.sbuf_tensor("slot_table", [1, 2, SLOTS], I32) as table, \
            nc.sbuf_tensor("w2_sb", [128, EXPERTS * F], F32) as w2:
        plan(nc, kept, table, w2, a)
        experts(nc, kept, table, w2, out)


def kernel(x, L0_tok_gamma, L0_tok_beta, L0_tok_W, L0_tok_b, L0_attn_Wq, L0_attn_Wv, L0_attn_Wk,
           L0_ffn_Ws, L0_ffn_bs, L0_ffn_W1, L0_ffn_b1, L0_ffn_W2, L0_ffn_b2):
    import concourse.bacc as bacc
    from concourse.bass_utils import run_bass_kernel_spmd

    def patches(p, g):
        b = p.shape[0]
        return np.asarray(p).reshape(b, 2, g, 2, 4, g, 2, 4).transpose(3, 6, 1, 4, 7, 2, 5, 0).reshape(128, g, g, b)

    def positions(p):
        return np.asarray(p).reshape(VARIANTS, 2, GRID, 2, 4, GRID, 2, 4).transpose(3, 6, 1, 4, 7, 2, 5, 0)\
            .reshape(128, TOKENS, VARIANTS)

    x = np.asarray(x)
    arrays = {
        "x_al": patches(x, GRID),
        "x_off": patches(np.pad(x, ((0, 0), (0, 0), (4, 4), (4, 4))), GRID + 1),
        "gamma": positions(L0_tok_gamma),
        "beta": positions(L0_tok_beta),
        "w_tok": np.asarray(L0_tok_W).reshape(D, VARIANTS, 2, 2, 4, 2, 4).transpose(3, 5, 2, 4, 6, 1, 0)
        .reshape(128, VARIANTS, D),
        "b_tok": np.asarray(L0_tok_b).reshape(1, D),
        "w_q": np.asarray(L0_attn_Wq), "w_k": np.asarray(L0_attn_Wv), "w_v": np.asarray(L0_attn_Wk),
        "w_s": np.asarray(L0_ffn_Ws),
        "b_s": np.asarray(L0_ffn_bs).reshape(1, EXPERTS),
        "w1": np.asarray(L0_ffn_W1).transpose(1, 0, 2).reshape(D, EXPERTS * F),
        "b1": np.asarray(L0_ffn_b1).reshape(EXPERTS, FC, 128).transpose(2, 0, 1).reshape(128, EXPERTS * FC),
        "w2": np.asarray(L0_ffn_W2).reshape(EXPERTS, FC, 128, D).transpose(2, 0, 1, 3).reshape(128, EXPERTS * F),
        "b2": np.asarray(L0_ffn_b2).reshape(1, EXPERTS * D),
        "const": constants(),
    }
    arrays = {n: np.ascontiguousarray(v) for n, v in arrays.items()}
    nc = bacc.Bacc("TRN2", target_bir_lowering=False, num_devices=1)
    aps = {n: nc.dram_tensor(n, v.shape, F32, kind="ExternalInput").ap() for n, v in arrays.items()}
    out = nc.dram_tensor("out", (ALL, D), F32, kind="ExternalOutput").ap()
    build(nc, out, **aps)
    r = run_bass_kernel_spmd(nc, [arrays], core_ids=[0])
    return r.results[0]["out"].reshape(IMAGES, TOKENS, D)
```

```python
from contextlib import ExitStack

import numpy as np
import concourse.bass as bass
from concourse import mybir

F32 = mybir.dt.float32
BF16 = mybir.dt.bfloat16
F16 = mybir.dt.float16
I32 = mybir.dt.int32
ALU = mybir.AluOpType
ACT = mybir.ActivationFunctionType
AX = mybir.AxisListType

IMAGES = 128
D = 128
GRID = 13
TOKENS = GRID * GRID
ALL = IMAGES * TOKENS
VARIANTS = 5
PIXELS = 10 * 104 * 104
TOK_EPS = 1e-7
LN_EPS = 1e-5
GROUP_AT = [0, 4, 7, 10]
GROUP_N = [4, 3, 3, 3]
GROUPS = len(GROUP_AT)
ROW_UNROLL = 4
PARTS = 12
CHUNKS = [(0, 4), (4, 7), (7, 10), (10, 13)]
RUNS = [(0, 0, 1), (0, 1, 4), (1, 4, 7), (2, 7, 10), (3, 10, 12), (3, 12, 13)]

PAIRS = IMAGES // 2
HEAD = 105
TAIL = TOKENS - HEAD
PAIR = 2 * TOKENS
EXPERTS = 8
F = 512
FC = F // 128
SLOT = 256
REGION = ALL + SLOT
DUMMY = EXPERTS * REGION
SLOTS = (ALL + EXPERTS * (SLOT - 1)) // SLOT
PAY = D + 4
NOBODY = 1 << 20
SLOT_UNROLL = 8
OUT_RING = 4
W_SCALE = 64.0
MASKED = -30000.0
SCORE_SCALE = 0.25 / float(np.sqrt(np.float32(D)))

C_ID, C_UP, C_TRI, C_TRIT, C_MULT = 0, 128, 256, 384, 448
C_DESC, C_RUN0, C_ID0, C_SLOT, C_END = 457, 465, 473, 476, 476 + 92


def constants():
    c = np.zeros((128, C_END), np.float32)
    k = np.arange(128)
    c[:, C_ID:C_ID + 128] = np.eye(128)
    c[:, C_UP:C_UP + 128] = k[:, None] < k[None, :]
    c[:, C_TRI:C_TRI + 128] = np.where(k[:, None] < k[None, :], 0.0, MASKED)
    c[:, C_TRIT:C_TRIT + 64] = np.where(k[:, None] % 64 < k[None, :64], 0.0, MASKED)
    r, s = k // 64, k // 32 % 2
    for a in range(3):
        for b in range(3):
            over = 2 - ((a == 0) & (r == 0)) - ((a == 2) & (r == 1))
            across = 2 - ((b == 0) & (s == 0)) - ((b == 2) & (s == 1))
            c[:, C_MULT + 3 * a + b] = 1 + over * across
    e = np.arange(EXPERTS)
    c[:, C_DESC:C_DESC + EXPERTS] = EXPERTS - e
    c[:, C_RUN0:C_RUN0 + EXPERTS] = e * REGION
    c[:, C_ID0] = k
    c[:, C_ID0 + 1] = TOKENS + k
    c[:, C_ID0 + 2] = np.where(k < TAIL, HEAD + k, TOKENS + HEAD + k - TAIL)
    c[:, C_SLOT:C_END] = np.arange(SLOTS)
    return c


def own_wait(eng, sem, value, passed):
    if not isinstance(value, int):
        value = eng.to_reg(value)
    eng.wait_ge(passed, 1)
    eng.wait_ge(sem, value)


class Kept:

    def __init__(self, nc):
        def sb(name, shape, dt=F32):
            return nc.alloc_sbuf_tensor(name, shape, dt)

        def dram(name, shape, dt=F32):
            return nc.dram_tensor(name, shape, dt, kind="Internal").ap()

        self.banks = [nc.alloc_psum_tensor(f"bank{i}", [128, 512], F32) for i in range(8)]
        self.const = sb("constants", [128, C_END])
        self.ident_bf = sb("ident_bf", [128, 128], BF16)
        self.w_qkv = sb("w_qkv", [128, 3, D])
        self.w_s = sb("w_s_sb", [128, EXPERTS])
        self.b_s = sb("b_s_sb", [128, EXPERTS])
        self.b1 = sb("b1_sb", [128, EXPERTS * FC])
        self.b2 = sb("b2_sb", [128, EXPERTS * D])
        self.w1_hi = sb("w1_hi", [128, EXPERTS * F], F16)
        self.w1_lo = sb("w1_lo", [128, EXPERTS * F], F16)
        self.run = [sb(f"run{i}", [128, EXPERTS]) for i in range(2)]
        self.h = dram("h_rows", (IMAGES, TOKENS * D))
        self.gb = dram("gamma_beta_parts", (PARTS, TOKENS * D), BF16)
        self.by_expert = dram("rows_by_expert", (DUMMY + SLOT, PAY))

    def col(self, at, n=1):
        return self.const[:, at:at + n]


def image_statistics(nc, kept, hnT, tok, a):
    with ExitStack() as ctx:
        def sb(name, shape, dt=F32):
            return ctx.enter_context(nc.sbuf_tensor("stats_" + name, shape, dt))

        def sem(name):
            return nc.alloc_semaphore("stats_" + name)

        ROW = GRID * IMAGES
        x_dram = a["x_al"].rearrange("p r c b -> p (r c b)")
        x = hnT[:, :].rearrange("p (r c b) -> p r c b", r=GRID, c=GRID)
        sq = sb("squares", [128, 2, 4 * ROW])
        red = sb("reduced_rows", [128, 2 * len(RUNS), IMAGES])
        beta = sb("beta_sb", [128, TOKENS, VARIANTS])
        b_tok = sb("b_tok_sb", [128, D])
        w1 = sb("w1_f32", [128, EXPERTS * F])
        rest = sb("parts_rest", [128, 2, 2, D])
        rest2 = sb("parts_rest2", [128, 2, 2, D])
        rest3 = sb("parts_rest3", [128, 2, 2, D])
        part = sb("parts", [128, 2, 2, 3, D], BF16)
        s12 = sb("image_sums", [128, 8])
        mhalf = sb("minus_half", [128, 1])
        sv = sb("minus_mean_and_deviation", [128, 2])
        svr = sb("image_parts_rest", [128, 2, 2])
        sp = sb("image_parts", [128, 2, 3], BF16)
        stp = sb("image_part_columns", [128, 2, 6])
        gb_ps, sum_ps, ssq_ps, st_ps = kept.banks[0], kept.banks[1], kept.banks[2], kept.banks[3]

        s_cst, s_wt, s_w, s_w1 = sem("c_loaded"), sem("tok_w_loaded"), sem("w_loaded"), sem("w1_loaded")
        s_x = [sem(f"x_chunk_loaded{i}") for i in range(4)]
        s_idb, s_sq, s_xred, s_sqred = sem("ident_cast"), sem("squared"), sem("x_reduced"), sem("sq_reduced")
        s_sums, s_gbp, s_ch, s_gbw = sem("sums_done"), sem("gb_products"), sem("split_step"), sem("gb_stored")
        s_pool, s_pow, s_stp, s_stT = sem("pool_step"), sem("rstd_img"), sem("stp_ready"), sem("stp_transposed")
        s_done, s_hi = sem("stT_ready"), sem("w1_hi_ready")
        s_ssq = sem("sq_products_done")
        T_AT, T_N = [0, 128], [128, TOKENS - 128]

        def squares(c):
            lo, hi = CHUNKS[c]
            return sq[:, c % 2, 0:(hi - lo) * ROW].rearrange("p (r c b) -> p r c b", c=GRID, b=IMAGES)

        with nc.Block() as block:
            @block.sync
            def _(sp_):
                sp_.dma_start(tok["w"][:, :, :], a["w_tok"]).then_inc(s_wt, 16)
                sp_.dma_start(tok["gamma"][:, :, :], a["gamma"]).then_inc(s_wt, 16)
                sp_.dma_start(beta[:, :, :], a["beta"]).then_inc(s_wt, 16)
                sp_.dma_start(kept.const[:, :], a["const"]).then_inc(s_cst, 16)
                for c, (lo, hi) in enumerate(CHUNKS):
                    sp_.dma_start(hnT[:, lo * ROW:hi * ROW], x_dram[:, lo * ROW:hi * ROW]).then_inc(s_x[c], 16)
                sp_.dma_start(w1[:, :], a["w1"]).then_inc(s_w1, 16)
                sp_.dma_start(b_tok[:, :], a["b_tok"].broadcast_to([128, D])).then_inc(s_w, 16)
                for i, n in enumerate(("w_q", "w_k", "w_v")):
                    sp_.dma_start(kept.w_qkv[:, i, :], a[n]).then_inc(s_w, 16)
                sp_.dma_start(kept.w_s[:, :], a["w_s"]).then_inc(s_w, 16)
                sp_.dma_start(kept.b_s[:, :], a["b_s"].broadcast_to([128, EXPERTS])).then_inc(s_w, 16)
                sp_.dma_start(kept.b1[:, :], a["b1"]).then_inc(s_w, 16)
                sp_.dma_start(kept.b2[:, :], a["b2"].broadcast_to([128, EXPERTS * D])).then_inc(s_w, 16)
                gb = kept.gb.rearrange("(q r) (t e) -> t q r e", q=2, e=D)
                for j in range(2):
                    sp_.wait_ge(s_ch, 6 * (j + 1))
                    for q in range(2):
                        for at, n in ((0, 3), (3, 2), (5, 1)):
                            sp_.dma_start(gb[T_AT[j]:T_AT[j] + T_N[j], q, at:at + n, :],
                                          part[0:T_N[j], j, q, 0:n, :]).then_inc(s_gbw, 16)
                sp_.wait_ge(s_gbw, 16 * 12)
                sp_.wait_ge(s_w, 16 * 8)

            @block.gpsimd
            def _(pool):
                nc.gpsimd.memset(mhalf[:, :], -0.5).then_inc(s_pool, 1)
                pool.wait_ge(s_hi, 1)
                nc.gpsimd.tensor_scalar(w1[:, :], w1[:, :], W_SCALE, None, ALU.mult).then_inc(s_pool, 1)
                pool.wait_ge(s_pool, 2)
                nc.gpsimd.tensor_tensor(kept.w1_lo[:, :], w1[:, :], kept.w1_hi[:, :], ALU.subtract)\
                    .then_inc(s_pool, 1)
                pool.wait_ge(s_stp, 4)
                nc.gpsimd.tensor_tensor(tok["rstd"][:, :], s12[:, 5:6], mhalf[:, :], ALU.pow).then_inc(s_pow, 1)

            @block.scalar
            def _(act):
                for c, (lo, hi) in enumerate(CHUNKS):
                    act.wait_ge(s_x[c], 16)
                    if c >= 2:
                        act.wait_ge(s_sqred, {2: 2, 3: 3}[c])
                        act.wait_ge(s_ssq, {2: 2, 3: 3}[c])
                    nc.scalar.activation(squares(c), x[:, lo:hi, :, :], ACT.Square).then_inc(s_sq, 1)
                act.wait_ge(s_w1, 16)
                nc.scalar.activation(kept.w1_hi[:, :], w1[:, :], ACT.Copy, scale=W_SCALE).then_inc(s_hi, 1)

            @block.vector
            def _(dve):
                dve.wait_ge(s_cst, 16)
                nc.vector.tensor_copy(kept.ident_bf[:, :], kept.col(C_ID, 128)).then_inc(s_idb, 1)
                for n, (c, first, end) in enumerate(RUNS):
                    dve.wait_ge(s_x[c], 16)
                    nc.vector.tensor_reduce(red[:, n, :], x[:, first:end, 1:GRID - 1, :]
                                            .rearrange("p r c b -> p b r c"), AX.XY, ALU.add).then_inc(s_xred, 1)
                for n, (c, first, end) in enumerate(RUNS):
                    dve.wait_ge(s_sq, c + 1)
                    at = CHUNKS[c][0]
                    nc.vector.tensor_reduce(red[:, len(RUNS) + n, :],
                                            squares(c)[:, first - at:end - at, 1:GRID - 1, :]
                                            .rearrange("p r c b -> p b r c"), AX.XY, ALU.add).then_inc(s_sqred, 1)
                dve.wait_ge(s_gbp, 1)
                dve.wait_ge(s_w, 16 * 8)
                steps = 0

                def link(ins):
                    nonlocal steps
                    steps += 1
                    ins.then_inc(s_ch, 1)
                    dve.wait_ge(s_ch, steps)

                for j in range(2):
                    n = T_N[j]
                    ps = gb_ps[0:n, 256 * j:256 * j + 256].rearrange("p (q e) -> p q e", q=2)
                    r = [t[0:n, j, :, :] for t in (rest, rest2, rest3)]
                    nc.vector.tensor_copy(r[0][:, 0, :], ps[:, 0, :])
                    link(nc.vector.tensor_tensor(r[0][:, 1, :], ps[:, 1, :], b_tok[0:n, :], ALU.add))
                    link(nc.vector.tensor_copy(part[0:n, j, :, 0, :], r[0]))
                    link(nc.vector.tensor_tensor(r[1], r[0], part[0:n, j, :, 0, :], ALU.subtract))
                    link(nc.vector.tensor_copy(part[0:n, j, :, 1, :], r[1]))
                    link(nc.vector.tensor_tensor(r[2], r[1], part[0:n, j, :, 1, :], ALU.subtract))
                    link(nc.vector.tensor_copy(part[0:n, j, :, 2, :], r[2]))
                dve.wait_ge(s_sums, 2)
                stp_steps = 0

                def then(ins):
                    nonlocal stp_steps
                    stp_steps += 1
                    ins.then_inc(s_stp, 1)
                    dve.wait_ge(s_stp, stp_steps)

                then(nc.vector.tensor_scalar(s12[:, 0:1], sum_ps[:, 0:1], 1.0 / PIXELS, None, ALU.mult))
                nc.vector.tensor_scalar(s12[:, 2:3], ssq_ps[:, 0:1], 1.0 / PIXELS, TOK_EPS, ALU.mult, ALU.add)
                then(nc.vector.tensor_tensor(s12[:, 3:4], s12[:, 0:1], s12[:, 0:1], ALU.mult))
                then(nc.vector.tensor_tensor(s12[:, 4:5], s12[:, 2:3], s12[:, 3:4], ALU.subtract))
                then(nc.vector.tensor_scalar(s12[:, 5:6], s12[:, 4:5], TOK_EPS, None, ALU.max))
                dve.wait_ge(s_pow, 1)
                nc.vector.tensor_scalar(sv[:, 0:1], s12[:, 0:1], -1.0, None, ALU.mult)
                then(nc.vector.tensor_tensor(sv[:, 1:2], s12[:, 5:6], tok["rstd"][:, :], ALU.mult))
                then(nc.vector.tensor_copy(sp[:, :, 0], sv[:, :]))
                then(nc.vector.tensor_tensor(svr[:, 0, :], sv[:, :], sp[:, :, 0], ALU.subtract))
                then(nc.vector.tensor_copy(sp[:, :, 1], svr[:, 0, :]))
                then(nc.vector.tensor_tensor(svr[:, 1, :], svr[:, 0, :], sp[:, :, 1], ALU.subtract))
                then(nc.vector.tensor_copy(sp[:, :, 2], svr[:, 1, :]))
                for q in range(2):
                    for at, n, p in ((0, 3, 0), (3, 2, 1), (5, 1, 2)):
                        last = nc.vector.tensor_copy(stp[:, q, at:at + n], sp[:, q, p:p + 1].broadcast_to([128, n]))
                then(last)
                dve.wait_ge(s_stT, 1)
                nc.vector.tensor_copy(tok["stT"][:, :], st_ps[0:PARTS, 0:IMAGES]).then_inc(s_done, 1)

            @block.tensor
            def _(pe):
                pe.wait_ge(s_wt, 48)
                for j in range(2):
                    for q, g in enumerate((tok["gamma"], beta)):
                        for v in range(VARIANTS):
                            last = nc.tensor.matmul(gb_ps[0:T_N[j], 256 * j + 128 * q:256 * j + 128 * q + D],
                                                    g[:, T_AT[j]:T_AT[j] + T_N[j], v], tok["w"][:, v, :],
                                                    start=v == 0, stop=v == VARIANTS - 1)
                last.then_inc(s_gbp, 1)
                pe.wait_ge(s_cst, 16)

                def edge(r):
                    return 0 if r == 0 else 2 if r == GRID - 1 else 1

                def sums(ps, source, ready, reduced, base, chunk_done):
                    for c, (lo, hi) in enumerate(CHUNKS):
                        ready(c)
                        for r in range(lo, hi):
                            for col, k in ((0, 0), (GRID - 1, 2)):
                                m = C_MULT + 3 * edge(r) + k
                                last = nc.tensor.matmul(ps[:, 0:1], source(c, r - lo, col), kept.col(m),
                                                        start=r == 0 and col == 0, stop=False)
                        if chunk_done is not None:
                            last.then_inc(chunk_done, 1)
                    for n, (c, first, end) in enumerate(RUNS):
                        pe.wait_ge(reduced, n + 1)
                        last = nc.tensor.matmul(ps[:, 0:1], red[:, base + n, :], kept.col(C_MULT + 3 * edge(first) + 1),
                                                start=False, stop=n == len(RUNS) - 1)
                    last.then_inc(s_sums, 1)

                sums(sum_ps, lambda c, r, col: x[:, CHUNKS[c][0] + r, col, :], lambda c: pe.wait_ge(s_x[c], 16),
                     s_xred, 0, None)
                sums(ssq_ps, lambda c, r, col: squares(c)[:, r, col, :], lambda c: pe.wait_ge(s_sq, c + 1),
                     s_sqred, len(RUNS), s_ssq)
                pe.wait_ge(s_stp, 11)
                nc.tensor.transpose(st_ps[0:PARTS, 0:IMAGES], stp[:, :, :].rearrange("p q r -> p (q r)"),
                                    kept.col(C_ID, 128)).then_inc(s_stT, 1)


def tokenizer(nc, kept, hnT, tok, a):
    with ExitStack() as ctx:
        def sb(name, shape, dt=F32):
            return ctx.enter_context(nc.sbuf_tensor("tok_" + name, shape, dt))

        def sem(name):
            return nc.alloc_semaphore("tok_" + name)

        xa = sb("x_aligned", [128, 2, GRID * IMAGES])
        xo = sb("x_offset", [128, 4, (GRID + 1) * IMAGES])
        gbr = sb("parts_row", [PARTS, 2, GRID * D], BF16)
        wg = sb("scaled_weights", [128, 4, VARIANTS, D])
        hrow = sb("h_row", [128, 2, GRID, D])
        hn = sb("h_normalised", [128, 2, 4, D])
        bn6 = sb("bn_stats", [128, 2, GRID, 6])
        mv = sb("mean_var", [128, 2, GRID, 2])
        ve = sb("var_eps", [128, 4])
        rs = sb("rstd", [128, 2, GRID])
        mhalf = sb("minus_half", [128, 4])
        eps = sb("eps", [128, 4])
        acc, tp = kept.banks[0:4], kept.banks[4:6]

        s_xa = [sem(f"x_aligned_loaded{i}") for i in range(2)]
        s_xo = [sem(f"x_offset_loaded{i}") for i in range(4)]
        s_gb = [sem(f"parts_row_loaded{i}") for i in range(2)]
        s_wgd, s_wga, s_tok = sem("weights_scaled_dve"), sem("weights_scaled_act"), sem("token_products")
        s_h, s_hst = sem("h_ready"), [sem(f"h_stored{i}") for i in range(2)]
        s_bn, s_mv, s_ve, s_rs = sem("bn_stats_done"), sem("mean_var_ready"), sem("var_eps_ready"), sem("rstd_ready")
        s_hn, s_tp, s_hnT, s_mh = sem("hn_ready"), sem("hn_transposed"), sem("hnT_written"), sem("mhalf_set")

        xa_d = a["x_al"].rearrange("p r c b -> p (r c b)")
        xo_d = a["x_off"].rearrange("p r c b -> p (r c b)")
        hnT_t = hnT[:, :].rearrange("p (b t) -> p t b", t=TOKENS)
        XA, XO, RD = GRID * IMAGES, (GRID + 1) * IMAGES, GRID * D

        def rows(eng, row):
            row(0, 0)
            with eng.Fori(0, (GRID - 1) // ROW_UNROLL) as i:
                for j in range(1, ROW_UNROLL + 1):
                    row(i, j)

        def lagged(i, j, g, lag):
            n = GROUPS * j + g - lag
            return None if n < 0 else (i, n // GROUPS, n % GROUPS)

        def drained(step, lag):
            i, j = (GRID - 1) // ROW_UNROLL - 1, ROW_UNROLL
            for n in range(lag):
                step(*lagged(i, j + 1, n, lag))

        def weights_free(eng, i, j, pj):
            before = GRID if pj == GRID - 1 else 4 if pj < 3 else 3
            if GRID * j + pj - before >= 0:
                eng.wait_ge(s_tok, GRID * (ROW_UNROLL * i + j) + pj - before + 1)

        def slot(pj):
            return 3 if pj == GRID - 1 else pj % 3

        with nc.Block() as block:
            @block.sync
            def _(sp):
                def load_xa(pi, n):
                    sp.dma_start(xa[:, n % 2, :], xa_d[:, bass.ds(pi * XA, XA)]).then_inc(s_xa[n % 2], 16)
                    sp.dma_start(gbr[:, n % 2, :], kept.gb[:, bass.ds(pi * RD, RD)]).then_inc(s_gb[n % 2], 16)

                def load_xo(pi, n):
                    sp.dma_start(xo[:, n % 4, :], xo_d[:, bass.ds(pi * XO, XO)]).then_inc(s_xo[n % 4], 16)

                def store(pi, j):
                    sp.wait_ge(s_h, GROUPS * (pi + 1))
                    sp.dma_start(kept.h[:, bass.ds(pi * RD, RD)],
                                 hrow[:, j % 2, :, :].rearrange("p t d -> p (t d)")).then_inc(s_hst[j % 2], 16)

                def refill(i, j, last):
                    pi = ROW_UNROLL * i + j
                    sp.wait_ge(s_tok, GRID * pi)
                    if not last or pi + 1 < GRID:
                        load_xa(pi + 1, j + 1)
                    if not last or pi + 3 < GRID + 1:
                        load_xo(pi + 3, j + 3)
                    store(pi - 1, j - 1)

                load_xa(0, 0)
                for n in range(4):
                    load_xo(n, n)
                    if n == 1:
                        load_xa(1, 1)
                with sp.Fori(0, 2) as i:
                    for j in range(1, ROW_UNROLL + 1):
                        refill(i, j, False)
                for j in range(1, ROW_UNROLL + 1):
                    refill(2, j, True)
                store(GRID - 1, 0)
                sp.wait_ge(s_hst[0], 16 * 7)
                sp.wait_ge(s_hst[1], 16 * 6)

            @block.scalar
            def _(act):
                def evacuate(i, j, g):
                    q, t = GROUPS * (ROW_UNROLL * i + j) + g, GRID * (ROW_UNROLL * i + j)
                    n = GROUP_N[g]
                    act.wait_ge(s_tok, t + GROUP_AT[g] + n)
                    nc.scalar.activation(hrow[:, j % 2, GROUP_AT[g]:GROUP_AT[g] + n, :].rearrange("p t d -> p (t d)"),
                                         acc[g][:, 0:n * D], ACT.Copy, scale=tok["rstd"][:, 0:1]).then_inc(s_h, 1)

                def write_hnT(i, j, g):
                    q, t = GROUPS * (ROW_UNROLL * i + j) + g, GRID * (ROW_UNROLL * i + j)
                    n = GROUP_N[g]
                    act.wait_ge(s_tp, q + 1)
                    nc.scalar.activation(hnT_t[:, bass.ds(t + GROUP_AT[g], n), :],
                                         tp[g % 2][:, 0:n * D].rearrange("p (t b) -> p t b", t=n),
                                         ACT.Copy).then_inc(s_hnT, 1)

                def row(i, j):
                    for g in range(GROUPS):
                        for pj in range(GROUP_AT[g], GROUP_AT[g] + GROUP_N[g]):
                            weights_free(act, i, j, pj)
                            t = GRID * (ROW_UNROLL * i + j) + pj
                            for v in (3, 4):
                                last = nc.scalar.activation(wg[:, slot(pj), v, :], tok["w"][:, v, :], ACT.Copy,
                                                            scale=tok["gamma"][:, bass.ds(t, 1), v])
                            last.then_inc(s_wga, 1)
                        if g == GROUPS - 1 and j > 0:
                            pi = ROW_UNROLL * i + j
                            act.wait_ge(s_hst[(j - 1) % 2], 16 * (2 * i + (j - 1) // 2 + 1))
                            act.wait_ge(s_hn, GROUPS * pi)
                        if (at := lagged(i, j, g, 1)) is not None:
                            evacuate(*at)
                        if (at := lagged(i, j, g, 4)) is not None:
                            write_hnT(*at)

                rows(act, row)
                last_i, last_j = (GRID - 1) // ROW_UNROLL - 1, ROW_UNROLL
                evacuate(last_i, last_j, GROUPS - 1)
                drained(write_hnT, 4)

            @block.vector
            def _(dve):
                nc.vector.memset(mhalf[:, :], -0.5).then_inc(s_mh, 1)
                nc.vector.memset(eps[:, :], LN_EPS).then_inc(s_mh, 1)

                def statistics(i, j, g):
                    q, t = GROUPS * (ROW_UNROLL * i + j) + g, GRID * (ROW_UNROLL * i + j)
                    dve.wait_ge(s_h, q + 1)
                    for pj in range(GROUP_AT[g], GROUP_AT[g] + GROUP_N[g]):
                        last = nc.vector.bn_stats(bn6[:, j % 2, pj, :], hrow[:, j % 2, pj, :])
                    last.then_inc(s_bn, 1)

                def aggregate(i, j, g):
                    q = GROUPS * (ROW_UNROLL * i + j) + g
                    own_wait(dve, s_bn, q + 1, s_mh)
                    for pj in range(GROUP_AT[g], GROUP_AT[g] + GROUP_N[g]):
                        last = nc.vector.bn_aggr(mv[:, j % 2, pj, :], bn6[:, j % 2, pj, :])
                    last.then_inc(s_mv, 1)

                def normalise(i, j, g):
                    q = GROUPS * (ROW_UNROLL * i + j) + g
                    dve.wait_ge(s_rs, q + 1)
                    if GROUPS * j + g >= 2:
                        dve.wait_ge(s_tp, q - 1)
                    for n in range(GROUP_N[g]):
                        pj = GROUP_AT[g] + n
                        last = nc.vector.tensor_scalar(hn[:, g % 2, n, :], hrow[:, j % 2, pj, :],
                                                       mv[:, j % 2, pj, 0:1], rs[:, j % 2, pj:pj + 1],
                                                       ALU.subtract, ALU.mult)
                    last.then_inc(s_hn, 1)

                def row(i, j):
                    for g in range(GROUPS):
                        for pj in range(GROUP_AT[g], GROUP_AT[g] + GROUP_N[g]):
                            weights_free(dve, i, j, pj)
                            t = GRID * (ROW_UNROLL * i + j) + pj
                            for v in range(3):
                                last = nc.vector.tensor_scalar(wg[:, slot(pj), v, :], tok["w"][:, v, :],
                                                               tok["gamma"][:, bass.ds(t, 1), v], None, ALU.mult)
                            last.then_inc(s_wgd, 1)
                        if g == GROUPS - 1 and j > 0:
                            dve.wait_ge(s_hn, GROUPS * (ROW_UNROLL * i + j))
                        if (at := lagged(i, j, g, 1)) is not None:
                            statistics(*at)
                        if (at := lagged(i, j, g, 2)) is not None:
                            normalise(*at)
                        if (at := lagged(i, j, g, 1)) is not None:
                            aggregate(*at)

                rows(dve, row)
                last_i, last_j = (GRID - 1) // ROW_UNROLL - 1, ROW_UNROLL
                statistics(last_i, last_j, GROUPS - 1)
                aggregate(last_i, last_j, GROUPS - 1)
                drained(normalise, 2)

            @block.gpsimd
            def _(pool):
                pool.wait_ge(s_mh, 2)

                def row(i, j):
                    for g in range(GROUPS):
                        q = GROUPS * (ROW_UNROLL * i + j) + g
                        pj, n = GROUP_AT[g], GROUP_N[g]
                        pool.wait_ge(s_mv, q + 1)
                        if GROUPS * j + g > 0:
                            pool.wait_ge(s_rs, q)
                        nc.gpsimd.tensor_tensor(ve[:, 0:n], mv[:, j % 2, pj:pj + n, 1], eps[:, 0:n], ALU.add)\
                            .then_inc(s_ve, 1)
                        pool.wait_ge(s_ve, q + 1)
                        nc.gpsimd.tensor_tensor(rs[:, j % 2, pj:pj + n], ve[:, 0:n], mhalf[:, 0:n], ALU.pow)\
                            .then_inc(s_rs, 1)

                rows(pool, row)

            @block.tensor
            def _(pe):
                def transposes(i, j, g):
                    q = GROUPS * (ROW_UNROLL * i + j) + g
                    pe.wait_ge(s_hn, q + 1)
                    if GROUPS * j + g >= 2:
                        pe.wait_ge(s_hnT, q - 1)
                    for n in range(GROUP_N[g]):
                        last = nc.tensor.transpose(tp[g % 2][:, n * D:(n + 1) * D], hn[:, g % 2, n, :],
                                                   kept.col(C_ID, 128))
                    last.then_inc(s_tp, 1)

                def row(i, j):
                    pi = ROW_UNROLL * i + j
                    pe.wait_ge(s_xa[j % 2], 16 * (2 * i + j // 2 + 1))
                    pe.wait_ge(s_gb[j % 2], 16 * (2 * i + j // 2 + 1))
                    pe.wait_ge(s_xo[j % 4], 16 * (i + j // 4 + 1))
                    pe.wait_ge(s_xo[(j + 1) % 4], 16 * (i + (j + 1) // 4 + 1))
                    for g in range(GROUPS):
                        if j > 0:
                            pe.wait_ge(s_h, GROUPS * pi + g - 3)
                        for n in range(GROUP_N[g]):
                            pj = GROUP_AT[g] + n
                            o = acc[g][:, n * D:(n + 1) * D]
                            nc.tensor.matmul(o, tok["stT"][:, :], gbr[:, j % 2, pj * D:(pj + 1) * D],
                                             start=True, stop=False)
                            pe.wait_ge(s_wgd, GRID * pi + pj + 1)
                            for v in range(VARIANTS):
                                if v == 3:
                                    pe.wait_ge(s_wga, GRID * pi + pj + 1)
                                if v == 0:
                                    patch = xa[:, j % 2, pj * IMAGES:(pj + 1) * IMAGES]
                                else:
                                    up, left = v <= 2, v in (1, 3)
                                    r, c = (j + up) % 4, pj + (not left)
                                    patch = xo[:, r, c * IMAGES:(c + 1) * IMAGES]
                                last = nc.tensor.matmul(o, patch, wg[:, slot(pj), v, :], start=False,
                                                        stop=v == VARIANTS - 1)
                            last.then_inc(s_tok, 1)
                        if (at := lagged(i, j, g, 3)) is not None:
                            transposes(*at)

                rows(pe, row)
                drained(transposes, 3)


def attention(nc, kept, hnT, a):
    with ExitStack() as ctx:
        def sb(name, shape, dt=F32):
            return ctx.enter_context(nc.sbuf_tensor("attn_" + name, shape, dt))

        def sem(name):
            return nc.alloc_semaphore("attn_" + name)

        RING = 4
        upper_bf = sb("upper_bf", [128, 128], BF16)
        ones_bf = sb("ones_bf", [128, 128], BF16)
        tri_bf = sb("tri_bf", [128, 128 + 64], BF16)
        x2 = sb("x_pair", [128, 2, PAIR])
        tqk = sb("tanh_qk", [128, 2, 2, PAIR])
        qk = sb("sigmoid_qk", [128, 2, 2, PAIR])
        tv = sb("tanh_v", [128, 2, 3, D])
        v1 = sb("sigmoid_v_and_twos", [128, 2, 3, D + 1])
        e = sb("exp_scores", [128, 2, PAIR + TAIL])
        hin = sb("h_in", [128, 2, 3, D])
        den = sb("denominators", [128, 2, 3])
        pay = sb("payload", [128, RING, 3, PAY])
        bn6 = sb("bn_stats2", [128, 3, 6])
        ve = sb("var_eps2", [128, 3])
        mhalf = sb("minus_half2", [128, 3])
        eps, ring_tokens = sb("eps", [128, 3]), sb("ring_tokens", [128, 3], I32)
        shift = sb("minus_mean_by_deviation", [128, 3])
        xn = sb("x_normalised", [128, 2, 3, D])
        xT = sb("x_transposed", [128, 2, 3, D])
        lb, d = sb("logits", [128, 3, EXPERTS]), sb("logits_less_max", [128, 3, EXPERTS])
        w, m, m2 = sb("tie_order", [128, 3, EXPERTS]), sb("max_logit", [128, 3]), sb("first_max", [128, 3])
        oh = sb("one_hot", [128, 2, 3, EXPERTS], BF16)
        ex = sb("exp_logits", [128, 2, 3, EXPERTS])
        se, rr, rro, pos = (sb("sum_exp", [128, 3]), sb("ranks", [128, 3, EXPERTS]),
                            sb("own_rank", [128, 3, EXPERTS]), sb("position", [128, 3]))
        idx = sb("row_index", [128, RING, 3], I32)
        qk_ps = kept.banks[0:2]
        v_ps, s_ps, o_ps, t_ps, lg_ps, rk_ps = kept.banks[2:8]
        N = [HEAD, HEAD, 128]

        s_init, s_x2, s_qkps, s_tqk, s_qk = sem("a_init"), sem("x2"), sem("qk_ps"), sem("tanh_qk"), sem("qk")
        s_vps, s_tv, s_v = sem("v_ps"), sem("tanh_v"), sem("v")
        s_sps, s_e, s_ops = sem("scores_ps"), sem("exp_scores"), sem("o_ps")
        s_hin = [sem(f"h_in{i}") for i in range(2)]
        s_h2, s_bn, s_mv, s_pool, s_rs = sem("h2"), sem("bn2"), sem("mv2"), sem("pool_step2"), sem("rstd2")
        s_xn, s_tps, s_xT, s_lg = sem("xn2"), sem("xT_ps"), sem("xT"), sem("logits_ps")
        s_choice, s_place, s_placed = sem("choice_step"), sem("place_step"), sem("placed")
        s_shift, s_ex, s_rk = sem("shift"), sem("exp_logits"), sem("ranks_ps")
        s_den = sem("den_step")
        s_sc = [sem(f"scattered{i}") for i in range(RING)]
        INITS = 20
        CHOICE, PLACE = 6, 5

        LAST = 5
        PEEL, UNROLL = 7, RING
        LOOPS = (PAIRS - PEEL) // UNROLL

        def steps(eng, step):
            for n in range(PEEL):
                step(0, n, lambda lag, n=n: n >= lag)
            with eng.Fori(0, LOOPS) as i:
                for j in range(PEEL, PEEL + UNROLL):
                    step(i, j, lambda lag: True)
            for n in range(PEEL + UNROLL * LOOPS, PAIRS + LAST):
                step(LOOPS, n - UNROLL * LOOPS, lambda lag, n=n: n - lag < PAIRS)

        with nc.Block() as block:
            @block.sync
            def _(sp):
                def load(i, j):
                    p = RING * i + j
                    if j >= 2:
                        sp.wait_ge(s_h2, p - 1)
                    h = kept.h
                    sp.dma_start(hin[0:HEAD, j % 2, 0:2, :], h[bass.ds(2 * p, 2), 0:HEAD * D]
                                 .rearrange("b (t e) -> t b e", e=D)).then_inc(s_hin[j % 2], 16)
                    for k in range(2):
                        sp.dma_start(hin[TAIL * k:TAIL * (k + 1), j % 2, 2, :], h[bass.ds(2 * p + k, 1), HEAD * D:]
                                     .rearrange("b (t e) -> (b t) e", e=D)).then_inc(s_hin[j % 2], 16)

                steps(sp, lambda i, j, live: live(0) and load(i, j))

            @block.gpsimd
            def _(pool):
                pool.wait_ge(s_init, INITS)
                last_row = pool.to_reg(DUMMY - 1)

                def rstd(i, j):
                    p = RING * i + j
                    pool.wait_ge(s_mv, p + 1)
                    o = pay[:, j % RING, :, :]
                    if j >= 1:
                        pool.wait_ge(s_rs, p)
                    nc.gpsimd.tensor_tensor(ve[:, :], o[:, :, D + 1], eps[:, :], ALU.add).then_inc(s_pool, 1)
                    if j >= RING:
                        number = o[:, :, D + 3].bitcast(I32)
                        nc.gpsimd.tensor_tensor(number, number, ring_tokens[:, :], ALU.add)
                    pool.wait_ge(s_pool, p + 1)
                    nc.gpsimd.tensor_tensor(o[:, :, D + 1], ve[:, :], mhalf[:, :], ALU.pow).then_inc(s_rs, 1)

                def scatter(i, j):
                    p = RING * i + j
                    own_wait(pool, s_placed, p + 1, s_init)
                    for k in range(3):
                        n = N[k]
                        nc.gpsimd.indirect_dma_start(
                            out=kept.by_expert[:, :],
                            out_offset=bass.IndirectOffsetOnAxis(ap=idx[0:n, j % RING, k:k + 1], axis=0),
                            in_=pay[0:n, j % RING, k, :], in_offset=None,
                            bounds_check=last_row, oob_is_err=False).then_inc(s_sc[j % RING], 16)

                def step(i, j, live):
                    if live(3):
                        rstd(i, j - 3)
                    if live(5):
                        scatter(i, j - 5)

                steps(pool, step)
                for scattered in s_sc:
                    pool.wait_ge(scattered, 48 * (PAIRS // RING))

            @block.scalar
            def _(act):
                nc.scalar.preload_act_table(ACT.Exp)
                act.wait_ge(s_init, INITS)

                def copy_x(i, j):
                    if j >= 2:
                        act.wait_ge(s_vps, RING * i + j - 1)
                    nc.scalar.activation(x2[:, j % 2, :], hnT[:, bass.ds((RING * i + j) * PAIR, PAIR)], ACT.Copy)\
                        .then_inc(s_x2, 1)

                def tanh_qk(i, j):
                    p = RING * i + j
                    act.wait_ge(s_qkps, p + 1)
                    if j >= 2:
                        act.wait_ge(s_qk, p - 1)
                    for k in range(2):
                        last = nc.scalar.activation(tqk[:, j % 2, k, :], qk_ps[k][:, 0:PAIR], ACT.Tanh, scale=0.5)
                    last.then_inc(s_tqk, 1)

                def tanh_v(i, j):
                    p = RING * i + j
                    act.wait_ge(s_vps, p + 1)
                    if j >= 2:
                        act.wait_ge(s_v, p - 1)
                    nc.scalar.activation(tv[:, j % 2, :, :].rearrange("p k e -> p (k e)"), v_ps[:, 0:3 * D],
                                         ACT.Tanh, scale=0.5).then_inc(s_tv, 1)

                def exp_scores(i, j):
                    p = RING * i + j
                    act.wait_ge(s_sps, p + 1)
                    if j >= 2:
                        act.wait_ge(s_ops, p - 1)
                    nc.scalar.activation(e[:, j % 2, :], s_ps[:, 0:PAIR + TAIL], ACT.Exp, scale=SCORE_SCALE)\
                        .then_inc(s_e, 1)

                def normalise(i, j):
                    p = RING * i + j
                    act.wait_ge(s_shift, p + 1)
                    if j >= 2:
                        act.wait_ge(s_tps, p - 1)
                    for k in range(3):
                        n = N[k]
                        last = nc.scalar.activation(xn[0:n, j % 2, k, :], pay[0:n, j % RING, k, 0:D], ACT.Identity,
                                                    bias=shift[0:n, k:k + 1],
                                                    scale=pay[0:n, j % RING, k, D + 1:D + 2])
                    last.then_inc(s_xn, 1)

                def copy_xT(i, j):
                    p = RING * i + j
                    act.wait_ge(s_tps, p + 1)
                    if j >= 2:
                        act.wait_ge(s_lg, p - 1)
                    nc.scalar.activation(xT[:, j % 2, :, :].rearrange("p k e -> p (k e)"), t_ps[:, 0:3 * D],
                                         ACT.Copy).then_inc(s_xT, 1)

                def exp_logits(i, j):
                    p = RING * i + j
                    act.wait_ge(s_choice, CHOICE * p + 3)
                    nc.scalar.activation(ex[:, j % 2, :, :], d[:, :, :], ACT.Exp).then_inc(s_ex, 1)

                def step(i, j, live):
                    if live(0):
                        copy_x(i, j)
                    if live(1):
                        tanh_qk(i, j - 1)
                    if live(3):
                        normalise(i, j - 3)
                    if live(4):
                        exp_logits(i, j - 4)
                    if live(1):
                        tanh_v(i, j - 1)
                    if live(3):
                        copy_xT(i, j - 3)
                    if live(1):
                        exp_scores(i, j - 1)

                steps(act, step)

            @block.vector
            def _(dve):
                inits = [
                    nc.vector.tensor_copy(upper_bf[:, :], kept.col(C_UP, 128)),
                    nc.vector.memset(ones_bf[:, :], 1.0),
                    nc.vector.tensor_copy(tri_bf[:, :], kept.col(C_TRI, 128 + 64)),
                    nc.vector.memset(v1[:, :, :, D:D + 1], 2.0),
                    nc.vector.memset(mhalf[:, :], -0.5),
                    nc.vector.memset(pay[:, :, :, 0:D + 3], 1.0),
                    *[nc.vector.tensor_scalar(pay[:, r, :, D + 3].bitcast(I32), kept.col(C_ID0, 3), float(r * PAIR),
                                              None, ALU.add) for r in range(RING)],
                    nc.vector.tensor_copy(kept.run[0][:, :], kept.col(C_RUN0, EXPERTS)),
                    nc.vector.memset(xn[:, :, :, :], 0.0),
                    nc.vector.memset(v_ps[:, :], 0.0),
                    nc.vector.memset(s_ps[:, :], 0.0),
                    nc.vector.memset(o_ps[:, :], 0.0),
                    nc.vector.memset(t_ps[:, :], 0.0),
                    nc.vector.memset(lg_ps[:, :], 0.0),
                    nc.vector.memset(rk_ps[:, :], 0.0),
                    nc.vector.memset(eps[:, :], LN_EPS),
                    nc.vector.memset(ring_tokens[:, :], RING * PAIR),
                ]
                assert len(inits) == INITS
                for ins in inits:
                    ins.then_inc(s_init, 1)
                dve.wait_ge(s_init, INITS)

                def plus_one_qk(i, j):
                    p = RING * i + j
                    dve.wait_ge(s_tqk, p + 1)
                    if j >= 2:
                        dve.wait_ge(s_sps, p - 1)
                    nc.vector.tensor_scalar(qk[:, j % 2, :, :], tqk[:, j % 2, :, :], 1.0, None, ALU.add)\
                        .then_inc(s_qk, 1)

                def plus_one_v(i, j):
                    p = RING * i + j
                    dve.wait_ge(s_tv, p + 1)
                    if j >= 2:
                        dve.wait_ge(s_ops, p - 1)
                    nc.vector.tensor_scalar(v1[:, j % 2, :, 0:D], tv[:, j % 2, :, :], 1.0, None, ALU.add)\
                        .then_inc(s_v, 1)

                def residual(i, j):
                    p = RING * i + j
                    o = o_ps[:, 0:3 * (D + 1)].rearrange("p (k e) -> p k e", k=3)
                    dve.wait_ge(s_ops, p + 1)
                    nc.vector.tensor_scalar(den[:, 0, :], o[:, :, D], 1e-30, None, ALU.max).then_inc(s_den, 1)
                    dve.wait_ge(s_den, 2 * p + 1)
                    nc.vector.reciprocal(den[:, 1, :], den[:, 0, :]).then_inc(s_den, 1)
                    dve.wait_ge(s_den, 2 * p + 2)
                    dve.wait_ge(s_hin[j % 2], 48 * (2 * i + j // 2 + 1))
                    if j >= RING:
                        dve.wait_ge(s_sc[j % RING], 48 * (i + j // RING))
                    for k in range(3):
                        last = nc.vector.scalar_tensor_tensor(
                            out=pay[0:N[k], j % RING, k, 0:D], in0=o[0:N[k], k, 0:D], scalar=den[0:N[k], 1, k:k + 1],
                            in1=hin[0:N[k], j % 2, k, :], op0=ALU.mult, op1=ALU.add)
                    last.then_inc(s_h2, 1)
                    dve.wait_ge(s_h2, p + 1)
                    for k in range(3):
                        last = nc.vector.bn_stats(bn6[0:N[k], k, :], pay[0:N[k], j % RING, k, 0:D])
                    last.then_inc(s_bn, 1)

                def aggregate(i, j):
                    own_wait(dve, s_bn, RING * i + j + 1, s_init)
                    for k in range(3):
                        last = nc.vector.bn_aggr(pay[0:N[k], j % RING, k, D:D + 2], bn6[0:N[k], k, :])
                    last.then_inc(s_mv, 1)

                def shifts(i, j):
                    p = RING * i + j
                    dve.wait_ge(s_rs, p + 1)
                    if j >= 1:
                        dve.wait_ge(s_xn, p)
                    o = pay[:, j % RING, :, :]
                    nc.vector.scalar_tensor_tensor(out=shift[:, :], in0=o[:, :, D], scalar=-1.0, in1=o[:, :, D + 1],
                                                   op0=ALU.mult, op1=ALU.mult).then_inc(s_shift, 1)

                def over_tiles(t):
                    return t[:, :].unsqueeze(1).broadcast_to([128, 3, EXPERTS])

                def over_experts(t):
                    return t[:, :].unsqueeze(2).broadcast_to([128, 3, EXPERTS])

                def route(i, j, live):
                    choosing, placing = live(4), live(5)
                    c, p = j - 4, j - 5
                    chosen, placed = CHOICE * (RING * i + c), PLACE * (RING * i + p)
                    desc = kept.col(C_DESC, EXPERTS).unsqueeze(1).broadcast_to([128, 3, EXPERTS])
                    lg = lg_ps[:, 0:3 * EXPERTS].rearrange("p (k e) -> p k e", k=3)
                    rk = rk_ps[:, 0:3 * EXPERTS].rearrange("p (k e) -> p k e", k=3)
                    run, run_next = kept.run[p % 2], kept.run[(p + 1) % 2]
                    if choosing:
                        dve.wait_ge(s_lg, RING * i + c + 1)
                        nc.vector.tensor_tensor(lb[:, :, :], lg, over_tiles(kept.b_s), ALU.add).then_inc(s_choice, 1)
                    if placing:
                        dve.wait_ge(s_rk, RING * i + p + 1)
                        if p >= 1:
                            dve.wait_ge(s_placed, RING * i + p)
                        nc.vector.tensor_tensor(rr[:, :, :], rk, over_tiles(run), ALU.add).then_inc(s_place, 1)
                    if choosing:
                        dve.wait_ge(s_choice, chosen + 1)
                        nc.vector.tensor_reduce(m[:, :], lb[:, :, :], AX.X, ALU.max).then_inc(s_choice, 1)
                    if placing:
                        dve.wait_ge(s_place, placed + 1)
                        nc.vector.tensor_tensor(rro[:, :, :], rr[:, :, :], oh[:, p % 2, :, :], ALU.mult)\
                            .then_inc(s_place, 1)
                    if choosing:
                        dve.wait_ge(s_choice, chosen + 2)
                        if c >= 1:
                            dve.wait_ge(s_ex, RING * i + c)
                        nc.vector.tensor_tensor(d[:, :, :], lb[:, :, :], over_experts(m), ALU.subtract)\
                            .then_inc(s_choice, 1)
                    if placing:
                        dve.wait_ge(s_place, placed + 2)
                        nc.vector.tensor_reduce(pos[:, :], rro[:, :, :], AX.X, ALU.add).then_inc(s_place, 1)
                    if choosing:
                        dve.wait_ge(s_choice, chosen + 3)
                        nc.vector.scalar_tensor_tensor(out=w[:, :, :], in0=d[:, :, :], scalar=0.0, in1=desc,
                                                       op0=ALU.is_equal, op1=ALU.mult).then_inc(s_choice, 1)
                    if placing:
                        dve.wait_ge(s_ex, RING * i + p + 1)
                        nc.vector.tensor_reduce(se[:, :], ex[:, p % 2, :, :], AX.X, ALU.add).then_inc(s_place, 1)
                        dve.wait_ge(s_place, placed + 3)
                        nc.vector.tensor_copy(idx[:, p % RING, :], pos[:, :]).then_inc(s_place, 1)
                    if choosing:
                        dve.wait_ge(s_choice, chosen + 4)
                        nc.vector.tensor_reduce(m2[:, :], w[:, :, :], AX.X, ALU.max).then_inc(s_choice, 1)
                    if placing:
                        dve.wait_ge(s_place, placed + 5)
                        nc.vector.reciprocal(pay[:, p % RING, :, D + 2], se[:, :])
                        nc.vector.tensor_tensor(run_next[:, :], run[:, :], rk_ps[:, 24:32], ALU.add)\
                            .then_inc(s_placed, 1)
                    if choosing:
                        dve.wait_ge(s_choice, chosen + 5)
                        if c >= 2:
                            dve.wait_ge(s_rk, RING * i + c - 1)
                        nc.vector.tensor_tensor(oh[:, c % 2, :, :], w[:, :, :], over_experts(m2), ALU.is_equal)\
                            .then_inc(s_choice, 1)

                def step(i, j, live):
                    route(i, j, live)
                    if live(3):
                        shifts(i, j - 3)
                    if live(1):
                        plus_one_qk(i, j - 1)
                    if live(2):
                        residual(i, j - 2)
                    if live(1):
                        plus_one_v(i, j - 1)
                    if live(2):
                        aggregate(i, j - 2)

                steps(dve, step)

            @block.tensor
            def _(pe):
                pe.wait_ge(s_init, INITS)

                def queries_keys(i, j):
                    p = RING * i + j
                    pe.wait_ge(s_x2, p + 1)
                    if j >= 1:
                        pe.wait_ge(s_tqk, p)
                    for k in range(2):
                        last = nc.tensor.matmul(qk_ps[k][:, 0:PAIR], kept.w_qkv[:, k, :], x2[:, j % 2, :],
                                                start=True, stop=True)
                    last.then_inc(s_qkps, 1)

                def values(i, j):
                    if j >= 1:
                        pe.wait_ge(s_tv, RING * i + j)
                    for k in range(2):
                        at = k * TOKENS
                        nc.tensor.matmul(v_ps[0:HEAD, k * D:(k + 1) * D], x2[:, j % 2, at:at + HEAD],
                                         kept.w_qkv[:, 2, :], start=True, stop=True)
                        last = nc.tensor.matmul(v_ps[TAIL * k:TAIL * (k + 1), 2 * D:3 * D],
                                                x2[:, j % 2, at + HEAD:at + TOKENS], kept.w_qkv[:, 2, :],
                                                start=True, stop=True)
                    last.then_inc(s_vps, 1)

                def scores(i, j):
                    p = RING * i + j
                    pe.wait_ge(s_qk, p + 1)
                    if j >= 1:
                        pe.wait_ge(s_e, p)
                    for k in range(2):
                        at = k * TOKENS
                        q, key = qk[:, j % 2, 0, :], qk[:, j % 2, 1, :]
                        nc.tensor.matmul(s_ps[0:HEAD, at:at + TOKENS], key[:, at:at + HEAD], q[:, at:at + TOKENS],
                                         start=True, stop=False)
                        nc.tensor.matmul(s_ps[0:HEAD, at:at + HEAD], kept.ident_bf[0:HEAD, 0:HEAD],
                                         tri_bf[0:HEAD, 0:HEAD], start=False, stop=True)
                        r = slice(TAIL * k, TAIL * (k + 1))
                        nc.tensor.matmul(s_ps[r, PAIR:PAIR + TAIL], key[:, at + HEAD:at + TOKENS],
                                         q[:, at + HEAD:at + TOKENS], start=True, stop=False)
                        last = nc.tensor.matmul(s_ps[r, PAIR:PAIR + TAIL], kept.ident_bf[r, r], tri_bf[r, 128:192],
                                                start=False, stop=True)
                    last.then_inc(s_sps, 1)

                def attend(i, j):
                    p = RING * i + j
                    pe.wait_ge(s_e, p + 1)
                    pe.wait_ge(s_v, p + 1)
                    if j >= 1:
                        pe.wait_ge(s_h2, p)
                    es, vs = e[:, j % 2, :], v1[:, j % 2, :, :]
                    for k in range(2):
                        at, r = k * TOKENS, slice(TAIL * k, TAIL * (k + 1))
                        nc.tensor.matmul(o_ps[0:HEAD, k * (D + 1):(k + 1) * (D + 1)], es[0:HEAD, at:at + HEAD],
                                         vs[0:HEAD, k, :], start=True, stop=True)
                        o = o_ps[r, 2 * (D + 1):3 * (D + 1)]
                        nc.tensor.matmul(o, es[0:HEAD, at + HEAD:at + TOKENS], vs[0:HEAD, k, :], start=True, stop=False)
                        last = nc.tensor.matmul(o, es[r, PAIR:PAIR + TAIL], vs[r, 2, :], start=False, stop=True)
                    last.then_inc(s_ops, 1)

                def transposes(i, j):
                    p = RING * i + j
                    pe.wait_ge(s_xn, p + 1)
                    if j >= 1:
                        pe.wait_ge(s_xT, p)
                    for k in range(3):
                        n = N[k]
                        last = nc.tensor.transpose(t_ps[:, k * D:k * D + n], xn[0:n, j % 2, k, :],
                                                   kept.const[0:n, C_ID:C_ID + n])
                    last.then_inc(s_tps, 1)

                def logits(i, j):
                    p = RING * i + j
                    pe.wait_ge(s_xT, p + 1)
                    if j >= 1:
                        pe.wait_ge(s_choice, CHOICE * (p - 1) + 1)
                    for k in range(3):
                        last = nc.tensor.matmul(lg_ps[0:N[k], k * EXPERTS:(k + 1) * EXPERTS], xT[:, j % 2, k, 0:N[k]],
                                                kept.w_s[:, :], start=True, stop=True)
                    last.then_inc(s_lg, 1)

                def ranks(i, j):
                    p = RING * i + j
                    pe.wait_ge(s_choice, CHOICE * (p + 1))
                    if j >= 1:
                        pe.wait_ge(s_placed, p)
                    for k in range(3):
                        o = rk_ps[:, k * EXPERTS:(k + 1) * EXPERTS]
                        for before in range(k):
                            nc.tensor.matmul(o, ones_bf[0:N[before], :], oh[0:N[before], j % 2, before, :],
                                             start=before == 0, stop=False)
                        nc.tensor.matmul(o, upper_bf[0:N[k], :], oh[0:N[k], j % 2, k, :], start=k == 0, stop=True)
                    for k in range(3):
                        last = nc.tensor.matmul(rk_ps[:, 24:32], ones_bf[0:N[k], :], oh[0:N[k], j % 2, k, :],
                                                start=k == 0, stop=k == 2)
                    last.then_inc(s_rk, 1)

                def step(i, j, live):
                    if live(1):
                        queries_keys(i, j - 1)
                    if live(2):
                        attend(i, j - 2)
                    if live(1):
                        values(i, j - 1)
                    if live(3):
                        transposes(i, j - 3)
                    if live(1):
                        scores(i, j - 1)
                    if live(3):
                        logits(i, j - 3)
                    if live(4):
                        ranks(i, j - 4)

                steps(pe, step)


def plan(nc, kept, table, w2, a):
    with ExitStack() as ctx:
        def sb(name, shape, dt=F32):
            return ctx.enter_context(nc.sbuf_tensor("plan_" + name, shape, dt))

        def sem(name):
            return nc.alloc_semaphore("plan_" + name)

        run_i = sb("run_i", [1, EXPERTS], I32)
        n_i = sb("slots_i", [1, 2, EXPERTS], I32)
        f = sb("expert_rows", [1, 8, EXPERTS])
        le = sb("expert_order", [1, EXPERTS, EXPERTS])
        nle = sb("slots_before", [1, EXPERTS, EXPERTS])
        ge = sb("slot_past_expert", [1, SLOTS, EXPERTS])
        gd = sb("slot_jumps", [1, SLOTS, EXPERTS])
        sl = sb("slot_rows", [1, 6, SLOTS])
        pad = sb("padding", [128, 2, PAY])
        s_pad, s_w2, s_p, s_fill = sem("padding_set"), sem("w2_loaded"), sem("plan_step"), sem("padding_stored")

        with nc.Block() as block:
            @block.sync
            def _(sp):
                sp.dma_start(w2[:, :], a["w2"]).then_inc(s_w2, 16)
                sp.wait_ge(s_pad, 2)
                rows = kept.by_expert
                sp.dma_start(rows[DUMMY:DUMMY + SLOT, :].rearrange("(p k) c -> p k c", k=2), pad[:, :, :])\
                    .then_inc(s_fill, 16)
                sp.wait_ge(s_p, 1)
                for x in range(EXPERTS):
                    at = sp.value_load(run_i[0:1, x:x + 1], min_val=0, max_val=DUMMY - SLOT)
                    sp.dma_start(rows[bass.ds(at, SLOT), :].rearrange("(p k) c -> p k c", k=2), pad[:, :, :])\
                        .then_inc(s_fill, 16)
                sp.wait_ge(s_fill, 16 * (EXPERTS + 1))
                sp.wait_ge(s_w2, 16)

            @block.vector
            def _(dve):
                nc.vector.memset(pad[:, :, 0:D + 3], 0.0).then_inc(s_pad, 1)
                nc.vector.memset(pad[:, :, D + 3:PAY].bitcast(I32), NOBODY).then_inc(s_pad, 1)
                count = 0

                def link(ins):
                    nonlocal count
                    count += 1
                    ins.then_inc(s_p, 1)
                    dve.wait_ge(s_p, count)

                run = kept.run[PAIRS % 2][0:1, :]
                c = kept.const
                link(nc.vector.tensor_copy(run_i[:, :], run))
                link(nc.vector.tensor_tensor(f[:, 0, :], run, c[0:1, C_RUN0:C_RUN0 + EXPERTS], ALU.subtract))
                link(nc.vector.tensor_scalar(f[:, 1, :], f[:, 0, :], float(SLOT - 1), None, ALU.add))
                link(nc.vector.tensor_copy(n_i[:, 0, :], f[:, 1, :]))
                link(nc.vector.tensor_scalar(n_i[:, 1, :], n_i[:, 0, :], int(np.log2(SLOT)), None,
                                             ALU.arith_shift_right))
                link(nc.vector.tensor_copy(f[:, 2, :], n_i[:, 1, :]))
                desc = c[0:1, C_DESC:C_DESC + EXPERTS]
                sq = [1, EXPERTS, EXPERTS]
                link(nc.vector.tensor_tensor(le[:, :, :], desc.unsqueeze(1).broadcast_to(sq),
                                             desc.unsqueeze(2).broadcast_to(sq), ALU.is_ge))
                link(nc.vector.tensor_tensor(nle[:, :, :], le[:, :, :], f[:, 2, :].unsqueeze(1).broadcast_to(sq),
                                             ALU.mult))
                link(nc.vector.tensor_reduce(f[:, 3, :], nle[:, :, :], AX.X, ALU.add))
                link(nc.vector.tensor_scalar(f[:, 4, :], f[:, 2, :], -float(SLOT), float(REGION), ALU.mult, ALU.add))
                se = [1, SLOTS, EXPERTS]
                s = c[0:1, C_SLOT:C_SLOT + SLOTS]
                link(nc.vector.tensor_tensor(ge[:, :, :], f[:, 3, :].unsqueeze(1).broadcast_to(se),
                                             s.unsqueeze(2).broadcast_to(se), ALU.is_le))
                link(nc.vector.tensor_reduce(sl[:, 0, :], ge[:, :, :], AX.X, ALU.add))
                link(nc.vector.tensor_scalar(sl[:, 1, :], sl[:, 0, :], float(EXPERTS - 1), None, ALU.min))
                link(nc.vector.tensor_copy(table[:, 0, :], sl[:, 1, :]))
                link(nc.vector.tensor_tensor(gd[:, :, :], ge[:, :, :], f[:, 4, :].unsqueeze(1).broadcast_to(se),
                                             ALU.mult))
                link(nc.vector.tensor_reduce(sl[:, 2, :], gd[:, :, :], AX.X, ALU.add))
                link(nc.vector.scalar_tensor_tensor(out=sl[:, 3, :], in0=s, scalar=float(SLOT), in1=sl[:, 2, :],
                                                    op0=ALU.mult, op1=ALU.add))
                link(nc.vector.tensor_scalar(sl[:, 4, :], sl[:, 3, :], float(DUMMY), None, ALU.min))
                link(nc.vector.tensor_copy(table[:, 1, :], sl[:, 4, :]))


def experts(nc, kept, table, w2, out):
    with ExitStack() as ctx:
        def sb(name, shape, dt=F32):
            return ctx.enter_context(nc.sbuf_tensor("ffn_" + name, shape, dt))

        def sem(name):
            return nc.alloc_semaphore("ffn_" + name)

        pay = sb("rows", [128, SLOT_UNROLL, 2, PAY])
        xn = sb("x_n", [128, 2, 2, D])
        xh = sb("x_hi", [128, 2, SLOT], F16)
        xl = sb("x_lo", [128, 2, SLOT], F16)
        g = sb("gelu", [128, 2, FC, SLOT])
        y = sb("ffn", [128, 2, 2, D])
        o = sb("out_rows", [128, OUT_RING, 2, D])
        up_ps = [kept.banks[0:2], kept.banks[2:4]]
        down_ps, t_ps = kept.banks[4:6], kept.banks[6:8]

        s_in = [sem(f"rows_loaded{i}") for i in range(SLOT_UNROLL)]
        s_xn, s_t, s_hi, s_lo = sem("x_n"), sem("x_t_ps"), sem("x_hi"), sem("x_lo")
        s_up, s_g, s_down, s_y, s_o = sem("up_ps"), sem("gelu"), sem("down_ps"), sem("y"), sem("out_rows")
        s_st = [sem(f"stored{i}") for i in range(OUT_RING)]

        PEEL = OUT_RING + 3
        LOOPS = (SLOTS - PEEL) // SLOT_UNROLL

        def steps(eng, step):
            for n in range(PEEL):
                step(0, n, lambda lag, n=n: n >= lag)
            with eng.Fori(0, LOOPS) as i:
                for j in range(PEEL, PEEL + SLOT_UNROLL):
                    step(i, j, lambda lag: True)
            for n in range(PEEL + SLOT_UNROLL * LOOPS, SLOTS + 3):
                step(LOOPS, n - SLOT_UNROLL * LOOPS, lambda lag, n=n: n - lag < SLOTS)

        def stores(i, j):
            return SLOT_UNROLL // OUT_RING * i + j // OUT_RING + 1

        def expert(eng, s):
            return eng.value_load(table[0:1, 0, bass.ds(s, 1)], min_val=0, max_val=EXPERTS - 1)

        with nc.Block() as block:
            @block.sync
            def _(sp):
                def load(i, j):
                    s = SLOT_UNROLL * i + j
                    at = sp.value_load(table[0:1, 1, bass.ds(s, 1)], min_val=0, max_val=DUMMY)
                    if j >= SLOT_UNROLL:
                        sp.wait_ge(s_st[j % OUT_RING], 32 * stores(i, j - SLOT_UNROLL))
                    sp.dma_start(pay[:, j % SLOT_UNROLL, :, :], kept.by_expert[bass.ds(at, SLOT), :]
                                 .rearrange("(k p) c -> p k c", k=2)).then_inc(s_in[j % SLOT_UNROLL], 16)

                for j in range(SLOT_UNROLL):
                    load(0, j)
                with sp.Fori(0, SLOTS // SLOT_UNROLL - 1) as i:
                    for j in range(SLOT_UNROLL, 2 * SLOT_UNROLL):
                        load(i, j)
                for j in range(SLOT_UNROLL, SLOT_UNROLL + SLOTS % SLOT_UNROLL):
                    load(SLOTS // SLOT_UNROLL - 1, j)

            @block.gpsimd
            def _(pool):
                last_row = pool.to_reg(ALL - 1)

                def store(i, j):
                    s = SLOT_UNROLL * i + j
                    own_wait(pool, s_o, s + 1, s_xn)
                    for k in range(2):
                        nc.gpsimd.indirect_dma_start(
                            out=out[:, :], out_offset=bass.IndirectOffsetOnAxis(
                                ap=pay[:, j % SLOT_UNROLL, k, D + 3:D + 4].bitcast(I32), axis=0),
                            in_=o[:, j % OUT_RING, k, :], in_offset=None,
                            bounds_check=last_row, oob_is_err=False).then_inc(s_st[j % OUT_RING], 16)

                steps(pool, lambda i, j, live: live(3) and store(i, j - 3))
                for s in range(SLOTS - OUT_RING, SLOTS):
                    pool.wait_ge(s_st[s % OUT_RING], 32 * stores(0, s))

            @block.scalar
            def _(act):
                nc.scalar.preload_act_table(ACT.Gelu)

                def high(i, j):
                    s = SLOT_UNROLL * i + j
                    act.wait_ge(s_t, s + 1)
                    if j >= 2:
                        act.wait_ge(s_up, s - 1)
                    nc.scalar.activation(xh[:, j % 2, :], t_ps[j % 2][:, 0:SLOT], ACT.Copy).then_inc(s_hi, 1)

                def gelu(i, j):
                    s = SLOT_UNROLL * i + j
                    x = expert(act, s)
                    act.wait_ge(s_up, s + 1)
                    if j >= 2:
                        act.wait_ge(s_down, s - 1)
                    for c in range(FC):
                        last = nc.scalar.activation(g[:, j % 2, c, :],
                                                    up_ps[j % 2][c // 2][:, c % 2 * SLOT:(c % 2 + 1) * SLOT],
                                                    ACT.Gelu, bias=kept.b1[:, bass.ds(x * FC + c, 1)],
                                                    scale=1.0 / W_SCALE)
                    last.then_inc(s_g, 1)

                def step(i, j, live):
                    if live(1):
                        high(i, j - 1)
                    if live(2):
                        gelu(i, j - 2)

                steps(act, step)

            @block.vector
            def _(dve):
                def normalise(i, j):
                    s = SLOT_UNROLL * i + j
                    dve.wait_ge(s_in[j % SLOT_UNROLL], 16 * (i + j // SLOT_UNROLL + 1))
                    if j >= 2:
                        dve.wait_ge(s_t, s - 1)
                    p = pay[:, j % SLOT_UNROLL, :, :]
                    for k in range(2):
                        last = nc.vector.tensor_scalar(xn[:, j % 2, k, :], p[:, k, 0:D], p[:, k, D:D + 1],
                                                       p[:, k, D + 1:D + 2], ALU.subtract, ALU.mult)
                    last.then_inc(s_xn, 1)

                def low(i, j):
                    s = SLOT_UNROLL * i + j
                    dve.wait_ge(s_hi, s + 1)
                    if j >= 2:
                        dve.wait_ge(s_up, s - 1)
                    nc.vector.tensor_tensor(xl[:, j % 2, :], t_ps[j % 2][:, 0:SLOT], xh[:, j % 2, :], ALU.subtract)\
                        .then_inc(s_lo, 1)

                def finish(i, j):
                    s = SLOT_UNROLL * i + j
                    x = expert(dve, s)
                    dve.wait_ge(s_down, s + 1)
                    if j >= OUT_RING:
                        dve.wait_ge(s_st[j % OUT_RING], 32 * stores(i, j - OUT_RING))
                    p = pay[:, j % SLOT_UNROLL, :, :]
                    last = nc.vector.tensor_tensor(y[:, j % 2, :, :],
                                                   down_ps[j % 2][:, 0:2 * D].rearrange("p (k e) -> p k e", k=2),
                                                   kept.b2[:, bass.ds(x * D, D)].unsqueeze(1)
                                                   .broadcast_to([128, 2, D]), ALU.add)
                    last.then_inc(s_y, 1)
                    dve.wait_ge(s_y, s + 1)
                    for k in range(2):
                        last = nc.vector.scalar_tensor_tensor(out=o[:, j % OUT_RING, k, :], in0=y[:, j % 2, k, :],
                                                              scalar=p[:, k, D + 2:D + 3], in1=p[:, k, 0:D],
                                                              op0=ALU.mult, op1=ALU.add)
                    last.then_inc(s_o, 1)

                def step(i, j, live):
                    if live(0):
                        normalise(i, j)
                    if live(1):
                        low(i, j - 1)
                    if live(3):
                        finish(i, j - 3)

                steps(dve, step)

            @block.tensor
            def _(pe):
                def transposes(i, j):
                    s = SLOT_UNROLL * i + j
                    pe.wait_ge(s_xn, s + 1)
                    if j >= 2:
                        pe.wait_ge(s_lo, s - 1)
                    for k in range(2):
                        last = nc.tensor.transpose(t_ps[j % 2][:, k * D:(k + 1) * D], xn[:, j % 2, k, :],
                                                   kept.col(C_ID, 128))
                    last.then_inc(s_t, 1)

                def up(i, j):
                    s = SLOT_UNROLL * i + j
                    x = expert(pe, s)
                    pe.wait_ge(s_lo, s + 1)
                    if j >= 2:
                        pe.wait_ge(s_g, s - 1)
                    for c in range(FC):
                        u = up_ps[j % 2][c // 2][:, c % 2 * SLOT:(c % 2 + 1) * SLOT]
                        hi, lo = (t[:, bass.ds(x * F + c * 128, 128)] for t in (kept.w1_hi, kept.w1_lo))
                        nc.tensor.matmul(u, hi, xh[:, j % 2, :], start=True, stop=False)
                        nc.tensor.matmul(u, hi, xl[:, j % 2, :], start=False, stop=False)
                        last = nc.tensor.matmul(u, lo, xh[:, j % 2, :], start=False, stop=True)
                    last.then_inc(s_up, 1)

                def down(i, j):
                    s = SLOT_UNROLL * i + j
                    x = expert(pe, s)
                    pe.wait_ge(s_g, s + 1)
                    if j >= 2:
                        pe.wait_ge(s_o, s - 1)
                    for k in range(2):
                        for c in range(FC):
                            last = nc.tensor.matmul(down_ps[j % 2][:, k * D:(k + 1) * D],
                                                    g[:, j % 2, c, k * 128:(k + 1) * 128],
                                                    w2[:, bass.ds(x * F + c * D, D)], start=c == 0, stop=c == FC - 1)
                    last.then_inc(s_down, 1)

                def step(i, j, live):
                    if live(1):
                        transposes(i, j - 1)
                    if live(2):
                        up(i, j - 2)
                    if live(3):
                        down(i, j - 3)

                steps(pe, step)


def build(nc, out, **a):
    kept = Kept(nc)
    with nc.sbuf_tensor("hnT", [128, ALL], F32) as hnT:
        with ExitStack() as ctx:
            def sb(name, shape, dt=F32):
                return ctx.enter_context(nc.sbuf_tensor(name, shape, dt))
            tok = {"w": sb("w_tok_sb", [128, VARIANTS, D]), "gamma": sb("gamma_sb", [128, TOKENS, VARIANTS]),
                   "rstd": sb("rstd_image", [128, 1]), "stT": sb("image_parts_T", [PARTS, IMAGES], BF16)}
            image_statistics(nc, kept, hnT, tok, a)
            tokenizer(nc, kept, hnT, tok, a)
        attention(nc, kept, hnT, a)
    with nc.sbuf_tensor("slot_table", [1, 2, SLOTS], I32) as table, \
            nc.sbuf_tensor("w2_sb", [128, EXPERTS * F], F32) as w2:
        plan(nc, kept, table, w2, a)
        experts(nc, kept, table, w2, out)


def kernel(x, L0_tok_gamma, L0_tok_beta, L0_tok_W, L0_tok_b, L0_attn_Wq, L0_attn_Wv, L0_attn_Wk,
           L0_ffn_Ws, L0_ffn_bs, L0_ffn_W1, L0_ffn_b1, L0_ffn_W2, L0_ffn_b2):
    import concourse.bacc as bacc
    from concourse.bass_utils import run_bass_kernel_spmd

    def patches(p, g):
        b = p.shape[0]
        return np.asarray(p).reshape(b, 2, g, 2, 4, g, 2, 4).transpose(3, 6, 1, 4, 7, 2, 5, 0).reshape(128, g, g, b)

    def positions(p):
        return np.asarray(p).reshape(VARIANTS, 2, GRID, 2, 4, GRID, 2, 4).transpose(3, 6, 1, 4, 7, 2, 5, 0)\
            .reshape(128, TOKENS, VARIANTS)

    x = np.asarray(x)
    arrays = {
        "x_al": patches(x, GRID),
        "x_off": patches(np.pad(x, ((0, 0), (0, 0), (4, 4), (4, 4))), GRID + 1),
        "gamma": positions(L0_tok_gamma),
        "beta": positions(L0_tok_beta),
        "w_tok": np.asarray(L0_tok_W).reshape(D, VARIANTS, 2, 2, 4, 2, 4).transpose(3, 5, 2, 4, 6, 1, 0)
        .reshape(128, VARIANTS, D),
        "b_tok": np.asarray(L0_tok_b).reshape(1, D),
        "w_q": np.asarray(L0_attn_Wq), "w_k": np.asarray(L0_attn_Wv), "w_v": np.asarray(L0_attn_Wk),
        "w_s": np.asarray(L0_ffn_Ws),
        "b_s": np.asarray(L0_ffn_bs).reshape(1, EXPERTS),
        "w1": np.asarray(L0_ffn_W1).transpose(1, 0, 2).reshape(D, EXPERTS * F),
        "b1": np.asarray(L0_ffn_b1).reshape(EXPERTS, FC, 128).transpose(2, 0, 1).reshape(128, EXPERTS * FC),
        "w2": np.asarray(L0_ffn_W2).reshape(EXPERTS, FC, 128, D).transpose(2, 0, 1, 3).reshape(128, EXPERTS * F),
        "b2": np.asarray(L0_ffn_b2).reshape(1, EXPERTS * D),
        "const": constants(),
    }
    arrays = {n: np.ascontiguousarray(v) for n, v in arrays.items()}
    nc = bacc.Bacc("TRN2", target_bir_lowering=False, num_devices=1)
    aps = {n: nc.dram_tensor(n, v.shape, F32, kind="ExternalInput").ap() for n, v in arrays.items()}
    out = nc.dram_tensor("out", (ALL, D), F32, kind="ExternalOutput").ap()
    build(nc, out, **aps)
    r = run_bass_kernel_spmd(nc, [arrays], core_ids=[0])
    return r.results[0]["out"].reshape(IMAGES, TOKENS, D)
```

```python
from contextlib import ExitStack

import numpy as np
import concourse.bass as bass
from concourse import mybir

F32 = mybir.dt.float32
BF16 = mybir.dt.bfloat16
F16 = mybir.dt.float16
I32 = mybir.dt.int32
ALU = mybir.AluOpType
ACT = mybir.ActivationFunctionType
AX = mybir.AxisListType

IMAGES = 128
D = 128
GRID = 13
TOKENS = GRID * GRID
ALL = IMAGES * TOKENS
VARIANTS = 5
PIXELS = 10 * 104 * 104
TOK_EPS = 1e-7
LN_EPS = 1e-5
GROUP_AT = [0, 4, 7, 10]
GROUP_N = [4, 3, 3, 3]
GROUPS = len(GROUP_AT)
ROW_UNROLL = 4
PARTS = 12
CHUNKS = [(0, 3), (3, 6), (6, 9), (9, 12), (12, 13)]
RUNS = [(0, 0, 1), (0, 1, 3), (1, 3, 6), (2, 6, 9), (3, 9, 12), (4, 12, 13)]
PE_CHUNK = 3

PAIRS = IMAGES // 2
HEAD = 105
TAIL = TOKENS - HEAD
PAIR = 2 * TOKENS
EXPERTS = 8
F = 512
FC = F // 128
SLOT = 256
REGION = ALL + SLOT
DUMMY = EXPERTS * REGION
SLOTS = (ALL + EXPERTS * (SLOT - 1)) // SLOT
PAY = D + 4
NOBODY = 1 << 20
SLOT_UNROLL = 8
RUN = SLOT_UNROLL + 2
WORDS = SLOTS - RUN + 1
OUT_RING = 4
W_SCALE = 64.0
MASKED = -30000.0
SCORE_SCALE = 0.25 / float(np.sqrt(np.float32(D)))

C_ID, C_UP, C_TRI, C_TRIT, C_MULT = 0, 128, 256, 384, 448
C_DESC, C_RUN0, C_ID0, C_HALF, C_END = 457, 465, 473, 476, 478


def constants():
    c = np.zeros((128, C_END), np.float32)
    k = np.arange(128)
    c[:, C_ID:C_ID + 128] = np.eye(128)
    c[:, C_UP:C_UP + 128] = k[:, None] < k[None, :]
    c[:, C_TRI:C_TRI + 128] = np.where(k[:, None] < k[None, :], 0.0, MASKED)
    c[:, C_TRIT:C_TRIT + 64] = np.where(k[:, None] % 64 < k[None, :64], 0.0, MASKED)
    r, s = k // 64, k // 32 % 2
    for a in range(3):
        for b in range(3):
            over = 2 - ((a == 0) & (r == 0)) - ((a == 2) & (r == 1))
            across = 2 - ((b == 0) & (s == 0)) - ((b == 2) & (s == 1))
            c[:, C_MULT + 3 * a + b] = 1 + over * across
    e = np.arange(EXPERTS)
    c[:, C_DESC:C_DESC + EXPERTS] = EXPERTS - e
    c[:, C_RUN0:C_RUN0 + EXPERTS] = e * REGION
    c[:, C_ID0] = k
    c[:, C_ID0 + 1] = TOKENS + k
    c[:, C_ID0 + 2] = np.where(k < TAIL, HEAD + k, TOKENS + HEAD + k - TAIL)
    c[:, C_HALF] = np.where(k == 0, 0.0, 0.5)
    c[:, C_HALF + 1] = 0.5
    return c


def own_wait(eng, sem, value, passed):
    if not isinstance(value, int):
        value = eng.to_reg(value)
    eng.wait_ge(passed, 1)
    eng.wait_ge(sem, value)


class Kept:

    def __init__(self, nc):
        def sb(name, shape, dt=F32):
            return nc.alloc_sbuf_tensor(name, shape, dt)

        def dram(name, shape, dt=F32):
            return nc.dram_tensor(name, shape, dt, kind="Internal").ap()

        self.banks = [nc.alloc_psum_tensor(f"bank{i}", [128, 512], F32) for i in range(8)]
        self.const = sb("constants", [128, C_END])
        self.ident_bf = sb("ident_bf", [128, 128], BF16)
        self.w_qkv = sb("w_qkv", [128, 3, D])
        self.w_s = sb("w_s_sb", [128, EXPERTS])
        self.b_s = sb("b_s_sb", [128, EXPERTS])
        self.b1 = sb("b1_sb", [128, EXPERTS * FC])
        self.b2 = sb("b2_parts", [96, EXPERTS * D], BF16)
        self.share = sb("one_32nd", [96, 128], BF16)
        self.run = [sb(f"run{i}", [128, EXPERTS]) for i in range(2)]
        self.h = dram("h_rows", (IMAGES, TOKENS * D))
        self.gb = dram("gamma_beta_parts", (PARTS, TOKENS * D), BF16)
        self.by_expert = dram("rows_by_expert", (DUMMY + SLOT, PAY))

    def col(self, at, n=1):
        return self.const[:, at:at + n]


class TokenizerRows:

    def __init__(self, nc, ctx, kept, a):
        self.xa = ctx.enter_context(nc.sbuf_tensor("x_aligned", [128, 2, GRID * IMAGES], F32))
        self.xo = ctx.enter_context(nc.sbuf_tensor("x_offset", [128, 4, (GRID + 1) * IMAGES], F32))
        self.gbr = ctx.enter_context(nc.sbuf_tensor("parts_row", [PARTS, 2, GRID * D], BF16))
        self.s_xa = [nc.alloc_semaphore(f"x_aligned_loaded{i}") for i in range(2)]
        self.s_xo = [nc.alloc_semaphore(f"x_offset_loaded{i}") for i in range(4)]
        self.s_gb = [nc.alloc_semaphore(f"parts_row_loaded{i}") for i in range(2)]
        self.xa_d = a["x_al"].rearrange("p r c b -> p (r c b)")
        self.xo_d = a["x_off"].rearrange("p r c b -> p (r c b)")
        self.gb_d = kept.gb

    def load_xa(self, eng, row, n):
        w = GRID * IMAGES
        eng.dma_start(self.xa[:, n % 2, :], self.xa_d[:, bass.ds(row * w, w)]).then_inc(self.s_xa[n % 2], 16)

    def load_parts(self, eng, row, n):
        w = GRID * D
        eng.dma_start(self.gbr[:, n % 2, :], self.gb_d[:, bass.ds(row * w, w)]).then_inc(self.s_gb[n % 2], 16)

    def load_xo(self, eng, row, n):
        w = (GRID + 1) * IMAGES
        eng.dma_start(self.xo[:, n % 4, :], self.xo_d[:, bass.ds(row * w, w)]).then_inc(self.s_xo[n % 4], 16)


def image_statistics(nc, kept, hnT, tok, rows_in, a):
    with ExitStack() as ctx:
        def sb(name, shape, dt=F32):
            return ctx.enter_context(nc.sbuf_tensor("stats_" + name, shape, dt))

        def sem(name):
            return nc.alloc_semaphore("stats_" + name)

        ROW = GRID * IMAGES
        x_dram = a["x_al"].rearrange("p r c b -> p (r c b)")
        x = hnT[:, :].rearrange("p (r c b) -> p r c b", r=GRID, c=GRID)
        sq = sb("squares", [128, 2, 3 * ROW])
        X_RUNS = [run for run in RUNS if run[0] < PE_CHUNK]
        red = sb("reduced_rows", [128, len(X_RUNS) + len(RUNS), IMAGES])
        inner = sb("inner_sums", [1, 4 * IMAGES])
        beta = sb("beta_sb", [128, TOKENS, VARIANTS])
        b_tok = sb("b_tok_sb", [128, D])
        rest = sb("parts_rest", [128, 2, 2, D])
        rest2 = sb("parts_rest2", [128, 2, 2, D])
        rest3 = sb("parts_rest3", [128, 2, 2, D])
        part = sb("parts", [128, 2, 2, 3, D], BF16)
        s12 = sb("image_sums", [128, 8])
        mhalf = sb("minus_half", [128, 1])
        sv = sb("minus_mean_and_deviation", [128, 2])
        svr = sb("image_parts_rest", [128, 2, 2])
        sp = sb("image_parts", [128, 2, 3], BF16)
        stp = sb("image_part_columns", [128, 2, 6])
        gb_ps, sum_ps, ssq_ps, st_ps = kept.banks[0], kept.banks[1], kept.banks[2], kept.banks[3]
        inner_ps = kept.banks[4]

        s_cst, s_wt, s_w, s_b = sem("c_loaded"), sem("tok_w_loaded"), sem("w_loaded"), sem("b_loaded")
        s_x = [sem(f"x_chunk_loaded{i}") for i in range(len(CHUNKS))]
        s_idb, s_sq, s_xred, s_sqred = sem("ident_cast"), sem("squared"), sem("x_reduced"), sem("sq_reduced")
        s_sums, s_gbp, s_ch, s_gbw = sem("sums_done"), sem("gb_products"), sem("split_step"), sem("gb_stored")
        s_half, s_pow, s_stp, s_stT = sem("minus_half_set"), sem("rstd_img"), sem("stp_ready"), sem("stp_transposed")
        s_done, s_ssq = sem("stT_ready"), sem("sq_products_done")
        s_inner, s_inner_sb = sem("inner_sums_ps"), sem("inner_sums_sb")
        T_AT, T_N = [0, 128], [128, TOKENS - 128]

        def squares(c):
            lo, hi = CHUNKS[c]
            return sq[:, c % 2, 0:(hi - lo) * ROW].rearrange("p (r c b) -> p r c b", c=GRID, b=IMAGES)

        with nc.Block() as block:
            @block.sync
            def _(sp_):
                sp_.dma_start(tok["w"][:, :, :], a["w_tok"]).then_inc(s_wt, 16)
                sp_.dma_start(tok["gamma"][:, :, :], a["gamma"]).then_inc(s_wt, 16)
                sp_.dma_start(beta[:, :, :], a["beta"]).then_inc(s_wt, 16)
                sp_.dma_start(kept.const[:, :], a["const"]).then_inc(s_cst, 16)
                sp_.dma_start(b_tok[:, :], a["b_tok"].broadcast_to([128, D])).then_inc(s_b, 16)
                for c, (lo, hi) in enumerate(CHUNKS):
                    sp_.dma_start(hnT[:, lo * ROW:hi * ROW], x_dram[:, lo * ROW:hi * ROW]).then_inc(s_x[c], 16)
                for i, n in enumerate(("w_q", "w_k", "w_v")):
                    sp_.dma_start(kept.w_qkv[:, i, :], a[n]).then_inc(s_w, 16)
                sp_.dma_start(kept.w_s[:, :], a["w_s"]).then_inc(s_w, 16)
                sp_.dma_start(kept.b_s[:, :], a["b_s"].broadcast_to([128, EXPERTS])).then_inc(s_w, 16)
                sp_.dma_start(kept.b1[:, :], a["b1"]).then_inc(s_w, 16)
                gb = kept.gb.rearrange("(q r) (t e) -> t q r e", q=2, e=D)
                for j in range(2):
                    sp_.wait_ge(s_ch, 6 * (j + 1))
                    for q in range(2):
                        for at, n in ((0, 3), (3, 2), (5, 1)):
                            sp_.dma_start(gb[T_AT[j]:T_AT[j] + T_N[j], q, at:at + n, :],
                                          part[0:T_N[j], j, q, 0:n, :]).then_inc(s_gbw, 16)
                for n in range(4):
                    rows_in.load_xo(sp_, n, n)
                    if n < 2:
                        rows_in.load_xa(sp_, n, n)
                sp_.wait_ge(s_gbw, 16 * 12)
                for n in range(2):
                    rows_in.load_parts(sp_, n, n)
                sp_.wait_ge(s_w, 16 * 6)

            @block.gpsimd
            def _(pool):
                nc.gpsimd.memset(mhalf[:, :], -0.5).then_inc(s_half, 1)
                pool.wait_ge(s_half, 1)
                pool.wait_ge(s_stp, 4)
                nc.gpsimd.tensor_tensor(tok["rstd"][:, :], s12[:, 5:6], mhalf[:, :], ALU.pow).then_inc(s_pow, 1)

            @block.scalar
            def _(act):
                for c, (lo, hi) in enumerate(CHUNKS):
                    act.wait_ge(s_x[c], 16)
                    if c >= 2:
                        act.wait_ge(s_sqred, sum(run[0] <= c - 2 for run in RUNS))
                        act.wait_ge(s_ssq, c - 1)
                    nc.scalar.activation(squares(c), x[:, lo:hi, :, :], ACT.Square).then_inc(s_sq, 1)
                act.wait_ge(s_inner, 1)
                nc.scalar.activation(inner[:, :], inner_ps[0:1, :], ACT.Copy).then_inc(s_inner_sb, 1)

            @block.vector
            def _(dve):
                dve.wait_ge(s_cst, 16)
                nc.vector.tensor_copy(kept.ident_bf[:, :], kept.col(C_ID, 128)).then_inc(s_idb, 1)
                dve.wait_ge(s_gbp, 1)
                dve.wait_ge(s_b, 16)
                steps = 0

                def link(ins):
                    nonlocal steps
                    steps += 1
                    ins.then_inc(s_ch, 1)
                    dve.wait_ge(s_ch, steps)

                for j in range(2):
                    n = T_N[j]
                    ps = gb_ps[0:n, 256 * j:256 * j + 256].rearrange("p (q e) -> p q e", q=2)
                    r = [t[0:n, j, :, :] for t in (rest, rest2, rest3)]
                    nc.vector.tensor_copy(r[0][:, 0, :], ps[:, 0, :])
                    link(nc.vector.scalar_tensor_tensor(out=r[0][:, 1, :], in0=ps[:, 1, :],
                                                        scalar=kept.const[0:n, C_HALF + j:C_HALF + j + 1],
                                                        in1=b_tok[0:n, :], op0=ALU.add, op1=ALU.add))
                    link(nc.vector.tensor_copy(part[0:n, j, :, 0, :], r[0]))
                    link(nc.vector.tensor_tensor(r[1], r[0], part[0:n, j, :, 0, :], ALU.subtract))
                    link(nc.vector.tensor_copy(part[0:n, j, :, 1, :], r[1]))
                    link(nc.vector.tensor_tensor(r[2], r[1], part[0:n, j, :, 1, :], ALU.subtract))
                    link(nc.vector.tensor_copy(part[0:n, j, :, 2, :], r[2]))

                def reduce_x(chunk):
                    for n, (c, first, end) in enumerate(X_RUNS):
                        if c == chunk:
                            dve.wait_ge(s_x[c], 16)
                            nc.vector.tensor_reduce(red[:, n, :], x[:, first:end, 1:GRID - 1, :]
                                                    .rearrange("p r c b -> p b r c"), AX.XY, ALU.add)\
                                .then_inc(s_xred, 1)

                def reduce_squares(chunk):
                    for n, (c, first, end) in enumerate(RUNS):
                        if c == chunk:
                            dve.wait_ge(s_sq, c + 1)
                            at = CHUNKS[c][0]
                            nc.vector.tensor_reduce(red[:, len(X_RUNS) + n, :],
                                                    squares(c)[:, first - at:end - at, 1:GRID - 1, :]
                                                    .rearrange("p r c b -> p b r c"), AX.XY, ALU.add)\
                                .then_inc(s_sqred, 1)

                for c in range(len(CHUNKS)):
                    reduce_x(c)
                    reduce_squares(c)
                dve.wait_ge(s_sums, 2)
                stp_steps = 0

                def then(ins):
                    nonlocal stp_steps
                    stp_steps += 1
                    ins.then_inc(s_stp, 1)
                    dve.wait_ge(s_stp, stp_steps)

                then(nc.vector.tensor_scalar(s12[:, 0:1], sum_ps[:, 0:1], 1.0 / PIXELS, None, ALU.mult))
                nc.vector.tensor_scalar(s12[:, 2:3], ssq_ps[:, 0:1], 1.0 / PIXELS, TOK_EPS, ALU.mult, ALU.add)
                then(nc.vector.tensor_tensor(s12[:, 3:4], s12[:, 0:1], s12[:, 0:1], ALU.mult))
                then(nc.vector.tensor_tensor(s12[:, 4:5], s12[:, 2:3], s12[:, 3:4], ALU.subtract))
                then(nc.vector.tensor_scalar(s12[:, 5:6], s12[:, 4:5], TOK_EPS, None, ALU.max))
                dve.wait_ge(s_pow, 1)
                nc.vector.tensor_scalar(sv[:, 0:1], s12[:, 0:1], -1.0, None, ALU.mult)
                then(nc.vector.tensor_tensor(sv[:, 1:2], s12[:, 5:6], tok["rstd"][:, :], ALU.mult))
                then(nc.vector.tensor_copy(sp[:, :, 0], sv[:, :]))
                then(nc.vector.tensor_tensor(svr[:, 0, :], sv[:, :], sp[:, :, 0], ALU.subtract))
                then(nc.vector.tensor_copy(sp[:, :, 1], svr[:, 0, :]))
                then(nc.vector.tensor_tensor(svr[:, 1, :], svr[:, 0, :], sp[:, :, 1], ALU.subtract))
                then(nc.vector.tensor_copy(sp[:, :, 2], svr[:, 1, :]))
                for q in range(2):
                    for at, n, p in ((0, 3, 0), (3, 2, 1), (5, 1, 2)):
                        last = nc.vector.tensor_copy(stp[:, q, at:at + n], sp[:, q, p:p + 1].broadcast_to([128, n]))
                then(last)
                dve.wait_ge(s_stT, 1)
                nc.vector.tensor_copy(tok["stT"][:, :], st_ps[0:PARTS, 0:IMAGES]).then_inc(s_done, 1)

            @block.tensor
            def _(pe):
                pe.wait_ge(s_wt, 48)
                for j in range(2):
                    for q, g in enumerate((tok["gamma"], beta)):
                        for v in range(VARIANTS):
                            last = nc.tensor.matmul(gb_ps[0:T_N[j], 256 * j + 128 * q:256 * j + 128 * q + D],
                                                    g[:, T_AT[j]:T_AT[j] + T_N[j], v], tok["w"][:, v, :],
                                                    start=v == 0, stop=v == VARIANTS - 1)
                last.then_inc(s_gbp, 1)
                pe.wait_ge(s_cst, 16)

                def edge(r):
                    return 0 if r == 0 else 2 if r == GRID - 1 else 1

                def edge_columns(ps, c, source):
                    lo, hi = CHUNKS[c]
                    for r in range(lo, hi):
                        for col, k in ((0, 0), (GRID - 1, 2)):
                            last = nc.tensor.matmul(ps[:, 0:1], source[:, r - lo, col, :],
                                                    kept.col(C_MULT + 3 * edge(r) + k),
                                                    start=r == 0 and col == 0, stop=False)
                    return last

                def inner_columns(c):
                    lo, hi = CHUNKS[c]
                    for r in range(lo, hi):
                        for col in range(1, GRID - 1, 4):
                            n = min(4, GRID - 1 - col)
                            last = nc.tensor.matmul(inner_ps[0:1, 0:n * IMAGES], kept.col(C_MULT + 3 * edge(r) + 1),
                                                    x[:, r, col:col + n, :], start=r == CHUNKS[PE_CHUNK][0] and col == 1,
                                                    stop=r == GRID - 1 and n < 4)
                    return last

                def reduced(chunks):
                    for runs, ready, base, ps in ((X_RUNS, s_xred, 0, sum_ps), (RUNS, s_sqred, len(X_RUNS), ssq_ps)):
                        for n, (c, first, end) in enumerate(runs):
                            if c in chunks:
                                pe.wait_ge(ready, n + 1)
                                last = nc.tensor.matmul(ps[:, 0:1], red[:, base + n, :],
                                                        kept.col(C_MULT + 3 * edge(first) + 1), start=False,
                                                        stop=(c, ps) == (len(CHUNKS) - 1, ssq_ps))
                    return last

                for c, (lo, hi) in enumerate(CHUNKS):
                    pe.wait_ge(s_x[c], 16)
                    edge_columns(sum_ps, c, x[:, lo:hi, :, :])
                    if c >= 3:
                        reduced([c - 3])
                    if c >= PE_CHUNK:
                        last = inner_columns(c)
                        if c == len(CHUNKS) - 1:
                            last.then_inc(s_inner, 1)
                    pe.wait_ge(s_sq, c + 1)
                    edge_columns(ssq_ps, c, squares(c)).then_inc(s_ssq, 1)
                reduced(range(2, len(CHUNKS))).then_inc(s_sums, 1)
                pe.wait_ge(s_inner_sb, 1)
                for n in range(4):
                    last = nc.tensor.matmul(sum_ps[:, 0:1], inner[0:1, n * IMAGES:(n + 1) * IMAGES],
                                            kept.const[0:1, C_ID:C_ID + 1], start=False, stop=n == 3)
                last.then_inc(s_sums, 1)
                pe.wait_ge(s_stp, 11)
                nc.tensor.transpose(st_ps[0:PARTS, 0:IMAGES], stp[:, :, :].rearrange("p q r -> p (q r)"),
                                    kept.col(C_ID, 128)).then_inc(s_stT, 1)


def tokenizer(nc, kept, hnT, tok, rows_in):
    with ExitStack() as ctx:
        def sb(name, shape, dt=F32):
            return ctx.enter_context(nc.sbuf_tensor("tok_" + name, shape, dt))

        def sem(name):
            return nc.alloc_semaphore("tok_" + name)

        xa, xo, gbr = rows_in.xa, rows_in.xo, rows_in.gbr
        s_xa, s_xo, s_gb = rows_in.s_xa, rows_in.s_xo, rows_in.s_gb
        wg = sb("scaled_weights", [128, 4, VARIANTS, D])
        hrow = sb("h_row", [128, 2, GRID, D])
        hn = sb("h_normalised", [128, 2, 4, D])
        bn6 = sb("bn_stats", [128, 2, GRID, 6])
        mv = sb("mean_var", [128, 2, GRID, 2])
        ve = sb("var_eps", [128, 4])
        rs = sb("rstd", [128, 2, GRID])
        mhalf = sb("minus_half", [128, 4])
        eps = sb("eps", [128, 4])
        acc, tp = kept.banks[0:4], kept.banks[4:6]

        s_wgd, s_wga, s_tok = sem("weights_scaled_dve"), sem("weights_scaled_act"), sem("token_products")
        s_h, s_hst = sem("h_ready"), [sem(f"h_stored{i}") for i in range(2)]
        s_bn, s_mv, s_ve, s_rs = sem("bn_stats_done"), sem("mean_var_ready"), sem("var_eps_ready"), sem("rstd_ready")
        s_hn, s_tp, s_hnT, s_mh = sem("hn_ready"), sem("hn_transposed"), sem("hnT_written"), sem("mhalf_set")

        hnT_t = hnT[:, :].rearrange("p (b t) -> p t b", t=TOKENS)
        RD = GRID * D

        def rows(eng, row):
            row(0, 0)
            with eng.Fori(0, (GRID - 1) // ROW_UNROLL) as i:
                for j in range(1, ROW_UNROLL + 1):
                    row(i, j)

        def lagged(i, j, g, lag):
            n = GROUPS * j + g - lag
            return None if n < 0 else (i, n // GROUPS, n % GROUPS)

        def drained(step, lag):
            i, j = (GRID - 1) // ROW_UNROLL - 1, ROW_UNROLL
            for n in range(lag):
                step(*lagged(i, j + 1, n, lag))

        def weights_free(eng, i, j, pj):
            before = GRID if pj == GRID - 1 else 4 if pj < 3 else 3
            if GRID * j + pj - before >= 0:
                eng.wait_ge(s_tok, GRID * (ROW_UNROLL * i + j) + pj - before + 1)

        def slot(pj):
            return 3 if pj == GRID - 1 else pj % 3

        with nc.Block() as block:
            @block.sync
            def _(sp):
                def store(pi, j):
                    sp.wait_ge(s_h, GROUPS * (pi + 1))
                    sp.dma_start(kept.h[:, bass.ds(pi * RD, RD)],
                                 hrow[:, j % 2, :, :].rearrange("p t d -> p (t d)")).then_inc(s_hst[j % 2], 16)

                def refill(i, j, last):
                    pi = ROW_UNROLL * i + j
                    sp.wait_ge(s_tok, GRID * pi)
                    if not last or pi + 1 < GRID:
                        rows_in.load_xa(sp, pi + 1, j + 1)
                        rows_in.load_parts(sp, pi + 1, j + 1)
                    if not last or pi + 3 < GRID + 1:
                        rows_in.load_xo(sp, pi + 3, j + 3)
                    store(pi - 1, j - 1)

                with sp.Fori(0, 2) as i:
                    for j in range(1, ROW_UNROLL + 1):
                        refill(i, j, False)
                for j in range(1, ROW_UNROLL + 1):
                    refill(2, j, True)
                store(GRID - 1, 0)
                sp.wait_ge(s_hst[0], 16 * 7)
                sp.wait_ge(s_hst[1], 16 * 6)

            @block.scalar
            def _(act):
                def evacuate(i, j, g):
                    q, t = GROUPS * (ROW_UNROLL * i + j) + g, GRID * (ROW_UNROLL * i + j)
                    n = GROUP_N[g]
                    act.wait_ge(s_tok, t + GROUP_AT[g] + n)
                    nc.scalar.activation(hrow[:, j % 2, GROUP_AT[g]:GROUP_AT[g] + n, :].rearrange("p t d -> p (t d)"),
                                         acc[g][:, 0:n * D], ACT.Copy, scale=tok["rstd"][:, 0:1]).then_inc(s_h, 1)

                def write_hnT(i, j, g):
                    q, t = GROUPS * (ROW_UNROLL * i + j) + g, GRID * (ROW_UNROLL * i + j)
                    n = GROUP_N[g]
                    act.wait_ge(s_tp, q + 1)
                    nc.scalar.activation(hnT_t[:, bass.ds(t + GROUP_AT[g], n), :],
                                         tp[g % 2][:, 0:n * D].rearrange("p (t b) -> p t b", t=n),
                                         ACT.Copy).then_inc(s_hnT, 1)

                def row(i, j):
                    for g in range(GROUPS):
                        for pj in range(GROUP_AT[g], GROUP_AT[g] + GROUP_N[g]):
                            weights_free(act, i, j, pj)
                            t = GRID * (ROW_UNROLL * i + j) + pj
                            for v in (3, 4):
                                last = nc.scalar.activation(wg[:, slot(pj), v, :], tok["w"][:, v, :], ACT.Copy,
                                                            scale=tok["gamma"][:, bass.ds(t, 1), v])
                            last.then_inc(s_wga, 1)
                        if g == GROUPS - 1 and j > 0:
                            pi = ROW_UNROLL * i + j
                            act.wait_ge(s_hst[(j - 1) % 2], 16 * (2 * i + (j - 1) // 2 + 1))
                            act.wait_ge(s_hn, GROUPS * pi)
                        if (at := lagged(i, j, g, 1)) is not None:
                            evacuate(*at)
                        if (at := lagged(i, j, g, 4)) is not None:
                            write_hnT(*at)

                rows(act, row)
                last_i, last_j = (GRID - 1) // ROW_UNROLL - 1, ROW_UNROLL
                evacuate(last_i, last_j, GROUPS - 1)
                drained(write_hnT, 4)

            @block.vector
            def _(dve):
                nc.vector.memset(mhalf[:, :], -0.5).then_inc(s_mh, 1)
                nc.vector.memset(eps[:, :], LN_EPS).then_inc(s_mh, 1)

                def statistics(i, j, g):
                    q, t = GROUPS * (ROW_UNROLL * i + j) + g, GRID * (ROW_UNROLL * i + j)
                    dve.wait_ge(s_h, q + 1)
                    for pj in range(GROUP_AT[g], GROUP_AT[g] + GROUP_N[g]):
                        last = nc.vector.bn_stats(bn6[:, j % 2, pj, :], hrow[:, j % 2, pj, :])
                    last.then_inc(s_bn, 1)

                def aggregate(i, j, g):
                    q = GROUPS * (ROW_UNROLL * i + j) + g
                    own_wait(dve, s_bn, q + 1, s_mh)
                    for pj in range(GROUP_AT[g], GROUP_AT[g] + GROUP_N[g]):
                        last = nc.vector.bn_aggr(mv[:, j % 2, pj, :], bn6[:, j % 2, pj, :])
                    last.then_inc(s_mv, 1)

                def normalise(i, j, g):
                    q = GROUPS * (ROW_UNROLL * i + j) + g
                    dve.wait_ge(s_rs, q + 1)
                    if GROUPS * j + g >= 2:
                        dve.wait_ge(s_tp, q - 1)
                    for n in range(GROUP_N[g]):
                        pj = GROUP_AT[g] + n
                        last = nc.vector.tensor_scalar(hn[:, g % 2, n, :], hrow[:, j % 2, pj, :],
                                                       mv[:, j % 2, pj, 0:1], rs[:, j % 2, pj:pj + 1],
                                                       ALU.subtract, ALU.mult)
                    last.then_inc(s_hn, 1)

                def row(i, j):
                    for g in range(GROUPS):
                        for pj in range(GROUP_AT[g], GROUP_AT[g] + GROUP_N[g]):
                            weights_free(dve, i, j, pj)
                            t = GRID * (ROW_UNROLL * i + j) + pj
                            for v in range(3):
                                last = nc.vector.tensor_scalar(wg[:, slot(pj), v, :], tok["w"][:, v, :],
                                                               tok["gamma"][:, bass.ds(t, 1), v], None, ALU.mult)
                            last.then_inc(s_wgd, 1)
                        if g == GROUPS - 1 and j > 0:
                            dve.wait_ge(s_hn, GROUPS * (ROW_UNROLL * i + j))
                        if (at := lagged(i, j, g, 1)) is not None:
                            statistics(*at)
                        if (at := lagged(i, j, g, 2)) is not None:
                            normalise(*at)
                        if (at := lagged(i, j, g, 1)) is not None:
                            aggregate(*at)

                rows(dve, row)
                last_i, last_j = (GRID - 1) // ROW_UNROLL - 1, ROW_UNROLL
                statistics(last_i, last_j, GROUPS - 1)
                aggregate(last_i, last_j, GROUPS - 1)
                drained(normalise, 2)

            @block.gpsimd
            def _(pool):
                pool.wait_ge(s_mh, 2)

                def row(i, j):
                    for g in range(GROUPS):
                        q = GROUPS * (ROW_UNROLL * i + j) + g
                        pj, n = GROUP_AT[g], GROUP_N[g]
                        pool.wait_ge(s_mv, q + 1)
                        if GROUPS * j + g > 0:
                            pool.wait_ge(s_rs, q)
                        nc.gpsimd.tensor_tensor(ve[:, 0:n], mv[:, j % 2, pj:pj + n, 1], eps[:, 0:n], ALU.add)\
                            .then_inc(s_ve, 1)
                        pool.wait_ge(s_ve, q + 1)
                        nc.gpsimd.tensor_tensor(rs[:, j % 2, pj:pj + n], ve[:, 0:n], mhalf[:, 0:n], ALU.pow)\
                            .then_inc(s_rs, 1)

                rows(pool, row)

            @block.tensor
            def _(pe):
                def transposes(i, j, g):
                    q = GROUPS * (ROW_UNROLL * i + j) + g
                    pe.wait_ge(s_hn, q + 1)
                    if GROUPS * j + g >= 2:
                        pe.wait_ge(s_hnT, q - 1)
                    for n in range(GROUP_N[g]):
                        last = nc.tensor.transpose(tp[g % 2][:, n * D:(n + 1) * D], hn[:, g % 2, n, :],
                                                   kept.col(C_ID, 128))
                    last.then_inc(s_tp, 1)

                def row(i, j):
                    pi = ROW_UNROLL * i + j
                    pe.wait_ge(s_xa[j % 2], 16 * (2 * i + j // 2 + 1))
                    pe.wait_ge(s_gb[j % 2], 16 * (2 * i + j // 2 + 1))
                    pe.wait_ge(s_xo[j % 4], 16 * (i + j // 4 + 1))
                    pe.wait_ge(s_xo[(j + 1) % 4], 16 * (i + (j + 1) // 4 + 1))
                    for g in range(GROUPS):
                        if j > 0:
                            pe.wait_ge(s_h, GROUPS * pi + g - 3)
                        lo, hi = GROUP_AT[g] * D, (GROUP_AT[g] + GROUP_N[g]) * D
                        nc.tensor.matmul(acc[g][:, 0:hi - lo], tok["stT"][:, :], gbr[:, j % 2, lo:hi],
                                         start=True, stop=False)
                        for n in range(GROUP_N[g]):
                            pj = GROUP_AT[g] + n
                            o = acc[g][:, n * D:(n + 1) * D]
                            pe.wait_ge(s_wgd, GRID * pi + pj + 1)
                            for v in range(VARIANTS):
                                if v == 3:
                                    pe.wait_ge(s_wga, GRID * pi + pj + 1)
                                if v == 0:
                                    patch = xa[:, j % 2, pj * IMAGES:(pj + 1) * IMAGES]
                                else:
                                    up, left = v <= 2, v in (1, 3)
                                    r, c = (j + up) % 4, pj + (not left)
                                    patch = xo[:, r, c * IMAGES:(c + 1) * IMAGES]
                                last = nc.tensor.matmul(o, patch, wg[:, slot(pj), v, :], start=False,
                                                        stop=v == VARIANTS - 1 and n == GROUP_N[g] - 1)
                            last.then_inc(s_tok, 1)
                        if (at := lagged(i, j, g, 3)) is not None:
                            transposes(*at)

                rows(pe, row)
                drained(transposes, 3)


def attention(nc, kept, hnT, ffn, plan, a):
    with ExitStack() as ctx:
        def sb(name, shape, dt=F32):
            return ctx.enter_context(nc.sbuf_tensor("attn_" + name, shape, dt))

        def sem(name):
            return nc.alloc_semaphore("attn_" + name)

        RING = 8
        upper_bf = sb("upper_bf", [128, 128], BF16)
        ones_bf = sb("ones_bf", [128, 128], BF16)
        tri_bf = sb("tri_bf", [128, 128 + 64], BF16)
        x2 = sb("x_pair", [128, 2, PAIR])
        tqk = sb("tanh_qk", [128, 2, 2, PAIR])
        qk = sb("sigmoid_qk", [128, 2, 2, PAIR])
        v1 = sb("tanh_v_and_twos", [128, 2, 3, D + 1])
        e = sb("exp_scores", [128, 2, PAIR + TAIL])
        hin = sb("h_in", [128, 2, 3, D])
        den = sb("denominators", [128, 2, 3])
        pay = sb("payload", [128, RING, 3, PAY])
        bn6 = sb("bn_stats2", [128, 3, 6])
        ve = sb("var_eps2", [128, 3])
        mhalf = sb("minus_half2", [128, 3])
        eps, ring_tokens = sb("eps", [128, 3]), sb("ring_tokens", [128, 3], I32)
        shift = sb("minus_mean_by_deviation", [128, 3])
        xn = sb("x_normalised", [128, 2, 3, D])
        xT = sb("x_transposed", [128, 2, 3, D])
        lb, d = sb("logits", [128, 3, EXPERTS]), sb("logits_less_max", [128, 3, EXPERTS])
        w, m, m2 = sb("tie_order", [128, 3, EXPERTS]), sb("max_logit", [128, 3]), sb("first_max", [128, 3])
        oh = sb("one_hot", [128, 2, 3, EXPERTS], BF16)
        ex = sb("exp_logits", [128, 2, 3, EXPERTS])
        se, rr, rro, pos = (sb("sum_exp", [128, 2, 3]), sb("ranks", [128, 3, EXPERTS]),
                            sb("own_rank", [128, 3, EXPERTS]), sb("position", [128, 3]))
        idx = sb("row_index", [128, RING, 3], I32)
        w_ffn = sb("w_ffn_f32", [128, 4, EXPERTS * D])
        b2 = w_ffn[0:96, 1:4, :]
        b2_mid = sb("b2_middle", [96, EXPERTS * D], BF16)
        qk_ps = kept.banks[0:2]
        v_ps, s_ps, o_ps, t_ps, lg_ps, rk_ps = kept.banks[2:8]
        N = [HEAD, HEAD, 128]

        s_init, s_x2, s_qkps, s_tqk, s_qk = sem("a_init"), sem("x2"), sem("qk_ps"), sem("tanh_qk"), sem("qk")
        s_vps, s_v = sem("v_ps"), sem("tanh_v")
        s_sps, s_e, s_ops = sem("scores_ps"), sem("exp_scores"), sem("o_ps")
        s_hin = [sem(f"h_in{i}") for i in range(2)]
        s_h2, s_bn, s_mv, s_pool, s_rs = sem("h2"), sem("bn2"), sem("mv2"), sem("pool_step2"), sem("rstd2")
        s_xn, s_tps, s_xT, s_lg = sem("xn2"), sem("xT_ps"), sem("xT"), sem("logits_ps")
        s_choice, s_place, s_placed = sem("choice_step"), sem("place_step"), sem("placed")
        s_shift, s_ex, s_rk = sem("shift"), sem("exp_logits"), sem("ranks_ps")
        s_b2, s_b2_step = sem("b2_loaded"), sem("b2_step")
        s_den, s_w_hi, s_w_lo = sem("den_step"), sem("w_hi"), sem("w_lo")
        s_w = [sem(f"w_part_loaded{i}") for i in range(4)]
        s_sc = [sem(f"scattered{i}") for i in range(RING)]
        INITS = 19 - 4 + RING
        CHOICE, PLACE = 6, 5

        LAST = 6
        PEEL, UNROLL = 12, RING
        LOOPS = (PAIRS - PEEL) // UNROLL
        W_STEP = 4

        def w_part(j):
            n = j - W_STEP
            if not 0 <= n < 2 * FC or j >= PEEL:
                return None
            names, c = ("w2_hi", "w2_lo") if n >= FC else ("w1_hi", "w1_lo"), n % FC
            return w_ffn[:, n % 4, :], ffn[names[0]][c][:, :], ffn[names[1]][c][:, :], n

        def steps(eng, step):
            for n in range(PEEL):
                step(0, n, lambda lag, n=n: n >= lag)
            with eng.Fori(0, LOOPS) as i:
                for j in range(PEEL, PEEL + UNROLL):
                    step(i, j, lambda lag: True)
            for n in range(PEEL + UNROLL * LOOPS, PAIRS + LAST):
                step(LOOPS, n - UNROLL * LOOPS, lambda lag, n=n: n - lag < PAIRS)

        with nc.Block() as block:
            @block.sync
            def _(sp):
                def load(i, j):
                    p = RING * i + j
                    if j >= 2:
                        sp.wait_ge(s_h2, p - 1)
                    h = kept.h
                    sp.dma_start(hin[0:HEAD, j % 2, 0:2, :], h[bass.ds(2 * p, 2), 0:HEAD * D]
                                 .rearrange("b (t e) -> t b e", e=D)).then_inc(s_hin[j % 2], 16)
                    for k in range(2):
                        sp.dma_start(hin[TAIL * k:TAIL * (k + 1), j % 2, 2, :], h[bass.ds(2 * p + k, 1), HEAD * D:]
                                     .rearrange("b (t e) -> (b t) e", e=D)).then_inc(s_hin[j % 2], 16)

                def step(i, j, live):
                    for n in {2: [0], 4: [1, 2, 3], 6: [4], 7: [5], 8: [6], 9: [7]}.get(j, []):
                        if 1 <= n < 4:
                            sp.wait_ge(s_b2_step, 7)
                        if n >= 4:
                            sp.wait_ge(s_w_lo, n - 3)
                        w, c = a["w2" if n >= FC else "w1"], n % FC
                        sp.dma_start(w_ffn[:, n % 4, :], w[:, c * EXPERTS * D:(c + 1) * EXPERTS * D])\
                            .then_inc(s_w[n % 4], 16)
                    if live(0):
                        load(i, j)
                    if j == 0:
                        sp.dma_start(b2[:, 0, :], a["b2"].broadcast_to([96, EXPERTS * D])).then_inc(s_b2, 16)

                steps(sp, step)
                plan.sync(sp)

            @block.gpsimd
            def _(pool):
                pool.wait_ge(s_init, INITS)
                last_row = pool.to_reg(DUMMY - 1)

                def rstd(i, j):
                    p = RING * i + j
                    pool.wait_ge(s_mv, p + 1)
                    o = pay[:, j % RING, :, :]
                    if j >= 1:
                        pool.wait_ge(s_rs, p)
                    nc.gpsimd.tensor_tensor(ve[:, :], o[:, :, D + 1], eps[:, :], ALU.add).then_inc(s_pool, 1)
                    if j >= RING:
                        number = o[:, :, D + 3].bitcast(I32)
                        nc.gpsimd.tensor_tensor(number, number, ring_tokens[:, :], ALU.add)
                    pool.wait_ge(s_pool, p + 1)
                    nc.gpsimd.tensor_tensor(o[:, :, D + 1], ve[:, :], mhalf[:, :], ALU.pow).then_inc(s_rs, 1)

                def scatter(i, j):
                    p = RING * i + j
                    own_wait(pool, s_placed, p + 1, s_init)
                    for k in range(3):
                        n = N[k]
                        nc.gpsimd.indirect_dma_start(
                            out=kept.by_expert[:, :],
                            out_offset=bass.IndirectOffsetOnAxis(ap=idx[0:n, j % RING, k:k + 1], axis=0),
                            in_=pay[0:n, j % RING, k, :], in_offset=None,
                            bounds_check=last_row, oob_is_err=False).then_inc(s_sc[j % RING], 16)

                def step(i, j, live):
                    if live(3):
                        rstd(i, j - 3)
                    if live(6):
                        scatter(i, j - 6)

                steps(pool, step)
                for scattered in s_sc:
                    pool.wait_ge(scattered, 48 * (PAIRS // RING))

            @block.scalar
            def _(act):
                nc.scalar.preload_act_table(ACT.Exp)
                act.wait_ge(s_init, INITS)

                def copy_x(i, j):
                    if j >= 2:
                        act.wait_ge(s_vps, RING * i + j - 1)
                    nc.scalar.activation(x2[:, j % 2, :], hnT[:, bass.ds((RING * i + j) * PAIR, PAIR)], ACT.Copy)\
                        .then_inc(s_x2, 1)

                def tanh_qk(i, j):
                    p = RING * i + j
                    act.wait_ge(s_qkps, p + 1)
                    if j >= 2:
                        act.wait_ge(s_qk, p - 1)
                    for k in range(2):
                        last = nc.scalar.activation(tqk[:, j % 2, k, :], qk_ps[k][:, 0:PAIR], ACT.Tanh, scale=0.5)
                    last.then_inc(s_tqk, 1)

                def tanh_v(i, j):
                    p = RING * i + j
                    act.wait_ge(s_vps, p + 1)
                    if j >= 2:
                        act.wait_ge(s_ops, p - 1)
                    nc.scalar.activation(v1[:, j % 2, :, 0:D], v_ps[:, 0:3 * D].rearrange("p (k e) -> p k e", k=3),
                                         ACT.Tanh, scale=0.5).then_inc(s_v, 1)

                def exp_scores(i, j):
                    p = RING * i + j
                    act.wait_ge(s_sps, p + 1)
                    if j >= 2:
                        act.wait_ge(s_ops, p - 1)
                    nc.scalar.activation(e[:, j % 2, :], s_ps[:, 0:PAIR + TAIL], ACT.Exp, scale=SCORE_SCALE)\
                        .then_inc(s_e, 1)

                def normalise(i, j):
                    p = RING * i + j
                    act.wait_ge(s_shift, p + 1)
                    if j >= 2:
                        act.wait_ge(s_tps, p - 1)
                    for k in range(3):
                        n = N[k]
                        last = nc.scalar.activation(xn[0:n, j % 2, k, :], pay[0:n, j % RING, k, 0:D], ACT.Identity,
                                                    bias=shift[0:n, k:k + 1],
                                                    scale=pay[0:n, j % RING, k, D + 1:D + 2])
                    last.then_inc(s_xn, 1)

                def copy_xT(i, j):
                    p = RING * i + j
                    act.wait_ge(s_tps, p + 1)
                    if j >= 2:
                        act.wait_ge(s_lg, p - 1)
                    nc.scalar.activation(xT[:, j % 2, :, :].rearrange("p k e -> p (k e)"), t_ps[:, 0:3 * D],
                                         ACT.Copy).then_inc(s_xT, 1)

                def exp_logits(i, j):
                    p = RING * i + j
                    act.wait_ge(s_choice, CHOICE * p + 3)
                    nc.scalar.activation(ex[:, j % 2, :, :], d[:, :, :], ACT.Exp).then_inc(s_ex, 1)

                def step(i, j, live):
                    if live(4):
                        copy_xT(i, j - 4)
                    if live(0):
                        copy_x(i, j)
                    if live(1):
                        tanh_qk(i, j - 1)
                    if live(3):
                        normalise(i, j - 3)
                    if live(4):
                        exp_logits(i, j - 4)
                    if live(1):
                        tanh_v(i, j - 1)
                        exp_scores(i, j - 1)
                    if (part := w_part(j)) is not None:
                        whole, hi, lo, n = part
                        act.wait_ge(s_w[n % 4], 16 * (n // 4 + 1))
                        nc.scalar.activation(hi, whole, ACT.Copy, scale=W_SCALE).then_inc(s_w_hi, 1)

                steps(act, step)
                plan.scalar(act)

            @block.vector
            def _(dve):
                inits = [
                    nc.vector.tensor_copy(upper_bf[:, :], kept.col(C_UP, 128)),
                    nc.vector.memset(ones_bf[:, :], 1.0),
                    nc.vector.memset(kept.share[:, :], 1.0 / 32),
                    nc.vector.tensor_copy(tri_bf[:, :], kept.col(C_TRI, 128 + 64)),
                    nc.vector.memset(v1[:, :, :, D:D + 1], 2.0),
                    nc.vector.memset(mhalf[:, :], -0.5),
                    nc.vector.memset(pay[:, :, :, D:D + 2], 1.0),
                    *[nc.vector.tensor_scalar(pay[:, r, :, D + 3].bitcast(I32), kept.col(C_ID0, 3), float(r * PAIR),
                                              None, ALU.add) for r in range(RING)],
                    nc.vector.tensor_copy(kept.run[0][:, :], kept.col(C_RUN0, EXPERTS)),
                    nc.vector.memset(v_ps[96:128, 0:2 * D], 0.0),
                    nc.vector.memset(s_ps[96:128, 0:PAIR], 0.0),
                    nc.vector.memset(o_ps[96:128, 0:2 * (D + 1)], 0.0),
                    nc.vector.memset(t_ps[:, 0:2 * D].rearrange("p (k e) -> p k e", k=2)[:, :, HEAD:D], 0.0),
                    nc.vector.memset(lg_ps[96:128, 0:2 * EXPERTS], 0.0),
                    nc.vector.memset(eps[:, :], LN_EPS),
                    nc.vector.memset(ring_tokens[:, :], RING * PAIR),
                ]
                assert len(inits) == INITS
                for ins in inits:
                    ins.then_inc(s_init, 1)
                dve.wait_ge(s_init, INITS)

                def split_b2(j):
                    whole, rest, rest2 = (b2[:, n, :] for n in range(3))
                    if j == 1:
                        dve.wait_ge(s_b2, 16)
                        nc.vector.tensor_scalar(whole, whole, W_SCALE, None, ALU.mult).then_inc(s_b2_step, 1)
                        dve.wait_ge(s_b2_step, 1)
                        nc.vector.tensor_copy(kept.b2[:, :], whole).then_inc(s_b2_step, 1)
                    if j == 2:
                        dve.wait_ge(s_b2_step, 2)
                        nc.vector.tensor_tensor(rest, whole, kept.b2[:, :], ALU.subtract).then_inc(s_b2_step, 1)
                        dve.wait_ge(s_b2_step, 3)
                        nc.vector.tensor_copy(b2_mid[:, :], rest).then_inc(s_b2_step, 1)
                    if j == 3:
                        dve.wait_ge(s_b2_step, 4)
                        nc.vector.tensor_tensor(rest2, rest, b2_mid[:, :], ALU.subtract).then_inc(s_b2_step, 1)
                        dve.wait_ge(s_b2_step, 5)
                        nc.vector.tensor_copy(kept.b2[32:64, :], b2_mid[32:64, :]).then_inc(s_b2_step, 1)
                        nc.vector.tensor_copy(kept.b2[64:96, :], b2[64:96, 2, :]).then_inc(s_b2_step, 1)

                def plus_one_qk(i, j):
                    p = RING * i + j
                    dve.wait_ge(s_tqk, p + 1)
                    if j >= 2:
                        dve.wait_ge(s_sps, p - 1)
                    nc.vector.tensor_scalar(qk[:, j % 2, :, :], tqk[:, j % 2, :, :], 1.0, None, ALU.add)\
                        .then_inc(s_qk, 1)

                def aggregate(i, j):
                    own_wait(dve, s_bn, RING * i + j + 1, s_init)
                    for k in range(3):
                        last = nc.vector.bn_aggr(pay[0:N[k], j % RING, k, D:D + 2], bn6[0:N[k], k, :])
                    last.then_inc(s_mv, 1)

                def shifts(i, j):
                    p = RING * i + j
                    dve.wait_ge(s_rs, p + 1)
                    if j >= 1:
                        dve.wait_ge(s_xn, p)
                    o = pay[:, j % RING, :, :]
                    nc.vector.scalar_tensor_tensor(out=shift[:, :], in0=o[:, :, D], scalar=-1.0, in1=o[:, :, D + 1],
                                                   op0=ALU.mult, op1=ALU.mult).then_inc(s_shift, 1)

                def over_tiles(t):
                    return t[:, :].unsqueeze(1).broadcast_to([128, 3, EXPERTS])

                def over_experts(t):
                    return t[:, :].unsqueeze(2).broadcast_to([128, 3, EXPERTS])

                def place(i, j):
                    p = RING * i + j
                    done = PLACE * p
                    rk = rk_ps[:, 0:3 * EXPERTS].rearrange("p (k e) -> p k e", k=3)
                    run, run_next = kept.run[j % 2], kept.run[(j + 1) % 2]
                    dve.wait_ge(s_rk, p + 1)
                    if j >= 1:
                        dve.wait_ge(s_placed, p)
                    nc.vector.tensor_tensor(rr[:, :, :], rk, over_tiles(run), ALU.add).then_inc(s_place, 1)
                    dve.wait_ge(s_ex, p + 1)
                    nc.vector.tensor_reduce(se[:, 0, :], ex[:, j % 2, :, :], AX.X, ALU.add).then_inc(s_place, 1)
                    dve.wait_ge(s_place, done + 1)
                    nc.vector.tensor_tensor(rro[:, :, :], rr[:, :, :], oh[:, j % 2, :, :], ALU.mult)\
                        .then_inc(s_place, 1)
                    dve.wait_ge(s_place, done + 2)
                    nc.vector.tensor_scalar(se[:, 1, :], se[:, 0, :], W_SCALE, None, ALU.mult).then_inc(s_place, 1)
                    dve.wait_ge(s_place, done + 3)
                    nc.vector.tensor_reduce(pos[:, :], rro[:, :, :], AX.X, ALU.add).then_inc(s_place, 1)
                    nc.vector.tensor_tensor(run_next[:, :], run[:, :], rk_ps[:, 24:32], ALU.add)
                    dve.wait_ge(s_place, done + 4)
                    nc.vector.reciprocal(pay[:, j % RING, :, D + 2], se[:, 1, :])
                    dve.wait_ge(s_place, done + 5)
                    nc.vector.tensor_copy(idx[:, j % RING, :], pos[:, :]).then_inc(s_placed, 1)

                def step(i, j, live):
                    choosing, attended = live(4), live(2)
                    c, b = j - 4, j - 2
                    chosen, den_steps = CHOICE * (RING * i + c), 2 * (RING * i + b)
                    o = o_ps[:, 0:3 * (D + 1)].rearrange("p (k e) -> p k e", k=3)
                    lg = lg_ps[:, 0:3 * EXPERTS].rearrange("p (k e) -> p k e", k=3)
                    desc = kept.col(C_DESC, EXPERTS).unsqueeze(1).broadcast_to([128, 3, EXPERTS])

                    if live(5):
                        place(i, j - 5)
                    if live(3):
                        shifts(i, j - 3)
                    if choosing:
                        dve.wait_ge(s_lg, RING * i + c + 1)
                        nc.vector.tensor_tensor(lb[:, :, :], lg, over_tiles(kept.b_s), ALU.add).then_inc(s_choice, 1)
                        dve.wait_ge(s_choice, chosen + 1)
                        nc.vector.tensor_reduce(m[:, :], lb[:, :, :], AX.X, ALU.max).then_inc(s_choice, 1)
                    if live(1):
                        plus_one_qk(i, j - 1)
                    if choosing:
                        dve.wait_ge(s_choice, chosen + 2)
                        if c >= 1:
                            dve.wait_ge(s_ex, RING * i + c)
                        nc.vector.tensor_tensor(d[:, :, :], lb[:, :, :], over_experts(m), ALU.subtract)\
                            .then_inc(s_choice, 1)
                    if attended:
                        dve.wait_ge(s_ops, RING * i + b + 1)
                        nc.vector.tensor_scalar(den[:, 0, :], o[:, :, D], 1e-30, None, ALU.max).then_inc(s_den, 1)
                    if choosing:
                        dve.wait_ge(s_choice, chosen + 3)
                        nc.vector.scalar_tensor_tensor(out=w[:, :, :], in0=d[:, :, :], scalar=0.0, in1=desc,
                                                       op0=ALU.is_equal, op1=ALU.mult).then_inc(s_choice, 1)
                    if attended:
                        dve.wait_ge(s_den, den_steps + 1)
                        nc.vector.reciprocal(den[:, 1, :], den[:, 0, :]).then_inc(s_den, 1)
                    if choosing:
                        dve.wait_ge(s_choice, chosen + 4)
                        nc.vector.tensor_reduce(m2[:, :], w[:, :, :], AX.X, ALU.max).then_inc(s_choice, 1)
                    if attended:
                        dve.wait_ge(s_den, den_steps + 2)
                        dve.wait_ge(s_hin[b % 2], 48 * (RING // 2 * i + b // 2 + 1))
                        if b >= RING:
                            dve.wait_ge(s_sc[b % RING], 48 * (i + b // RING))
                        for k in range(3):
                            last = nc.vector.scalar_tensor_tensor(
                                out=pay[0:N[k], b % RING, k, 0:D], in0=o[0:N[k], k, 0:D],
                                scalar=den[0:N[k], 1, k:k + 1], in1=hin[0:N[k], b % 2, k, :],
                                op0=ALU.mult, op1=ALU.add)
                        last.then_inc(s_h2, 1)
                    if choosing:
                        dve.wait_ge(s_choice, chosen + 5)
                        if c >= 2:
                            dve.wait_ge(s_rk, RING * i + c - 1)
                        nc.vector.tensor_tensor(oh[:, c % 2, :, :], w[:, :, :], over_experts(m2), ALU.is_equal)\
                            .then_inc(s_choice, 1)
                    if attended:
                        dve.wait_ge(s_h2, RING * i + b + 1)
                        for k in range(3):
                            last = nc.vector.bn_stats(bn6[0:N[k], k, :], pay[0:N[k], b % RING, k, 0:D])
                        last.then_inc(s_bn, 1)
                        aggregate(i, b)
                    if j < PEEL:
                        split_b2(j)
                    if (part := w_part(j)) is not None:
                        whole, hi, lo, n = part
                        dve.wait_ge(s_w_hi, n + 1)
                        nc.vector.scalar_tensor_tensor(out=lo, in0=whole, scalar=W_SCALE, in1=hi, op0=ALU.mult,
                                                       op1=ALU.subtract).then_inc(s_w_lo, 1)

                steps(dve, step)
                dve.wait_ge(s_placed, PAIRS)
                plan.vector(dve)

            @block.tensor
            def _(pe):
                pe.wait_ge(s_init, INITS)

                def queries_keys(i, j):
                    p = RING * i + j
                    pe.wait_ge(s_x2, p + 1)
                    if j >= 1:
                        pe.wait_ge(s_tqk, p)
                    for k in range(2):
                        last = nc.tensor.matmul(qk_ps[k][:, 0:PAIR], kept.w_qkv[:, k, :], x2[:, j % 2, :],
                                                start=True, stop=True)
                    last.then_inc(s_qkps, 1)

                def values(i, j):
                    if j >= 1:
                        pe.wait_ge(s_v, RING * i + j)
                    for k in range(2):
                        at = k * TOKENS
                        nc.tensor.matmul(v_ps[0:HEAD, k * D:(k + 1) * D], x2[:, j % 2, at:at + HEAD],
                                         kept.w_qkv[:, 2, :], start=True, stop=True)
                        last = nc.tensor.matmul(v_ps[TAIL * k:TAIL * (k + 1), 2 * D:3 * D],
                                                x2[:, j % 2, at + HEAD:at + TOKENS], kept.w_qkv[:, 2, :],
                                                start=True, stop=True)
                    last.then_inc(s_vps, 1)

                def scores(i, j):
                    p = RING * i + j
                    pe.wait_ge(s_qk, p + 1)
                    if j >= 1:
                        pe.wait_ge(s_e, p)
                    for k in range(2):
                        at = k * TOKENS
                        q, key = qk[:, j % 2, 0, :], qk[:, j % 2, 1, :]
                        nc.tensor.matmul(s_ps[0:HEAD, at:at + TOKENS], key[:, at:at + HEAD], q[:, at:at + TOKENS],
                                         start=True, stop=False)
                        nc.tensor.matmul(s_ps[0:HEAD, at:at + HEAD], kept.ident_bf[0:HEAD, 0:HEAD],
                                         tri_bf[0:HEAD, 0:HEAD], start=False, stop=True)
                        r = slice(TAIL * k, TAIL * (k + 1))
                        nc.tensor.matmul(s_ps[r, PAIR:PAIR + TAIL], key[:, at + HEAD:at + TOKENS],
                                         q[:, at + HEAD:at + TOKENS], start=True, stop=False)
                        last = nc.tensor.matmul(s_ps[r, PAIR:PAIR + TAIL], kept.ident_bf[r, r], tri_bf[r, 128:192],
                                                start=False, stop=True)
                    last.then_inc(s_sps, 1)

                def attend(i, j):
                    p = RING * i + j
                    pe.wait_ge(s_e, p + 1)
                    pe.wait_ge(s_v, p + 1)
                    if j >= 1:
                        pe.wait_ge(s_h2, p)
                    es, vs = e[:, j % 2, :], v1[:, j % 2, :, :]
                    for k in range(2):
                        at, r = k * TOKENS, slice(TAIL * k, TAIL * (k + 1))
                        nc.tensor.matmul(o_ps[0:HEAD, k * (D + 1):(k + 1) * (D + 1)], es[0:HEAD, at:at + HEAD],
                                         vs[0:HEAD, k, :], start=True, stop=True)
                        o = o_ps[r, 2 * (D + 1):3 * (D + 1)]
                        nc.tensor.matmul(o, es[0:HEAD, at + HEAD:at + TOKENS], vs[0:HEAD, k, :], start=True, stop=False)
                        last = nc.tensor.matmul(o, es[r, PAIR:PAIR + TAIL], vs[r, 2, :], start=False, stop=True)
                    last.then_inc(s_ops, 1)

                def transposes(i, j):
                    p = RING * i + j
                    pe.wait_ge(s_xn, p + 1)
                    if j >= 1:
                        pe.wait_ge(s_xT, p)
                    for k in range(3):
                        n = N[k]
                        last = nc.tensor.transpose(t_ps[:, k * D:k * D + n], xn[0:n, j % 2, k, :],
                                                   kept.const[0:n, C_ID:C_ID + n])
                    last.then_inc(s_tps, 1)

                def logits(i, j):
                    p = RING * i + j
                    pe.wait_ge(s_xT, p + 1)
                    if j >= 1:
                        pe.wait_ge(s_choice, CHOICE * (p - 1) + 1)
                    for k in range(3):
                        last = nc.tensor.matmul(lg_ps[0:N[k], k * EXPERTS:(k + 1) * EXPERTS], xT[:, j % 2, k, 0:N[k]],
                                                kept.w_s[:, :], start=True, stop=True)
                    last.then_inc(s_lg, 1)

                def ranks(i, j):
                    p = RING * i + j
                    pe.wait_ge(s_choice, CHOICE * (p + 1))
                    if j >= 1:
                        pe.wait_ge(s_placed, p)
                    for k in range(3):
                        o = rk_ps[:, k * EXPERTS:(k + 1) * EXPERTS]
                        for before in range(k):
                            nc.tensor.matmul(o, ones_bf[0:N[before], :], oh[0:N[before], j % 2, before, :],
                                             start=before == 0, stop=False)
                        nc.tensor.matmul(o, upper_bf[0:N[k], :], oh[0:N[k], j % 2, k, :], start=k == 0, stop=True)
                    for k in range(3):
                        last = nc.tensor.matmul(rk_ps[:, 24:32], ones_bf[0:N[k], :], oh[0:N[k], j % 2, k, :],
                                                start=k == 0, stop=k == 2)
                    last.then_inc(s_rk, 1)

                def step(i, j, live):
                    if live(1):
                        queries_keys(i, j - 1)
                    if live(4):
                        logits(i, j - 4)
                    if live(2):
                        attend(i, j - 2)
                    if live(1):
                        values(i, j - 1)
                        scores(i, j - 1)
                    if live(3):
                        transposes(i, j - 3)
                    if live(4):
                        ranks(i, j - 4)

                steps(pe, step)
                plan.tensor(pe)


class Plan:

    def __init__(self, nc, ctx, kept, table):
        def sb(name, shape, dt=F32):
            return ctx.enter_context(nc.sbuf_tensor("plan_" + name, shape, dt))

        def sem(name):
            return nc.alloc_semaphore("plan_" + name)

        run_i = sb("run_i", [1, EXPERTS], I32)
        n_i = sb("slots_i", [SLOTS, 2, EXPERTS], I32)
        f = sb("expert_rows", [SLOTS, 5, EXPERTS])
        le = sb("expert_order", [SLOTS, EXPERTS, EXPERTS])
        nle = sb("slots_before", [SLOTS, EXPERTS, EXPERTS])
        ge = sb("slot_past_expert", [SLOTS, EXPERTS])
        gd = sb("slot_jumps", [SLOTS, EXPERTS])
        sl = sb("slot_columns", [SLOTS, 5])
        xs = sb("slot_experts", [1, 4, SLOTS])
        wi = sb("words_i", [1, 3, WORDS], I32)
        row_ps = kept.banks[0]
        pad = sb("padding", [128, 2, PAY])
        s_pad, s_p, s_fill = sem("padding_set"), sem("plan_step"), sem("padding_stored")
        s_col, s_row, s_fill2 = sem("slot_columns"), sem("slot_rows"), sem("padding_stored_act")

        rows = kept.by_expert

        def fill(eng, experts, stored):
            eng.wait_ge(s_p, 1)
            for x in experts:
                at = eng.value_load(run_i[0:1, x:x + 1], min_val=0, max_val=DUMMY - SLOT)
                eng.dma_start(rows[bass.ds(at, SLOT), :].rearrange("(p k) c -> p k c", k=2), pad[:, :, :])\
                    .then_inc(stored, 16)

        def sync(sp):
            sp.wait_ge(s_pad, 2)
            sp.dma_start(rows[DUMMY:DUMMY + SLOT, :].rearrange("(p k) c -> p k c", k=2), pad[:, :, :])\
                .then_inc(s_fill, 16)
            fill(sp, range(EXPERTS // 2), s_fill)
            sp.wait_ge(s_fill, 16 * (EXPERTS // 2 + 1))

        def scalar(act):
            act.wait_ge(s_pad, 2)
            fill(act, range(EXPERTS // 2, EXPERTS), s_fill2)
            act.wait_ge(s_fill2, 16 * (EXPERTS // 2))

        def tensor(pe):
            pe.wait_ge(s_col, 1)
            for n, col in enumerate((1, 4)):
                last = nc.tensor.matmul(row_ps[0:1, n * SLOTS:(n + 1) * SLOTS], sl[:, col:col + 1],
                                        kept.const[0:SLOTS, C_ID:C_ID + SLOTS], start=True, stop=True)
            last.then_inc(s_row, 1)

        def vector(dve):
            nc.vector.memset(pad[:, :, 0:D + 3], 0.0).then_inc(s_pad, 1)
            nc.vector.memset(pad[:, :, D + 3:PAY].bitcast(I32), NOBODY).then_inc(s_pad, 1)
            count = 0

            def link(ins):
                nonlocal count
                count += 1
                ins.then_inc(s_p, 1)
                dve.wait_ge(s_p, count)

            run = kept.run[PAIRS % 2][0:SLOTS, :]
            c = kept.const[0:SLOTS, :]
            desc = c[:, C_DESC:C_DESC + EXPERTS]
            sq = [SLOTS, EXPERTS, EXPERTS]
            link(nc.vector.tensor_copy(run_i[:, :], run[0:1, :]))
            link(nc.vector.tensor_tensor(f[:, 0, :], run, c[:, C_RUN0:C_RUN0 + EXPERTS], ALU.subtract))
            nc.vector.tensor_tensor(le[:, :, :], desc.unsqueeze(1).broadcast_to(sq),
                                    desc.unsqueeze(2).broadcast_to(sq), ALU.is_ge)
            link(nc.vector.tensor_scalar(f[:, 1, :], f[:, 0, :], float(SLOT - 1), None, ALU.add))
            link(nc.vector.tensor_copy(n_i[:, 0, :], f[:, 1, :]))
            link(nc.vector.tensor_scalar(n_i[:, 1, :], n_i[:, 0, :], int(np.log2(SLOT)), None,
                                         ALU.arith_shift_right))
            link(nc.vector.tensor_copy(f[:, 2, :], n_i[:, 1, :]))
            nc.vector.tensor_scalar(f[:, 4, :], f[:, 2, :], -float(SLOT), float(REGION), ALU.mult, ALU.add)
            link(nc.vector.tensor_tensor(nle[:, :, :], le[:, :, :], f[:, 2, :].unsqueeze(1).broadcast_to(sq),
                                         ALU.mult))
            link(nc.vector.tensor_reduce(f[:, 3, :], nle[:, :, :], AX.X, ALU.add))
            s = c[:, C_ID0:C_ID0 + 1]
            link(nc.vector.tensor_tensor(ge[:, :], f[:, 3, :], s.broadcast_to([SLOTS, EXPERTS]), ALU.is_le))
            nc.vector.tensor_reduce(sl[:, 0:1], ge[:, :], AX.X, ALU.add)
            link(nc.vector.tensor_tensor(gd[:, :], ge[:, :], f[:, 4, :], ALU.mult))
            nc.vector.tensor_scalar(sl[:, 1:2], sl[:, 0:1], float(EXPERTS - 1), None, ALU.min)
            link(nc.vector.tensor_reduce(sl[:, 2:3], gd[:, :], AX.X, ALU.add))
            link(nc.vector.scalar_tensor_tensor(out=sl[:, 3:4], in0=s, scalar=float(SLOT), in1=sl[:, 2:3],
                                                op0=ALU.mult, op1=ALU.add))
            nc.vector.tensor_scalar(sl[:, 4:5], sl[:, 3:4], float(DUMMY), None, ALU.min).then_inc(s_col, 1)
            dve.wait_ge(s_row, 1)
            link(nc.vector.tensor_copy(xs[:, 0, :], row_ps[0:1, 0:SLOTS]))
            nc.vector.tensor_copy(table[:, 0:2, :].rearrange("p n s -> p (n s)"), row_ps[0:1, 0:2 * SLOTS])
            for m, n in enumerate((1, 2, 4)):
                width = SLOTS + 1 - 2 * n
                link(nc.vector.scalar_tensor_tensor(out=xs[:, m + 1, 0:width], in0=xs[:, m, n:n + width],
                                                    scalar=float(EXPERTS ** n), in1=xs[:, m, 0:width],
                                                    op0=ALU.mult, op1=ALU.add))
            link(nc.vector.tensor_copy(wi[:, 1, :], xs[:, 1, RUN - 2:RUN - 2 + WORDS]))
            nc.vector.tensor_copy(wi[:, 0, :], xs[:, 3, 0:WORDS])
            link(nc.vector.tensor_scalar(wi[:, 2, :], wi[:, 1, :], 3 * (RUN - 2), None, ALU.logical_shift_left))
            link(nc.vector.tensor_tensor(table[:, 2, 0:WORDS], wi[:, 0, :], wi[:, 2, :], ALU.bitwise_or))

        self.scalar, self.tensor = scalar, tensor
        self.sync, self.vector = sync, vector


def experts(nc, kept, table, ffn, out):
    with ExitStack() as ctx:
        def sb(name, shape, dt=F32):
            return ctx.enter_context(nc.sbuf_tensor("ffn_" + name, shape, dt))

        def sem(name):
            return nc.alloc_semaphore("ffn_" + name)

        pay = sb("rows", [128, SLOT_UNROLL, 2, PAY])
        xn = sb("x_n", [128, 2, 2, D])
        xh = sb("x_hi", [128, 2, SLOT], F16)
        xl = sb("x_lo", [128, 2, SLOT], F16)
        g = sb("gelu", [128, 2, FC, SLOT])
        HALVES = 4
        gh = sb("gelu_hi", [128, HALVES, FC, SLOT], F16)
        gl = sb("gelu_lo", [128, HALVES, FC, SLOT], F16)
        o = sb("out_rows", [128, OUT_RING, 2, D])
        up_ps = [kept.banks[0:2], kept.banks[2:4]]
        down_ps, t_ps = kept.banks[4:6], kept.banks[6:8]

        s_in = [sem(f"rows_loaded{i}") for i in range(SLOT_UNROLL)]
        s_xn, s_t, s_hi, s_lo = sem("x_n"), sem("x_t_ps"), sem("x_hi"), sem("x_lo")
        s_up, s_g, s_ghi, s_glo = sem("up_ps"), sem("gelu"), sem("gelu_hi"), sem("gelu_lo")
        s_down, s_o = sem("down_ps"), sem("out_rows")
        s_st = [sem(f"stored{i}") for i in range(OUT_RING)]

        LAST = 4
        PEEL = OUT_RING + LAST
        LOOPS = (SLOTS - PEEL) // SLOT_UNROLL

        def steps(eng, step, round_begins=lambda i: None):
            for n in range(PEEL):
                step(0, n, lambda lag, n=n: n >= lag)
            with eng.Fori(0, LOOPS) as i:
                round_begins(i)
                for j in range(PEEL, PEEL + SLOT_UNROLL):
                    step(i, j, lambda lag: True)
            for n in range(PEEL + SLOT_UNROLL * LOOPS, SLOTS + LAST):
                step(LOOPS, n - SLOT_UNROLL * LOOPS, lambda lag, n=n: n - lag < SLOTS)

        def stores(i, j):
            return SLOT_UNROLL // OUT_RING * i + j // OUT_RING + 1

        def expert(eng, s):
            return eng.value_load(table[0:1, 0, bass.ds(s, 1)], min_val=0, max_val=EXPERTS - 1)

        with nc.Block() as block:
            @block.sync
            def _(sp):
                def load(i, j):
                    s = SLOT_UNROLL * i + j
                    at = sp.value_load(table[0:1, 1, bass.ds(s, 1)], min_val=0, max_val=DUMMY)
                    if j >= SLOT_UNROLL:
                        sp.wait_ge(s_st[j % OUT_RING], 32 * stores(i, j - SLOT_UNROLL))
                    sp.dma_start(pay[:, j % SLOT_UNROLL, :, :], kept.by_expert[bass.ds(at, SLOT), :]
                                 .rearrange("(k p) c -> p k c", k=2)).then_inc(s_in[j % SLOT_UNROLL], 16)

                for j in range(SLOT_UNROLL):
                    load(0, j)
                with sp.Fori(0, SLOTS // SLOT_UNROLL - 1) as i:
                    for j in range(SLOT_UNROLL, 2 * SLOT_UNROLL):
                        load(i, j)
                for j in range(SLOT_UNROLL, SLOT_UNROLL + SLOTS % SLOT_UNROLL):
                    load(SLOTS // SLOT_UNROLL - 1, j)

            @block.gpsimd
            def _(pool):
                last_row = pool.to_reg(ALL - 1)

                def store(i, j):
                    s = SLOT_UNROLL * i + j
                    own_wait(pool, s_o, s + 1, s_xn)
                    for k in range(2):
                        nc.gpsimd.indirect_dma_start(
                            out=out[:, :], out_offset=bass.IndirectOffsetOnAxis(
                                ap=pay[:, j % SLOT_UNROLL, k, D + 3:D + 4].bitcast(I32), axis=0),
                            in_=o[:, j % OUT_RING, k, :], in_offset=None,
                            bounds_check=last_row, oob_is_err=False).then_inc(s_st[j % OUT_RING], 16)

                steps(pool, lambda i, j, live: live(4) and store(i, j - 4))
                for s in range(SLOTS - OUT_RING, SLOTS):
                    pool.wait_ge(s_st[s % OUT_RING], 32 * stores(0, s))

            @block.scalar
            def _(act):
                nc.scalar.preload_act_table(ACT.Gelu)

                def high(i, j):
                    s = SLOT_UNROLL * i + j
                    act.wait_ge(s_t, s + 1)
                    if j >= 2:
                        act.wait_ge(s_up, 2 * (s - 1))
                    nc.scalar.activation(xh[:, j % 2, :], t_ps[j % 2][:, 0:SLOT], ACT.Copy).then_inc(s_hi, 1)

                def gelu(i, j):
                    s = SLOT_UNROLL * i + j
                    x = expert(act, s)
                    if j >= 2:
                        act.wait_ge(s_glo, s - 1)
                    for c in range(FC):
                        if c % 2 == 0:
                            act.wait_ge(s_up, 2 * s + c // 2 + 1)
                        last = nc.scalar.activation(g[:, j % 2, c, :],
                                                    up_ps[j % 2][c // 2][:, c % 2 * SLOT:(c % 2 + 1) * SLOT],
                                                    ACT.Gelu, bias=kept.b1[:, bass.ds(x * FC + c, 1)],
                                                    scale=1.0 / W_SCALE)
                    last.then_inc(s_g, 1)

                def gelu_high(i, j):
                    s = SLOT_UNROLL * i + j
                    act.wait_ge(s_g, s + 1)
                    if j >= HALVES:
                        act.wait_ge(s_down, s - HALVES + 1)
                    nc.scalar.activation(gh[:, j % HALVES, :, :], g[:, j % 2, :, :], ACT.Copy).then_inc(s_ghi, 1)

                def step(i, j, live):
                    if live(1):
                        high(i, j - 1)
                    if live(3):
                        gelu_high(i, j - 3)
                    if live(2):
                        gelu(i, j - 2)

                steps(act, step)

            @block.vector
            def _(dve):
                def normalise(i, j):
                    s = SLOT_UNROLL * i + j
                    dve.wait_ge(s_in[j % SLOT_UNROLL], 16 * (i + j // SLOT_UNROLL + 1))
                    if j >= 2:
                        dve.wait_ge(s_t, s - 1)
                    p = pay[:, j % SLOT_UNROLL, :, :]
                    for k in range(2):
                        last = nc.vector.tensor_scalar(xn[:, j % 2, k, :], p[:, k, 0:D], p[:, k, D:D + 1],
                                                       p[:, k, D + 1:D + 2], ALU.subtract, ALU.mult)
                    last.then_inc(s_xn, 1)

                def low(i, j):
                    s = SLOT_UNROLL * i + j
                    dve.wait_ge(s_hi, s + 1)
                    if j >= 2:
                        dve.wait_ge(s_up, 2 * (s - 1))
                    nc.vector.tensor_tensor(xl[:, j % 2, :], t_ps[j % 2][:, 0:SLOT], xh[:, j % 2, :], ALU.subtract)\
                        .then_inc(s_lo, 1)

                def gelu_low(i, j):
                    s = SLOT_UNROLL * i + j
                    dve.wait_ge(s_ghi, s + 1)
                    if j >= HALVES:
                        dve.wait_ge(s_down, s - HALVES + 1)
                    nc.vector.tensor_tensor(gl[:, j % HALVES, :, :], g[:, j % 2, :, :], gh[:, j % HALVES, :, :],
                                            ALU.subtract)\
                        .then_inc(s_glo, 1)

                def finish(i, j):
                    s = SLOT_UNROLL * i + j
                    dve.wait_ge(s_down, s + 1)
                    if j >= OUT_RING:
                        dve.wait_ge(s_st[j % OUT_RING], 32 * stores(i, j - OUT_RING))
                    p = pay[:, j % SLOT_UNROLL, :, :]
                    for k in range(2):
                        last = nc.vector.scalar_tensor_tensor(out=o[:, j % OUT_RING, k, :], in0=down_ps[j % 2][:, k * D:(k + 1) * D],
                                                              scalar=p[:, k, D + 2:D + 3], in1=p[:, k, 0:D],
                                                              op0=ALU.mult, op1=ALU.add)
                    last.then_inc(s_o, 1)

                def step(i, j, live):
                    if live(0):
                        normalise(i, j)
                    if live(1):
                        low(i, j - 1)
                    if live(3):
                        gelu_low(i, j - 3)
                    if live(4):
                        finish(i, j - 4)

                steps(dve, step)

            @block.tensor
            def _(pe):
                def transposes(i, j):
                    s = SLOT_UNROLL * i + j
                    pe.wait_ge(s_xn, s + 1)
                    if j >= 2:
                        pe.wait_ge(s_lo, s - 1)
                    for k in range(2):
                        last = nc.tensor.transpose(t_ps[j % 2][:, k * D:(k + 1) * D], xn[:, j % 2, k, :],
                                                   kept.col(C_ID, 128))
                    last.then_inc(s_t, 1)

                def up(i, j, x):
                    s = SLOT_UNROLL * i + j
                    pe.wait_ge(s_lo, s + 1)
                    if j >= 2:
                        pe.wait_ge(s_g, s - 1)
                    for c in range(FC):
                        u = up_ps[j % 2][c // 2][:, c % 2 * SLOT:(c % 2 + 1) * SLOT]
                        hi, lo = (ffn[n][c][:, bass.ds(x * D, D)] for n in ("w1_hi", "w1_lo"))
                        nc.tensor.matmul(u, hi, xh[:, j % 2, :], start=True, stop=False)
                        nc.tensor.matmul(u, hi, xl[:, j % 2, :], start=False, stop=False)
                        last = nc.tensor.matmul(u, lo, xh[:, j % 2, :], start=False, stop=True)
                        if c % 2 == 1:
                            last.then_inc(s_up, 1)

                def down(i, j, x):
                    s = SLOT_UNROLL * i + j
                    pe.wait_ge(s_glo, s + 1)
                    if j >= 2:
                        pe.wait_ge(s_o, s - 1)
                    o = down_ps[j % 2][:, 0:2 * D].rearrange("p (k e) -> p k e", k=2)
                    nc.tensor.matmul(o, kept.share[:, :], kept.b2[:, bass.ds(x * D, D)].unsqueeze(1)
                                     .broadcast_to([96, 2, D]), start=True, stop=False)
                    for k in range(2):
                        for c in range(FC):
                            ghi, glo = (t[:, j % HALVES, c, k * 128:(k + 1) * 128] for t in (gh, gl))
                            whi, wlo = (ffn[n][c][:, bass.ds(x * D, D)] for n in ("w2_hi", "w2_lo"))
                            nc.tensor.matmul(o[:, k, :], ghi, whi, start=False, stop=False)
                            nc.tensor.matmul(o[:, k, :], ghi, wlo, start=False, stop=False)
                            last = nc.tensor.matmul(o[:, k, :], glo, whi, start=False,
                                                    stop=k == 1 and c == FC - 1)
                    last.then_inc(s_down, 1)

                word = None

                def load_word(i):
                    nonlocal word
                    word = pe.value_load(table[0:1, 2, bass.ds(SLOT_UNROLL * i + PEEL - 4, 1)], min_val=0,
                                         max_val=EXPERTS ** RUN - 1)

                def expert_of(i, j):
                    if isinstance(i, int):
                        return expert(pe, SLOT_UNROLL * i + j)
                    return (word >> 3 * (j - PEEL + 4)) & (EXPERTS - 1)

                def step(i, j, live):
                    if live(1):
                        transposes(i, j - 1)
                    if live(2):
                        up(i, j - 2, expert_of(i, j - 2))
                    if live(4):
                        down(i, j - 4, expert_of(i, j - 4))

                steps(pe, step, load_word)


def build(nc, out, **a):
    kept = Kept(nc)
    with nc.sbuf_tensor("hnT", [128, ALL], F32) as hnT:
        with ExitStack() as ctx:
            def sb(name, shape, dt=F32):
                return ctx.enter_context(nc.sbuf_tensor(name, shape, dt))
            tok = {"w": sb("w_tok_sb", [128, VARIANTS, D]), "gamma": sb("gamma_sb", [128, TOKENS, VARIANTS]),
                   "rstd": sb("rstd_image", [128, 1]), "stT": sb("image_parts_T", [PARTS, IMAGES], BF16)}
            rows_in = TokenizerRows(nc, ctx, kept, a)
            image_statistics(nc, kept, hnT, tok, rows_in, a)
            tokenizer(nc, kept, hnT, tok, rows_in)
        with nc.sbuf_tensor("slot_table", [1, 3, SLOTS], I32) as table, ExitStack() as ctx:
            ffn = {n: [ctx.enter_context(nc.sbuf_tensor(f"{n}{c}", [128, EXPERTS * D], F16)) for c in range(FC)]
                   for n in ("w1_hi", "w1_lo", "w2_hi", "w2_lo")}
            with ExitStack() as plan_ctx:
                attention(nc, kept, hnT, ffn, Plan(nc, plan_ctx, kept, table), a)
            experts(nc, kept, table, ffn, out)


def kernel(x, L0_tok_gamma, L0_tok_beta, L0_tok_W, L0_tok_b, L0_attn_Wq, L0_attn_Wv, L0_attn_Wk,
           L0_ffn_Ws, L0_ffn_bs, L0_ffn_W1, L0_ffn_b1, L0_ffn_W2, L0_ffn_b2):
    import concourse.bacc as bacc
    from concourse.bass_utils import run_bass_kernel_spmd

    def patches(p, g):
        b = p.shape[0]
        return np.asarray(p).reshape(b, 2, g, 2, 4, g, 2, 4).transpose(3, 6, 1, 4, 7, 2, 5, 0).reshape(128, g, g, b)

    def positions(p):
        return np.asarray(p).reshape(VARIANTS, 2, GRID, 2, 4, GRID, 2, 4).transpose(3, 6, 1, 4, 7, 2, 5, 0)\
            .reshape(128, TOKENS, VARIANTS)

    x = np.asarray(x)
    arrays = {
        "x_al": patches(x, GRID),
        "x_off": patches(np.pad(x, ((0, 0), (0, 0), (4, 4), (4, 4))), GRID + 1),
        "gamma": positions(L0_tok_gamma),
        "beta": positions(L0_tok_beta),
        "w_tok": np.asarray(L0_tok_W).reshape(D, VARIANTS, 2, 2, 4, 2, 4).transpose(3, 5, 2, 4, 6, 1, 0)
        .reshape(128, VARIANTS, D),
        "b_tok": np.asarray(L0_tok_b).reshape(1, D),
        "w_q": np.asarray(L0_attn_Wq), "w_k": np.asarray(L0_attn_Wv), "w_v": np.asarray(L0_attn_Wk),
        "w_s": np.asarray(L0_ffn_Ws),
        "b_s": np.asarray(L0_ffn_bs).reshape(1, EXPERTS),
        "w1": np.asarray(L0_ffn_W1).reshape(EXPERTS, D, FC, 128).transpose(1, 2, 0, 3).reshape(D, EXPERTS * F),
        "b1": np.asarray(L0_ffn_b1).reshape(EXPERTS, FC, 128).transpose(2, 0, 1).reshape(128, EXPERTS * FC),
        "w2": np.asarray(L0_ffn_W2).reshape(EXPERTS, FC, 128, D).transpose(2, 1, 0, 3).reshape(128, EXPERTS * F),
        "b2": np.asarray(L0_ffn_b2).reshape(1, EXPERTS * D),
        "const": constants(),
    }
    arrays = {n: np.ascontiguousarray(v) for n, v in arrays.items()}
    nc = bacc.Bacc("TRN2", target_bir_lowering=False, num_devices=1)
    aps = {n: nc.dram_tensor(n, v.shape, F32, kind="ExternalInput").ap() for n, v in arrays.items()}
    out = nc.dram_tensor("out", (ALL, D), F32, kind="ExternalOutput").ap()
    build(nc, out, **aps)
    r = run_bass_kernel_spmd(nc, [arrays], core_ids=[0])
    return r.results[0]["out"].reshape(IMAGES, TOKENS, D)
```
